# Optimizing a Trainium2 kernel written in Bass

```python
import numpy as np
import jax
import jax.numpy as jnp

def _softmax(x, axis=-1):
    return jax.nn.softmax(x, axis=axis)

def _gelu(x):
    return jax.nn.gelu(x, approximate=True)

def _silu(x):
    return jax.nn.silu(x)

def _sigmoid(x):
    return jax.nn.sigmoid(x)

def _layernorm(x, axis=-1, eps=1e-05):
    m = jnp.mean(x, axis=axis, keepdims=True)
    v = jnp.var(x, axis=axis, keepdims=True)
    return (x - m) / jnp.sqrt(v + eps)

def _scatter_add(tgt, idx, src, axis=0):
    return tgt.at[idx].add(src)

def _segment_sum(src, seg, n):
    return jax.ops.segment_sum(src, seg, n)
kernel_name = 'mk_sandwich_d1_jaxref_r8_410b5a'

def setup_inputs(seed: int=0):
    np.random.seed(seed)
    _w = jnp.asarray

    def _L0_attn_setup():
        import jax, jax.numpy as jnp
        import numpy as np
        EMB_DIM = 33
        FREQ = 10.0
        ORDER = 2

        def _hyena_filter(L, D, w1, b1, w2, b2, filt_bias, filt_decay):
            t = jnp.linspace(0.0, 1.0, L)[:, None]
            bands = jnp.linspace(0.0, EMB_DIM - 1.0, EMB_DIM)[None, :]
            pe = jnp.sin(t * bands * FREQ)
            h = jnp.sin(FREQ * (pe @ w1.T + b1)) @ w2.T + b2
            h = h.reshape(L, ORDER, D).transpose(1, 2, 0)
            t_window = jnp.linspace(0.0, 1.0, L)[None, None, :]
            decay = jnp.exp(-jnp.exp(filt_decay)[..., None] * t_window)
            h = h * decay + filt_bias[..., None]
            return h * (1.0 / L)

        def _depthwise_conv3(x, w, b):
            xp = jnp.pad(x, ((0, 0), (0, 0), (1, 1)))
            return w[:, 0, None] * xp[:, :, :-2] + w[:, 1, None] * xp[:, :, 1:-1] + w[:, 2, None] * xp[:, :, 2:] + b[:, None]
        key = jax.random.key(seed)
        ks = jax.random.split(key, 8)
        B, L, D = (2, 512, 128)
        OD = (ORDER + 1) * D
        std = 0.02
        return {'u': jax.random.normal(ks[0], (B, L, D), jnp.float32), 'w_in': jax.random.normal(ks[1], (OD, D), jnp.float32) * std, 'b_in': jnp.zeros((OD,), jnp.float32), 'conv_w': jax.random.normal(ks[2], (OD, 3), jnp.float32) * std, 'conv_b': jnp.zeros((OD,), jnp.float32), 'w1': jax.random.normal(ks[3], (64, EMB_DIM), jnp.float32) * std, 'b1': jnp.zeros((64,), jnp.float32), 'w2': jax.random.normal(ks[4], (ORDER * D, 64), jnp.float32) * std, 'b2': jnp.zeros((ORDER * D,), jnp.float32), 'filt_bias': jnp.zeros((ORDER, D), jnp.float32), 'filt_decay': jnp.ones((ORDER, D), jnp.float32) * -3.0, 'w_out': jax.random.normal(ks[5], (D, D), jnp.float32) * std, 'b_out': jnp.zeros((D,), jnp.float32)}
    _L0_attn_in = _L0_attn_setup()

    def _L0_ffn_setup():
        import jax, jax.numpy as jnp
        import numpy as np
        D_MODEL = 128
        N_HEADS = 16
        HEAD_DIM = D_MODEL // N_HEADS
        FFN_DIM = 512
        N_EXPERTS = 8
        CAP_FRAC = 0.25
        MOE_TOKEN_DROPOUT = 0.2
        LN_EPS = 1e-05
        B, S = (4, 64)

        def _layer_norm(x, g, b):
            mu = x.mean(-1, keepdims=True)
            var = ((x - mu) ** 2).mean(-1, keepdims=True)
            return (x - mu) * jax.lax.rsqrt(var + LN_EPS) * g + b

        def _self_attention(x, wq, bq, wk, bk, wv, bv, wo, bo):
            b, s, d = x.shape
            q = ((x @ wq + bq) * HEAD_DIM ** (-0.5)).reshape(b, s, N_HEADS, HEAD_DIM)
            k = (x @ wk + bk).reshape(b, s, N_HEADS, HEAD_DIM)
            v = (x @ wv + bv).reshape(b, s, N_HEADS, HEAD_DIM)
            scores = jnp.einsum('bqhd,bkhd->bhqk', q, k)
            p = jax.nn.softmax(scores, axis=-1)
            o = jnp.einsum('bhqk,bkhd->bqhd', p, v).reshape(b, s, d)
            return o @ wo + bo

        def _moe_ffn(x, wr, w1, b1, w2, b2):
            T, D = x.shape
            C = int(np.ceil(CAP_FRAC * T))
            logits = x @ wr
            probs = jax.nn.softmax(logits, axis=-1)
            top1 = jnp.argmax(probs, axis=-1)
            m1 = jax.nn.one_hot(top1, N_EXPERTS, dtype=x.dtype)
            top2 = jnp.argmax(jnp.where(m1 > 0, -jnp.inf, logits), axis=-1)
            m2 = jax.nn.one_hot(top2, N_EXPERTS, dtype=x.dtype)
            loc1 = jnp.cumsum(m1, axis=0) - 1.0
            loc2 = jnp.cumsum(m2, axis=0) - 1.0 + m1.sum(0, keepdims=True)
            m1 = m1 * (loc1 < C)
            m2 = m2 * (loc2 < C)
            t1 = (probs * m1).sum(-1)
            t2 = (probs * m2).sum(-1)
            denom = jnp.maximum(t1 + t2, jnp.finfo(x.dtype).eps)
            t1, t2 = (t1 / denom, t2 / denom)
            tok = jnp.arange(T)
            s1 = loc1[tok, top1].astype(jnp.int32)
            s2 = loc2[tok, top2].astype(jnp.int32)
            v1 = m1[tok, top1] > 0
            v2 = m2[tok, top2] > 0
            s1 = jnp.where(v1, s1, C)
            s2 = jnp.where(v2, s2, C)
            buf = jnp.zeros((N_EXPERTS, C, D), x.dtype)
            buf = buf.at[top1, s1].set(x, mode='drop')
            buf = buf.at[top2, s2].set(x, mode='drop')
            h = jax.nn.relu(jnp.einsum('ecd,edf->ecf', buf, w1) + b1[:, None, :])
            y = (jnp.einsum('ecf,efd->ecd', h, w2) + b2[:, None, :]) * (1.0 - MOE_TOKEN_DROPOUT)
            y1 = y[top1, jnp.minimum(s1, C - 1)]
            y2 = y[top2, jnp.minimum(s2, C - 1)]
            g1 = t1 * v1
            g2 = t2 * v2
            return g1[:, None] * y1 + g2[:, None] * y2
        key = jax.random.key(seed)
        ks = jax.random.split(key, 20)

        def w(k, shape, scale=0.02):
            return jax.random.normal(k, shape, jnp.float32) * scale
        return {'x': jax.random.normal(ks[0], (B, S, D_MODEL), jnp.float32), 'wq': w(ks[1], (D_MODEL, D_MODEL)), 'bq': w(ks[2], (D_MODEL,)), 'wk': w(ks[3], (D_MODEL, D_MODEL)), 'bk': w(ks[4], (D_MODEL,)), 'wv': w(ks[5], (D_MODEL, D_MODEL)), 'bv': w(ks[6], (D_MODEL,)), 'wo': w(ks[7], (D_MODEL, D_MODEL)), 'bo': w(ks[8], (D_MODEL,)), 'ln1_g': 1.0 + w(ks[9], (D_MODEL,)), 'ln1_b': w(ks[10], (D_MODEL,)), 'ln2_g': 1.0 + w(ks[11], (D_MODEL,)), 'ln2_b': w(ks[12], (D_MODEL,)), 'wr': w(ks[13], (D_MODEL, N_EXPERTS)), 'w1': w(ks[14], (N_EXPERTS, D_MODEL, FFN_DIM)), 'b1': w(ks[15], (N_EXPERTS, FFN_DIM)), 'w2': w(ks[16], (N_EXPERTS, FFN_DIM, D_MODEL)), 'b2': w(ks[17], (N_EXPERTS, D_MODEL))}
    _L0_ffn_in = _L0_ffn_setup()
    _d = {'L0_attn_u': _L0_attn_in['u'], 'L0_attn_w_in': _L0_attn_in['w_in'], 'L0_attn_b_in': _L0_attn_in['b_in'], 'L0_attn_conv_w': _L0_attn_in['conv_w'], 'L0_attn_conv_b': _L0_attn_in['conv_b'], 'L0_attn_w1': _L0_attn_in['w1'], 'L0_attn_b1': _L0_attn_in['b1'], 'L0_attn_w2': _L0_attn_in['w2'], 'L0_attn_b2': _L0_attn_in['b2'], 'L0_attn_filt_bias': _L0_attn_in['filt_bias'], 'L0_attn_filt_decay': _L0_attn_in['filt_decay'], 'L0_attn_w_out': _L0_attn_in['w_out'], 'L0_attn_b_out': _L0_attn_in['b_out'], 'L0_ffn_wq': _L0_ffn_in['wq'], 'L0_ffn_bq': _L0_ffn_in['bq'], 'L0_ffn_wk': _L0_ffn_in['wk'], 'L0_ffn_bk': _L0_ffn_in['bk'], 'L0_ffn_wv': _L0_ffn_in['wv'], 'L0_ffn_bv': _L0_ffn_in['bv'], 'L0_ffn_wo': _L0_ffn_in['wo'], 'L0_ffn_bo': _L0_ffn_in['bo'], 'L0_ffn_ln1_g': _L0_ffn_in['ln1_g'], 'L0_ffn_ln1_b': _L0_ffn_in['ln1_b'], 'L0_ffn_ln2_g': _L0_ffn_in['ln2_g'], 'L0_ffn_ln2_b': _L0_ffn_in['ln2_b'], 'L0_ffn_wr': _L0_ffn_in['wr'], 'L0_ffn_w1': _L0_ffn_in['w1'], 'L0_ffn_b1': _L0_ffn_in['b1'], 'L0_ffn_w2': _L0_ffn_in['w2'], 'L0_ffn_b2': _L0_ffn_in['b2']}
    _x0 = _d['L0_attn_u']
    _d['L0_attn_u'] = jax.random.normal(jax.random.fold_in(jax.random.key(seed), 1), (1, 2048, 128), dtype=_x0.dtype)
    del _x0
    return _d

def reference(L0_attn_u, L0_attn_w_in, L0_attn_b_in, L0_attn_conv_w, L0_attn_conv_b, L0_attn_w1, L0_attn_b1, L0_attn_w2, L0_attn_b2, L0_attn_filt_bias, L0_attn_filt_decay, L0_attn_w_out, L0_attn_b_out, L0_ffn_wq, L0_ffn_bq, L0_ffn_wk, L0_ffn_bk, L0_ffn_wv, L0_ffn_bv, L0_ffn_wo, L0_ffn_bo, L0_ffn_ln1_g, L0_ffn_ln1_b, L0_ffn_ln2_g, L0_ffn_ln2_b, L0_ffn_wr, L0_ffn_w1, L0_ffn_b1, L0_ffn_w2, L0_ffn_b2):

    def _L0_attn_ref(u, w_in, b_in, conv_w, conv_b, w1, b1, w2, b2, filt_bias, filt_decay, w_out, b_out):
        import jax, jax.numpy as jnp
        import numpy as np
        EMB_DIM = 33
        FREQ = 10.0
        ORDER = 2

        def _hyena_filter(L, D, w1, b1, w2, b2, filt_bias, filt_decay):
            t = jnp.linspace(0.0, 1.0, L)[:, None]
            bands = jnp.linspace(0.0, EMB_DIM - 1.0, EMB_DIM)[None, :]
            pe = jnp.sin(t * bands * FREQ)
            h = jnp.sin(FREQ * (pe @ w1.T + b1)) @ w2.T + b2
            h = h.reshape(L, ORDER, D).transpose(1, 2, 0)
            t_window = jnp.linspace(0.0, 1.0, L)[None, None, :]
            decay = jnp.exp(-jnp.exp(filt_decay)[..., None] * t_window)
            h = h * decay + filt_bias[..., None]
            return h * (1.0 / L)

        def _depthwise_conv3(x, w, b):
            xp = jnp.pad(x, ((0, 0), (0, 0), (1, 1)))
            return w[:, 0, None] * xp[:, :, :-2] + w[:, 1, None] * xp[:, :, 1:-1] + w[:, 2, None] * xp[:, :, 2:] + b[:, None]
        B, L, D = u.shape
        res = u @ w_in.T + b_in
        res = res.transpose(0, 2, 1)
        res = _depthwise_conv3(res, conv_w, conv_b)
        res = res.reshape(B, ORDER + 1, D, L)
        x = res[:, :-1]
        v = res[:, -1]
        h = _hyena_filter(L, D, w1, b1, w2, b2, filt_bias, filt_decay)
        n_fft = 2 * L
        for n in range(ORDER):
            v_fft = jnp.fft.rfft(v, n=n_fft, axis=-1)
            h_fft = jnp.fft.rfft(h[n], n=n_fft, axis=-1)
            y = jnp.fft.irfft(v_fft * h_fft, n=n_fft, axis=-1)[..., :L]
            v = y * x[:, n]
        return v.transpose(0, 2, 1) @ w_out.T + b_out

    def _L0_ffn_ref(x, wq, bq, wk, bk, wv, bv, wo, bo, ln1_g, ln1_b, ln2_g, ln2_b, wr, w1, b1, w2, b2):
        import jax, jax.numpy as jnp
        import numpy as np
        D_MODEL = 128
        N_HEADS = 16
        HEAD_DIM = D_MODEL // N_HEADS
        FFN_DIM = 512
        N_EXPERTS = 8
        CAP_FRAC = 0.25
        MOE_TOKEN_DROPOUT = 0.2
        LN_EPS = 1e-05
        B, S = (4, 64)

        def _layer_norm(x, g, b):
            mu = x.mean(-1, keepdims=True)
            var = ((x - mu) ** 2).mean(-1, keepdims=True)
            return (x - mu) * jax.lax.rsqrt(var + LN_EPS) * g + b

        def _self_attention(x, wq, bq, wk, bk, wv, bv, wo, bo):
            b, s, d = x.shape
            q = ((x @ wq + bq) * HEAD_DIM ** (-0.5)).reshape(b, s, N_HEADS, HEAD_DIM)
            k = (x @ wk + bk).reshape(b, s, N_HEADS, HEAD_DIM)
            v = (x @ wv + bv).reshape(b, s, N_HEADS, HEAD_DIM)
            scores = jnp.einsum('bqhd,bkhd->bhqk', q, k)
            p = jax.nn.softmax(scores, axis=-1)
            o = jnp.einsum('bhqk,bkhd->bqhd', p, v).reshape(b, s, d)
            return o @ wo + bo

        def _moe_ffn(x, wr, w1, b1, w2, b2):
            T, D = x.shape
            C = int(np.ceil(CAP_FRAC * T))
            logits = x @ wr
            probs = jax.nn.softmax(logits, axis=-1)
            top1 = jnp.argmax(probs, axis=-1)
            m1 = jax.nn.one_hot(top1, N_EXPERTS, dtype=x.dtype)
            top2 = jnp.argmax(jnp.where(m1 > 0, -jnp.inf, logits), axis=-1)
            m2 = jax.nn.one_hot(top2, N_EXPERTS, dtype=x.dtype)
            loc1 = jnp.cumsum(m1, axis=0) - 1.0
            loc2 = jnp.cumsum(m2, axis=0) - 1.0 + m1.sum(0, keepdims=True)
            m1 = m1 * (loc1 < C)
            m2 = m2 * (loc2 < C)
            t1 = (probs * m1).sum(-1)
            t2 = (probs * m2).sum(-1)
            denom = jnp.maximum(t1 + t2, jnp.finfo(x.dtype).eps)
            t1, t2 = (t1 / denom, t2 / denom)
            tok = jnp.arange(T)
            s1 = loc1[tok, top1].astype(jnp.int32)
            s2 = loc2[tok, top2].astype(jnp.int32)
            v1 = m1[tok, top1] > 0
            v2 = m2[tok, top2] > 0
            s1 = jnp.where(v1, s1, C)
            s2 = jnp.where(v2, s2, C)
            buf = jnp.zeros((N_EXPERTS, C, D), x.dtype)
            buf = buf.at[top1, s1].set(x, mode='drop')
            buf = buf.at[top2, s2].set(x, mode='drop')
            h = jax.nn.relu(jnp.einsum('ecd,edf->ecf', buf, w1) + b1[:, None, :])
            y = (jnp.einsum('ecf,efd->ecd', h, w2) + b2[:, None, :]) * (1.0 - MOE_TOKEN_DROPOUT)
            y1 = y[top1, jnp.minimum(s1, C - 1)]
            y2 = y[top2, jnp.minimum(s2, C - 1)]
            g1 = t1 * v1
            g2 = t2 * v2
            return g1[:, None] * y1 + g2[:, None] * y2
        h = _layer_norm(x, ln1_g, ln1_b)
        h = _self_attention(h, wq, bq, wk, bk, wv, bv, wo, bo)
        x = x + h
        h = _layer_norm(x, ln2_g, ln2_b)
        b, s, d = h.shape
        moe = _moe_ffn(h.reshape(b * s, d), wr, w1, b1, w2, b2).reshape(b, s, d)
        return x + moe
    x = L0_attn_u
    x = x + _layernorm(_L0_attn_ref(_layernorm(x, axis=-1), L0_attn_w_in, L0_attn_b_in, L0_attn_conv_w, L0_attn_conv_b, L0_attn_w1, L0_attn_b1, L0_attn_w2, L0_attn_b2, L0_attn_filt_bias, L0_attn_filt_decay, L0_attn_w_out, L0_attn_b_out), axis=-1)
    x = x + _layernorm(_L0_ffn_ref(_layernorm(x, axis=-1), L0_ffn_wq, L0_ffn_bq, L0_ffn_wk, L0_ffn_bk, L0_ffn_wv, L0_ffn_bv, L0_ffn_wo, L0_ffn_bo, L0_ffn_ln1_g, L0_ffn_ln1_b, L0_ffn_ln2_g, L0_ffn_ln2_b, L0_ffn_wr, L0_ffn_w1, L0_ffn_b1, L0_ffn_w2, L0_ffn_b2), axis=-1)
    return x

_drawn_inputs = setup_inputs


def setup_inputs(seed=0):
    import zlib

    import numpy as np

    out = dict(_drawn_inputs(seed))
    spreads = {'L0_attn_b_in': (0.0, 0.8),
     'L0_attn_conv_b': (0.0, 0.8),
     'L0_attn_b1': (0.0, 0.8),
     'L0_attn_b2': (0.0, 0.8),
     'L0_attn_filt_bias': (0.0, 0.8),
     'L0_attn_filt_decay': (-3.0, 0.6),
     'L0_attn_b_out': (0.0, 0.1)}
    factors = {'L0_attn_w_in': 8.0,
     'L0_attn_conv_w': 8.0,
     'L0_attn_w1': 8.0,
     'L0_attn_w2': 8.0,
     'L0_attn_w_out': 8.0,
     'L0_ffn_wq': 8.0,
     'L0_ffn_bq': 8.0,
     'L0_ffn_wk': 8.0,
     'L0_ffn_bk': 64.0,
     'L0_ffn_wv': 3.623,
     'L0_ffn_bv': 8.0,
     'L0_ffn_wo': 3.756,
     'L0_ffn_bo': 5.996,
     'L0_ffn_ln1_g': 8.0,
     'L0_ffn_ln1_b': 8.0,
     'L0_ffn_ln2_g': 8.0,
     'L0_ffn_ln2_b': 8.0,
     'L0_ffn_wr': 2.891,
     'L0_ffn_w1': 3.433,
     'L0_ffn_b1': 51.914,
     'L0_ffn_w2': 2.878,
     'L0_ffn_b2': 50.36}
    for name, (base, spread) in spreads.items():
        noise = np.random.default_rng([zlib.crc32(name.encode()), seed]).standard_normal(out[name].shape)
        drawn = base * np.exp(spread * noise) if base else spread * noise
        out[name] = jnp.asarray(drawn.astype(out[name].dtype))
    for name, factor in factors.items():
        out[name] = (out[name] * factor).astype(out[name].dtype)
    return out
```

```python
from contextlib import ExitStack

import numpy as np

import concourse.bass as bass
from concourse import mybir

ALU = mybir.AluOpType
ACT = mybir.ActivationFunctionType
AX = mybir.AxisListType
F32 = mybir.dt.float32
BF16 = mybir.dt.bfloat16

P = 128
L, D = 2048, 128
NT = L // P
ORDER, EMB, HID = 2, 33, 64
FREQ = 10.0
LN_EPS = 1e-5
BANK = 512
NB = 8

R = 64
N_FFT = R * R
H1 = R // 2
NJ = P // H1
assert N_FFT == 2 * L and NT * NJ == R

TWO_PI_HI = 6.28125
TWO_PI_LO = float(2 * np.pi - TWO_PI_HI)
ROUND = 1.5 * 2.0 ** 23

NH, HD = 16, 8
NE, FF = 8, 512
CAP = L // 4
KEEP = 0.8


def shape_constants():
    f32 = np.float32
    i, p = np.meshgrid(np.arange(NT), np.arange(P), indexing="ij")
    tok = R * (p % H1) + NJ * i + p // H1
    lin = np.linspace(0.0, 1.0, L, dtype=f32)
    bands = np.linspace(0.0, EMB - 1.0, EMB, dtype=f32)
    pe = np.sin((lin[:, None] * bands[None, :] * f32(FREQ)).astype(np.float64)).astype(f32)
    c = {"c_pe": pe[tok.reshape(-1)].T, "c_negt": -lin[tok].T}
    n1, n2, k2 = np.arange(H1), np.arange(R), np.arange(R)
    f1 = np.zeros((H1, R))
    f1[:, 0], f1[:, 1] = 1.0, (-1.0) ** n1
    g = np.zeros((R, H1))
    g[0], g[1] = 1.0, (-1.0) ** n1
    for m in range(1, H1):
        a = 2 * np.pi * n1 * m / R
        f1[:, 2 * m], f1[:, 2 * m + 1] = np.cos(a), -np.sin(a)
        g[2 * m], g[2 * m + 1] = 2 * np.cos(a), -2 * np.sin(a)
    c["c_f1"] = np.kron(np.eye(NJ), f1)
    c["c_g"] = np.kron(np.eye(2), g / (N_FFT * L))
    m_fwd = np.zeros((2, R, H1 + 1, 2, R))
    m_inv = np.zeros((2, R, H1 + 1, 2, R))
    for k1 in range(H1 + 1):
        th = 2 * np.pi * n2[:, None] * (k1 + R * k2[None, :]) / N_FFT
        if k1 == 0 or k1 == H1:
            m_fwd[k1 // H1, :, k1, 0], m_fwd[k1 // H1, :, k1, 1] = np.cos(th), -np.sin(th)
        else:
            m_fwd[0, :, k1, 0], m_fwd[1, :, k1, 0] = np.cos(th), np.sin(th)
            m_fwd[0, :, k1, 1], m_fwd[1, :, k1, 1] = -np.sin(th), np.cos(th)
        m_inv[0, :, k1, 0], m_inv[1, :, k1, 0] = np.cos(th).T, -np.sin(th).T
        m_inv[0, :, k1, 1], m_inv[1, :, k1, 1] = np.sin(th).T, np.cos(th).T
    c["c_fwd"] = m_fwd.reshape(P, -1)
    inv = m_inv.reshape(2, R, -1)
    c["c_inv"] = np.concatenate([inv[0], inv[1], -inv[0]])
    edge = np.zeros((4, 2, P))
    edge[0, 0, 0] = edge[2, 1, P - 1] = -1.0
    c["c_edge"] = edge.reshape(4, -1)
    c["c_ident"] = np.eye(P)
    q = np.arange(P)
    jq, nq = q // H1, q % H1
    c["c_before"] = np.stack([
        nq[:, None] < nq[None, :],
        nq[:, None] == nq[None, :],
        (nq[:, None] == nq[None, :]) & (jq[:, None] <= jq[None, :]),
    ], axis=1).reshape(P, -1)
    return {k: np.ascontiguousarray(v, dtype=f32) for k, v in c.items()}


def tiles_of(dram):
    v = dram.rearrange("(n i j) d -> n i j d", i=NT, j=NJ)
    return [v[:, :, j, :] for j in range(NJ)]


def chain(eng, s):
    count = [0]

    def link(ins):
        count[0] += 1
        ins.then_inc(s, 1)
        eng.wait_ge(s, count[0])
    return link


class Norm:

    def __init__(self, nc, sb, sem, name):
        self.stats = sb(name + "_stats", [P, NT, 6], F32)
        self.mv = sb(name + "_mv", [P, NT, 2], F32)
        self.rstd = sb(name + "_rstd", [P, NT], F32)
        self.var_ready = sem(name + "_var_ready")
        self.std_ready = sem(name + "_std_ready")

    def vector_stats(self, dve, link, x):
        for i in range(NT):
            ins = dve.bn_stats(self.stats[:, i, :], x[:, i, :])
        link(ins)
        for i in range(NT):
            ins = dve.bn_aggr(self.mv[:, i, :], self.stats[:, i, :])
        link(ins)
        dve.tensor_scalar(self.rstd[:, :], self.mv[:, :, 1], LN_EPS, None, ALU.add).then_inc(self.var_ready, 1)

    def scalar_sqrt(self, act):
        act.wait_ge(self.var_ready, 1)
        act.activation(self.rstd[:, :], self.rstd[:, :], ACT.Sqrt).then_inc(self.std_ready, 1)

    def vector_apply(self, dve, link, out, x):
        dve.wait_ge(self.std_ready, 1)
        link(dve.reciprocal(self.rstd[:, :], self.rstd[:, :]))
        for i in range(NT):
            ins = dve.tensor_scalar(out[:, i, :], x[:, i, :], self.mv[:, i, 0:1], self.rstd[:, i:i + 1],
                                    ALU.subtract, ALU.mult)
        return ins


def bcast_rows(vec, n):
    return bass.AP(vec.tensor, vec.offset, [[0, n]] + [list(x) for x in vec.ap])


class Units:

    def __init__(self):
        self.who, self.base = [], {}

    def stage(self, name, who):
        self.base[name] = len(self.who)
        self.who += who

    def number(self, name, n=0):
        return self.base[name] + n

    def taken(self, who, below):
        return sum(x in (who, "B") for x in self.who[:below])


def hyena(nc, a, x1, ident):
    u = Units()
    alt = lambda n: ("AD" * n)[:n]
    u.stage("small_T", "D")
    u.stage("arg", "DDDD")
    u.stage("w_in_T", "ADA")
    u.stage("bias_T", "D")
    u.stage("bias_b", "D")
    u.stage("xn_T", alt(4))
    u.stage("filt", "D" * 8)
    u.stage("proj", "D" * NT)
    for o in range(ORDER):
        u.stage(f"h{o}_first", alt(8))
        u.stage(f"h{o}_turn", alt(8))
        u.stage(f"h{o}_spec", "B" * 9)
        u.stage(f"v{o}_first", alt(8))
        u.stage(f"v{o}_turn", alt(8))
        u.stage(f"v{o}_spec", "D" * 9)
        u.stage(f"v{o}_back", alt(8))
        u.stage(f"v{o}_return", alt(8))
        u.stage(f"v{o}_time", "D" * 4)
    u.stage("v_T", alt(4))
    u.stage("out", "D" * 4)

    with ExitStack() as ctx:
        def sb(name, shape, dt=F32):
            return ctx.enter_context(nc.sbuf_tensor("hy_" + name, shape, dt))

        def sem(name):
            return ctx.enter_context(nc.semaphore("hy_" + name))

        ps = ctx.enter_context(nc.psum_tensor("hy_ps", [P, NB, BANK], F32))
        branches = sb("branches", [P, NT, 3 * D])
        filt = sb("filt", [P, NT, ORDER * D])
        buf_a = sb("buf_a", [P, (H1 + 1) * P])
        buf_b = sb("buf_b", [P, (H1 + 1) * P])
        buf_c = sb("buf_c", [P, (H1 + 1) * P])
        spec_re = sb("spec_re", [P, H1 + 1, P])
        spec_im = sb("spec_im", [P, H1 + 1, P])
        m_fwd = sb("m_fwd", [P, H1 + 1, P])
        m_inv = sb("m_inv", [P, H1 + 1, P])
        m_inv_i = sb("m_inv_i", [P, H1 + 1, P])
        f1 = sb("f1", [P, NJ * R])
        gt = sb("gt", [P, 2 * H1])
        wk = sb("wk", [P, 3, 3 * D])
        w_in = buf_c[:, 0:384].rearrange("p (b d) -> p b d", b=3)
        ws = buf_c[:, 384:384 + 9 * 128].rearrange("p (t b d) -> p t b d", t=3, b=3)
        cw = sb("cw", [P, 3, 3])
        b_in = sb("b_in", [P, 3])
        bc = sb("bc", [P, 3, 4])
        bias_row = sb("bias_row", [4, 3 * D])
        ones4 = sb("ones4", [4, P])
        edge = sb("edge", [4, 2 * P])
        bias_b = sb("bias_b", [P, 3 * D])
        w1 = sb("w1", [HID, EMB])
        w2 = sb("w2", [P, 2, HID])
        b1 = sb("b1", [HID, 1])
        w1_T = sb("w1_T", [EMB, HID])
        w2_T = sb("w2_T", [P, ORDER * D])
        w_out = sb("w_out", [P, D])
        w_out_T = sb("w_out_T", [P, D])
        b_out = sb("b_out", [P, D])
        negt = sb("negt", [P, NT])
        rate = sb("rate", [P, ORDER * D])
        f_bias = sb("f_bias", [P, ORDER * D])
        xn_T = sb("xn_T", [P, (R + 2) * H1])
        pe_T = spec_im[0:EMB, :, :].rearrange("p a b -> p (a b)")[:, 2048:4096]
        arg = buf_a[0:HID, 0:L]
        turns = buf_a[0:HID, L:2 * L]
        sin_T = buf_b[:, 0:L]
        decay = spec_re[:, 0:H1, :].rearrange("p a b -> p (a b)").rearrange("p (i c) -> p i c", i=NT)
        xn = spec_im[:, 0:NT, :]
        norm_x = Norm(nc, sb, sem, "norm_x")
        norm_y = Norm(nc, sb, sem, "norm_y")
        y = buf_b[:, 0:L].rearrange("p (i d) -> p i d", i=NT)

        x_loaded = sem("x_loaded")
        small_loaded = sem("small_loaded")
        tables_loaded = sem("tables_loaded")
        fwd_loaded = sem("fwd_loaded")
        inv_loaded = sem("inv_loaded")
        row_loaded = sem("row_loaded")
        pe_unit = sem("pe_unit")
        act_taken = sem("act_taken")
        dve_taken = sem("dve_taken")
        dve_chain = sem("dve_chain")
        pool_chain = sem("pool_chain")
        zeroed = sem("zeroed")
        taps_ready = sem("taps_ready")
        arg_ready = sem("arg_ready")
        rate_ready = sem("rate_ready")
        sin_ready = sem("sin_ready")
        decay_ready = sem("decay_ready")
        xn_ready = sem("xn_ready")
        filt_ready = sem("filt_ready")
        halo_ready = sem("halo_ready")
        x1_ready = sem("x1_ready")
        spec_copied = sem("spec_copied")

        def taken(eng, below):
            if n := u.taken("A", below):
                eng.wait_ge(act_taken, n)
            if n := u.taken("D", below):
                eng.wait_ge(dve_taken, n)

        def bank(n):
            return ps[:, n % NB, :]

        def a_view(t):
            return t[:, 0:R * R].rearrange("p (c n) -> p n c", n=R)

        block = ctx.enter_context(nc.Block())

        small = [
            (w1[:, :], a["w1"]), (w2[:, :, :], a["w2"].rearrange("(b p) h -> p b h", p=P)),
            (w_out[:, :], a["w_out"]), (b1[:, :], a["b1"].rearrange("(p o) -> p o", o=1)),
            (ident[:, :], a["c_ident"]), (pe_T, a["c_pe"]),
            (rate[:, :], bcast_rows(a["filt_decay"].rearrange("o d -> (o d)"), P)),
            (negt[:, :], a["c_negt"]),
        ]
        tables = [
            (w_in, a["w_in"].rearrange("(b p) d -> p b d", p=P)),
            (cw[:, :, :], a["conv_w"].rearrange("(b p) k -> p b k", p=P)),
            (b_in[:, :], a["b_in"].rearrange("(b p) -> p b", p=P)),
            (bc[:, :, 3], a["conv_b"].rearrange("(b p) -> p b", p=P)),
            (edge[:, :], a["c_edge"]), (f1[:, :], a["c_f1"]), (gt[:, :], a["c_g"]),
            (f_bias[:, :], bcast_rows(a["filt_bias"].rearrange("o d -> (o d)"), P)),
            (b_out[:, :], bcast_rows(a["b_out"], P)),
        ]

        @block.sync
        def _(sp):
            for j, v in enumerate(tiles_of(a["u"])):
                sp.dma_start(x1[H1 * j:H1 * j + H1, :, :], v).then_inc(x_loaded, 16)
            sp.wait_ge(tables_loaded, 16 * len(tables))
            sp.dma_start(m_fwd[:, :, :].rearrange("p a b -> p (a b)"), a["c_fwd"]).then_inc(fwd_loaded, 16)
            sp.dma_start(m_inv[:, :, :].rearrange("p a b -> p (a b)"), a["c_inv"][0:P, :]).then_inc(inv_loaded, 16)
            sp.dma_start(m_inv_i[:, :, :].rearrange("p a b -> p (a b)"), a["c_inv"][R:R + P, :]).then_inc(inv_loaded, 16)
            for o in range(ORDER):
                taken(sp, u.number(f"h{o}_spec", 9))
                sp.dma_start(spec_re[R:P, :, :], spec_re[0:R, :, :]).then_inc(spec_copied, 16)
                sp.dma_start(spec_im[0:R, :, :], spec_im[R:P, :, :]).then_inc(spec_copied, 16)

        def mine(name, n, who):
            return u.who[u.number(name, n)] == who

        def take_weights(who, take):
            for k in range(3):
                if mine("w_in_T", k, who):
                    take("w_in_T", k, wk[:, k, :], bank(u.number("w_in_T", k))[:, 0:3 * D])

        def take_xn(who, take):
            for n in range(4):
                if mine("xn_T", n, who):
                    take("xn_T", n, xn_T[:, H1 + BANK * n:H1 + BANK * n + BANK], bank(u.number("xn_T", n)))

        def take_fft(name, who, take):
            for n in range(8):
                if mine(name + "_first", n, who):
                    src = bank(u.number(name + "_first", n)).rearrange("p (n c) -> p n c", c=R)
                    take(name + "_first", n, a_view(buf_a)[:, 8 * n:8 * n + 8, :], src)
            for n in range(8):
                if mine(name + "_turn", n, who):
                    take(name + "_turn", n, buf_b[:, BANK * n:BANK * n + BANK], bank(u.number(name + "_turn", n)))

        def spec_blocks(n):
            return slice(H1, H1 + 1) if n == 0 else slice(4 * n - 4, 4 * n)

        def take_spec(o, who, take):
            half, spec = (slice(0, R), spec_re) if who == "A" else (slice(R, P), spec_im)
            for n in range(9):
                dst = spec[half, spec_blocks(n), :].rearrange("p a b -> p (a b)")
                take(f"h{o}_spec", n, dst, bank(u.number(f"h{o}_spec", n))[half, 0:dst.shape[1]])

        def take_back(o, who, take):
            v = buf_b[:, 0:R * R].rearrange("p (n c) -> p c n", c=R)
            for n in range(8):
                if mine(f"v{o}_back", n, who):
                    src = bank(u.number(f"v{o}_back", n)).rearrange("p (c n) -> p c n", n=R)
                    take(f"v{o}_back", n, v[:, 8 * n:8 * n + 8, :], src)
            for n in range(8):
                if mine(f"v{o}_return", n, who):
                    take(f"v{o}_return", n, buf_a[:, BANK * n:BANK * n + BANK], bank(u.number(f"v{o}_return", n)))

        def take_v(who, take):
            for n in range(4):
                if mine("v_T", n, who):
                    take("v_T", n, buf_a[:, BANK * n:BANK * n + BANK], bank(u.number("v_T", n)))

        @block.gpsimd
        def _(pool):
            link = chain(pool, pool_chain)
            link(pool.memset(sin_T, 0.0))
            link(pool.memset(w2_T[:, :], 0.0))
            pool.dma_start(w2_T[HID:HID + 1, :], a["b2"].rearrange("(o d) -> o d", o=1)).then_inc(row_loaded, 16)
            link(pool.memset(sin_T[HID:HID + 1, :], 1.0))
            link(pool.memset(xn_T[:, 0:1], 0.0))
            link(pool.memset(xn_T[:, (R + 2) * H1 - 1:(R + 2) * H1], 0.0))
            pool.memset(ones4[:, :], 1.0).then_inc(zeroed, 1)
            pool.wait_ge(tables_loaded, 16 * len(tables))
            for k in range(3):
                for b in range(3):
                    pool.tensor_scalar(ws[:, k, b, :], w_in[:, b, :], cw[:, b, k:k + 1], None, ALU.mult)
            for k in range(3):
                ins = pool.tensor_tensor(bc[:, :, k], b_in[:, :], cw[:, :, k], ALU.mult)
            ins.then_inc(taps_ready, 1)
            for n in range(8):
                pool.wait_ge(dve_taken, u.taken("D", u.number("filt", n) + 1))
                for i in (2 * n, 2 * n + 1):
                    ins = pool.tensor_tensor(filt[:, i, :], filt[:, i, :], f_bias[:, :], ALU.add)
                ins.then_inc(filt_ready, 1)

        @block.scalar
        def _(act):
            for dst, src in small:
                act.dma_start(dst, src).then_inc(small_loaded, 16)
            for dst, src in tables:
                act.dma_start(dst, src, allow_slow_non_contiguous=True).then_inc(tables_loaded, 16)
            norm_x.scalar_sqrt(act)
            act.wait_ge(small_loaded, 16 * len(small))
            act.activation(rate[:, :], rate[:, :], ACT.Exp).then_inc(rate_ready, 1)
            act.wait_ge(rate_ready, 1)
            for i in range(NT):
                ins = act.activation(decay[:, i, :], rate[:, :], ACT.Exp, scale=negt[:, i:i + 1])
            ins.then_inc(decay_ready, 1)

            def take(name, n, dst, src):
                act.wait_ge(pe_unit, u.number(name, n) + 1)
                act.activation(dst, src, ACT.Copy).then_inc(act_taken, 1)

            take_weights("A", take)
            act.wait_ge(arg_ready, 1)
            act.wait_ge(zeroed, 1)
            act.activation(sin_T[0:HID, :], arg, ACT.Sin).then_inc(sin_ready, 1)
            take_xn("A", take)
            for o in range(ORDER):
                take_fft(f"h{o}", "A", take)
                take_spec(o, "A", take)
                take_fft(f"v{o}", "A", take)
                take_back(o, "A", take)
            take_v("A", take)
            norm_y.scalar_sqrt(act)

        @block.vector
        def _(dve):
            link = chain(dve, dve_chain)

            def take(name, n, dst, src):
                dve.wait_ge(pe_unit, u.number(name, n) + 1)
                dve.tensor_copy(dst, src).then_inc(dve_taken, 1)

            dve.wait_ge(x_loaded, 16 * NJ)
            norm_x.vector_stats(dve, link, x1)
            dve.wait_ge(pe_unit, u.number("small_T") + 1)
            dve.wait_ge(row_loaded, 16)
            b = bank(u.number("small_T"))
            dve.tensor_copy(w1_T[:, :], b[0:EMB, 0:HID])
            dve.tensor_copy(w2_T[0:HID, :], b[0:HID, D:D + 2 * D])
            dve.tensor_copy(w_out_T[:, :], b[:, 3 * D:4 * D]).then_inc(dve_taken, 1)
            for n in range(4):
                dve.wait_ge(pe_unit, u.number("arg", n) + 1)
                ins = dve.tensor_scalar(arg[:, BANK * n:BANK * n + BANK], bank(u.number("arg", n))[0:HID, :],
                                        b1[:, 0:1], FREQ, ALU.add, ALU.mult).then_inc(dve_taken, 1)
            dve.wait_ge(dve_taken, u.taken("D", u.number("arg", 3) + 1))
            link(dve.tensor_scalar(turns, arg, 1.0 / (2 * np.pi), ROUND, ALU.mult, ALU.add))
            link(dve.tensor_scalar(turns, turns, ROUND, None, ALU.subtract))
            link(dve.scalar_tensor_tensor(out=arg, in0=turns, scalar=-TWO_PI_HI, in1=arg, op0=ALU.mult, op1=ALU.add))
            link(dve.scalar_tensor_tensor(out=arg, in0=turns, scalar=-TWO_PI_LO, in1=arg, op0=ALU.mult, op1=ALU.add))
            dve.tensor_scalar(arg, arg, 3.1415925, -3.1415925, ALU.min, ALU.max).then_inc(arg_ready, 1)
            norm_x.vector_apply(dve, link, xn, x1).then_inc(xn_ready, 1)
            take_weights("D", take)
            take("bias_T", 0, bias_row[:, :], bank(u.number("bias_T"))[0:4, 0:3 * D])
            take("bias_b", 0, bias_b[:, :], bank(u.number("bias_b"))[:, 0:3 * D])
            take_xn("D", take)
            dve.wait_ge(dve_taken, u.taken("D", u.number("xn_T", 4)))
            dve.wait_ge(act_taken, u.taken("A", u.number("xn_T", 4)))
            dve.wait_ge(zeroed, 1)
            dve.tensor_copy(xn_T[:, 1:H1], xn_T[:, R * H1:R * H1 + H1 - 1])
            dve.tensor_copy(xn_T[:, (R + 1) * H1:(R + 2) * H1 - 1], xn_T[:, H1 + 1:2 * H1]).then_inc(halo_ready, 1)
            dve.wait_ge(decay_ready, 1)
            for n in range(8):
                dve.wait_ge(pe_unit, u.number("filt", n) + 1)
                dve.tensor_tensor(filt[:, 2 * n:2 * n + 2, :].rearrange("p i c -> p (i c)"),
                                  bank(u.number("filt", n)),
                                  decay[:, 2 * n:2 * n + 2, :].rearrange("p i c -> p (i c)"),
                                  ALU.mult).then_inc(dve_taken, 1)
            for i in range(NT):
                n = u.number("proj", i)
                dve.wait_ge(pe_unit, n + 1)
                dve.tensor_tensor(branches[:, i, :], bank(n)[:, 0:3 * D], bias_b[:, :], ALU.add)\
                   .then_inc(dve_taken, 1)
            for o in range(ORDER):
                take_fft(f"h{o}", "D", take)
                take_spec(o, "D", take)
                take_fft(f"v{o}", "D", take)
                dve.wait_ge(act_taken, u.taken("A", u.number(f"v{o}_turn")))
                dve.wait_ge(spec_copied, 32 * (o + 1))
                for n in range(9):
                    m = u.number(f"v{o}_spec", n)
                    s = spec_blocks(n)
                    w = (s.stop - s.start) * P
                    dve.wait_ge(pe_unit, m + 1)
                    for spec, dst in ((spec_re, buf_a), (spec_im, buf_c)):
                        ins = dve.tensor_tensor(dst[:, s.start * P:s.stop * P], bank(m)[:, 0:w],
                                                spec[:, s, :].rearrange("p a b -> p (a b)"), ALU.mult)
                    ins.then_inc(dve_taken, 1)
                take_back(o, "D", take)
                for n in range(4):
                    m = u.number(f"v{o}_time", n)
                    dve.wait_ge(pe_unit, m + 1)
                    dve.tensor_tensor(branches[:, 4 * n:4 * n + 4, 2 * D:3 * D],
                                      bank(m).rearrange("p (i d) -> p i d", d=D),
                                      branches[:, 4 * n:4 * n + 4, o * D:o * D + D], ALU.mult)\
                       .then_inc(dve_taken, 1)
            take_v("D", take)
            for n in range(4):
                m = u.number("out", n)
                dve.wait_ge(pe_unit, m + 1)
                dve.tensor_tensor(y[:, 4 * n:4 * n + 4, :], bank(m).rearrange("p (i d) -> p i d", d=D),
                                  b_out[:, :].rearrange("p (o d) -> p o d", o=1).to_broadcast([P, 4, D]),
                                  ALU.add).then_inc(dve_taken, 1)
            dve.wait_ge(dve_taken, u.taken("D", len(u.who)))
            norm_y.vector_stats(dve, link, y)
            link(norm_y.vector_apply(dve, link, y, y))
            dve.tensor_tensor(x1[:, :, :], x1[:, :, :], y, ALU.add).then_inc(x1_ready, 1)

        @block.tensor
        def _(pe):
            def start_unit(name, n=0):
                m = u.number(name, n)
                if m >= NB:
                    taken(pe, m - NB + 1)
                return bank(m)

            def shifted(i, k):
                return xn_T[:, (NJ * i + k) * H1:(NJ * i + k) * H1 + P]

            pe.wait_ge(small_loaded, 16 * len(small))
            b = start_unit("small_T")
            pe.transpose(b[0:EMB, 0:HID], w1[:, :], ident[0:HID, 0:HID])
            for k in range(2):
                pe.transpose(b[0:HID, D + D * k:2 * D + D * k], w2[:, k, :], ident[:, :])
            pe.transpose(b[:, 3 * D:4 * D], w_out[:, :], ident[:, :]).then_inc(pe_unit, 1)
            taken(pe, u.number("arg"))
            for n in range(4):
                b = start_unit("arg", n)
                pe.matmul(b[0:HID, :], w1_T[:, :], pe_T[:, BANK * n:BANK * n + BANK], start=True, stop=True)\
                  .then_inc(pe_unit, 1)
            pe.wait_ge(taps_ready, 1)
            for k in range(3):
                b = start_unit("w_in_T", k)
                for c in range(3):
                    ins = pe.transpose(b[:, D * c:D * c + D], ws[:, k, c, :], ident[:, :])
                ins.then_inc(pe_unit, 1)
            b = start_unit("bias_T")
            for c in range(3):
                ins = pe.transpose(b[0:4, D * c:D * c + D], bc[:, c, :], ident[:, :])
            ins.then_inc(pe_unit, 1)
            taken(pe, u.number("bias_b"))
            pe.wait_ge(zeroed, 1)
            b = start_unit("bias_b")
            pe.matmul(b[:, 0:3 * D], ones4[:, :], bias_row[:, :], start=True, stop=True).then_inc(pe_unit, 1)
            pe.wait_ge(xn_ready, 1)
            for n in range(4):
                b = start_unit("xn_T", n)
                for i in range(4):
                    ins = pe.transpose(b[:, P * i:P * i + P], xn[:, 4 * n + i, :], ident[:, :])
                ins.then_inc(pe_unit, 1)
            pe.wait_ge(sin_ready, 1)
            for n in range(8):
                b = start_unit("filt", n)
                for i in (2 * n, 2 * n + 1):
                    ins = pe.matmul(b[:, 256 * (i % 2):256 * (i % 2) + 256], sin_T[:, P * i:P * i + P], w2_T[:, :],
                                    start=True, stop=True)
                ins.then_inc(pe_unit, 1)

            def fft(name, x):
                for n in range(8):
                    b = start_unit(name + "_first", n)
                    for i in (2 * n, 2 * n + 1):
                        ins = pe.matmul(b[:, 256 * (i % 2):256 * (i % 2) + 256], x[:, i, :], f1[:, :],
                                        start=True, stop=True)
                    ins.then_inc(pe_unit, 1)
                taken(pe, u.number(name + "_turn"))
                for n in range(8):
                    b = start_unit(name + "_turn", n)
                    for i in range(4):
                        m = 4 * n + i
                        ins = pe.transpose(b[:, P * i:P * i + P], buf_a[:, P * m:P * m + P], ident[:, :])
                    ins.then_inc(pe_unit, 1)
                taken(pe, u.number(name + "_spec"))

            def spec_unit(b, n):
                s = spec_blocks(n)
                for q, k1 in enumerate(range(s.start, s.stop)):
                    m = k1 % H1
                    ins = pe.matmul(b[:, P * q:P * q + P], m_fwd[:, k1, :], buf_b[:, P * m:P * m + P], start=True, stop=True)
                ins.then_inc(pe_unit, 1)

            pe.wait_ge(halo_ready, 1)
            for i in range(NT):
                b = start_unit("proj", i)
                edges = {0: 0, NT - 1: 1}
                for k in range(3):
                    lhs = shifted(i, k)
                    ins = pe.matmul(b[:, 0:3 * D], lhs, wk[:, k, :], start=(k == 0),
                                    stop=(k == 2 and i not in edges))
                if i in edges:
                    e = edges[i]
                    ins = pe.matmul(b[:, 0:3 * D], edge[:, e * P:e * P + P], bias_row[:, :], start=False, stop=True)
                ins.then_inc(pe_unit, 1)
            taken(pe, u.number("h0_first"))
            pe.wait_ge(filt_ready, 8)
            for o in range(ORDER):
                fft(f"h{o}", filt[:, :, o * D:o * D + D])
                pe.wait_ge(fwd_loaded, 16)
                for n in range(9):
                    spec_unit(start_unit(f"h{o}_spec", n), n)
                fft(f"v{o}", branches[:, :, 2 * D:3 * D])
                for n in range(9):
                    spec_unit(start_unit(f"v{o}_spec", n), n)
                pe.wait_ge(inv_loaded, 32)
                for n in range(8):
                    taken(pe, u.number(f"v{o}_spec", n + 2))
                    b = start_unit(f"v{o}_back", n)
                    for q in range(4):
                        k1 = 4 * n + q
                        parts = [(0, 0, R), (H1, R, R)] if k1 == 0 else [(k1, 0, P)]
                        for k, at, w in parts:
                            dst = b[:, P * q + at:P * q + at + w]
                            pe.matmul(dst, buf_a[:, P * k:P * k + P], m_inv[:, k, 0:w], start=True, stop=False)
                            ins = pe.matmul(dst, buf_c[:, P * k:P * k + P], m_inv_i[:, k, 0:w], start=False, stop=True)
                    ins.then_inc(pe_unit, 1)
                taken(pe, u.number(f"v{o}_return"))
                for n in range(8):
                    b = start_unit(f"v{o}_return", n)
                    for i in range(4):
                        m = 4 * n + i
                        ins = pe.transpose(b[:, P * i:P * i + P], buf_b[:, P * m:P * m + P], ident[:, :])
                    ins.then_inc(pe_unit, 1)
                taken(pe, u.number(f"v{o}_time"))
                for n in range(4):
                    b = start_unit(f"v{o}_time", n)
                    for jh in range(2):
                        rhs = buf_a[:, 8 * n * P:8 * (n + 1) * P].rearrange("p (i q c) -> p q i c", q=2, c=P)[:, jh]
                        ins = pe.matmul(b[R * jh:R * jh + R, :], gt[:, :], rhs, start=True, stop=True)
                    ins.then_inc(pe_unit, 1)
                taken(pe, u.number(f"v{o}_time", 4))
            for n in range(4):
                b = start_unit("v_T", n)
                for i in range(4):
                    ins = pe.transpose(b[:, P * i:P * i + P], branches[:, 4 * n + i, 2 * D:3 * D], ident[:, :])
                ins.then_inc(pe_unit, 1)
            taken(pe, u.number("out"))
            for n in range(4):
                b = start_unit("out", n)
                for i in range(4):
                    m = 4 * n + i
                    ins = pe.matmul(b[:, P * i:P * i + P], buf_a[:, P * m:P * m + P], w_out_T[:, :], start=True, stop=True)
                ins.then_inc(pe_unit, 1)




def attention_operands(nc, a, x1, z, vs, ident, scr):
    u = Units()
    u.stage("h_T", "DDDD")
    u.stage("q", "DDDD")
    u.stage("k", "DDDD")
    u.stage("v", "DDDD")
    with ExitStack() as ctx:
        def sb(name, shape, dt=F32):
            return ctx.enter_context(nc.sbuf_tensor("op_" + name, shape, dt))

        def sem(name):
            return ctx.enter_context(nc.semaphore("op_" + name))

        ps = ctx.enter_context(nc.psum_tensor("op_ps", [P, NB, BANK], F32))
        zn = sb("zn", [P, NT, D])
        h_T = sb("h_T", [P, L])
        w = {n: sb("w" + n, [P, D]) for n in "qkv"}
        bias = {n: sb("bias_" + n, [P, 1]) for n in "qk"}
        bias_v = sb("bias_v", [P, D])
        g1 = sb("g1", [P, 1])
        be1 = sb("be1", [P, 1])
        full = {n: sb("full_" + n, [P, L]) for n in "qk"}
        parts = {n: [sb(f"part_{n}{i}", [P, L], BF16) for i in range(3)] for n in "qk"}
        norm_1 = Norm(nc, sb, sem, "norm_1")
        norm_2 = Norm(nc, sb, sem, "norm_2")

        loaded = sem("loaded")
        chain_d = sem("chain")
        pe_unit = sem("pe_unit")
        taken = sem("taken")
        zn_ready = sem("zn_ready")
        ones_ready = sem("ones_ready")
        full_ready = sem("full_ready")
        part1_ready = sem("part1_ready")
        part2_ready = sem("part2_ready")
        rest1_ready = sem("rest1_ready")
        part3_ready = sem("part3_ready")
        stored = sem("parts_stored")
        col = lambda v: v.rearrange("(p o) -> p o", o=1)
        loads = [(w[n][:, :], a["w" + n]) for n in "qkv"]
        loads += [(bias[n][:, :], col(a["b" + n])) for n in "qk"]
        loads += [(bias_v[:, :], bcast_rows(a["bv"], P)), (g1[:, :], col(a["ln1_g"])), (be1[:, :], col(a["ln1_b"]))]

        def bank(name, n):
            return ps[:, u.number(name, n) % NB, :]

        block = ctx.enter_context(nc.Block())

        @block.sync
        def _(sp):
            for dst, src in loads:
                sp.dma_start(dst, src).then_inc(loaded, 16)
            for m, n in enumerate("qk"):
                for i, s in enumerate((part1_ready, part2_ready, part3_ready)):
                    sp.wait_ge(s, m + 1)
                    sp.dma_start(scr[n][:, i, :, :], parts[n][i][:, :]).then_inc(stored, 16)
            sp.wait_ge(stored, 96)

        @block.gpsimd
        def _(pool):
            pool.memset(vs[:, :, :, HD:HD + 1], 1.0).then_inc(ones_ready, 1)

        @block.scalar
        def _(act):
            norm_1.scalar_sqrt(act)
            norm_2.scalar_sqrt(act)
            for m, n in enumerate("qk"):
                act.wait_ge(full_ready, m + 1)
                act.activation(parts[n][0][:, :], full[n][:, :], ACT.Copy).then_inc(part1_ready, 1)
                act.wait_ge(rest1_ready, m + 1)
                act.activation(parts[n][1][:, :], full[n][:, :], ACT.Copy).then_inc(part2_ready, 1)

        @block.vector
        def _(dve):
            link = chain(dve, chain_d)
            norm_1.vector_stats(dve, link, x1)
            link(norm_1.vector_apply(dve, link, z, x1))
            norm_2.vector_stats(dve, link, z)
            norm_2.vector_apply(dve, link, zn, z).then_inc(zn_ready, 1)
            dve.wait_ge(loaded, 16 * len(loads))
            for n in range(4):
                dve.wait_ge(pe_unit, u.number("h_T", n) + 1)
                dve.tensor_scalar(h_T[:, BANK * n:BANK * n + BANK], bank("h_T", n), g1[:, 0:1], be1[:, 0:1],
                                  ALU.mult, ALU.add).then_inc(taken, 1)
            for m, name in enumerate("qk"):
                scale = HD ** -0.5 if name == "q" else 1.0
                for n in range(4):
                    dve.wait_ge(pe_unit, u.number(name, n) + 1)
                    dve.tensor_scalar(full[name][:, BANK * n:BANK * n + BANK], bank(name, n),
                                      bias[name][:, 0:1], scale, ALU.add, ALU.mult).then_inc(taken, 1)
                dve.wait_ge(taken, u.number(name, 4))
                dve.nop().then_inc(full_ready, 1)
            for m, name in enumerate("qk"):
                dve.wait_ge(part1_ready, m + 1)
                dve.tensor_tensor(full[name][:, :], full[name][:, :], parts[name][0][:, :], ALU.subtract)\
                   .then_inc(rest1_ready, 1)
            for n in range(4):
                dve.wait_ge(pe_unit, u.number("v", n) + 1)
                dve.tensor_tensor(
                    vs[:, :, 4 * n:4 * n + 4, 0:HD].rearrange("p h i e -> p i h e"),
                    bank("v", n).rearrange("p (i h e) -> p i h e", i=4, h=NH),
                    bias_v[:, :].rearrange("p (o h e) -> p o h e", o=1, h=NH).to_broadcast([P, 4, NH, HD]),
                    ALU.add).then_inc(taken, 1)
            for m, name in enumerate("qk"):
                dve.wait_ge(part2_ready, m + 1)
                dve.tensor_tensor(parts[name][2][:, :], full[name][:, :], parts[name][1][:, :], ALU.subtract)\
                   .then_inc(part3_ready, 1)

        @block.tensor
        def _(pe):
            pe.wait_ge(zn_ready, 1)
            for n in range(4):
                for i in range(4):
                    ins = pe.transpose(bank("h_T", n)[:, P * i:P * i + P], zn[:, 4 * n + i, :], ident[:, :])
                ins.then_inc(pe_unit, 1)
            pe.wait_ge(loaded, 16 * len(loads))
            for name in "qk":
                for n in range(4):
                    pe.wait_ge(taken, n + 1 if name == "q" else 4)
                    pe.matmul(bank(name, n), w[name][:, :], h_T[:, BANK * n:BANK * n + BANK], start=True, stop=True)\
                      .then_inc(pe_unit, 1)
            for n in range(4):
                pe.wait_ge(taken, u.number("v", n) - NB + 1)
                for i in range(4):
                    m = 4 * n + i
                    ins = pe.matmul(bank("v", n)[:, P * i:P * i + P], h_T[:, P * m:P * m + P], w["v"][:, :],
                                    start=True, stop=True)
                ins.then_inc(pe_unit, 1)


PARTS = 3
ROWS = PARTS * PARTS * HD
MROW = 96
assert ROWS <= MROW
G = 3
AHEAD = NT + 4
CHUNK = L // BANK
N_STEP = NH * NT


def attention(nc, vs, ident, scr):
    loops = (NH - 1) // G
    assert loops * G == NH - 1
    body = G * NT
    with ExitStack() as ctx:
        def sb(name, shape, dt=F32):
            return ctx.enter_context(nc.sbuf_tensor("at_" + name, shape, dt))

        def sem(name):
            return ctx.enter_context(nc.semaphore("at_" + name))

        ps_s = ctx.enter_context(nc.psum_tensor("ps_s", [P, 2, 2 * BANK], F32))
        ps_m = ctx.enter_context(nc.psum_tensor("ps_m", [P, 3, BANK], F32))
        ps_o = ctx.enter_context(nc.psum_tensor("ps_o", [P, BANK], F32))
        ps_t = ps_s[:, 1, 0:P // 2].bitcast(BF16)
        q_op = [sb(f"q_op{b}", [P, L], BF16) for b in range(G)]
        k_op = [sb(f"k_op{b}", [P, L], BF16) for b in range(G)]
        v_op = [sb(f"v_op{b}", [P, NT, 32]) for b in range(G)]
        prob = [sb(f"prob{b}", [P, L]) for b in range(3)]
        o_out = [sb(f"o_out{b}", [P, BANK]) for b in range(G)]
        ident_b = sb("ident_b", [P, P], BF16)
        maxes = sb("maxes", [P, NT, CHUNK])
        neg = sb("neg", [P, NT])
        neg_parts = sb("neg_parts", [P, P], BF16)
        neg_T = sb("neg_T", [PARTS * NT, P], BF16)

        zeroed = sem("zeroed")
        pool_chain = sem("pool_chain")
        op_loaded = [sem(f"op_loaded{b}") for b in range(G)]
        score_ready = sem("score_ready")
        exp_done = sem("exp_done")
        max_mm = sem("max_mm")
        max_done = sem("max_done")
        pv_done = sem("pv_done")
        neg_chain = sem("neg_chain")
        neg_ready = sem("neg_ready")
        neg_turned = sem("neg_turned")
        neg_T_ready = sem("neg_T_ready")
        row_loaded = sem("neg_row_loaded")
        v_ready = sem("v_ready")
        o_taken = sem("o_taken")
        o_stored = [sem(f"o_stored{b}") for b in range(G)]

        N_LOAD = 4
        TURN = 12
        FREE_SCORE, FREE_MAX, FREE_PROB = 2, 3, 3

        block = ctx.enter_context(nc.Block())

        @block.sync
        def _(sp):
            def load(h, b):
                q = scr["q"][bass.ds(h, 1)].rearrange("o a e t -> (o a e) t")
                sp.dma_start(q_op[b][0:ROWS, :],
                             q.rearrange("(o r) t -> o r t", o=1).to_broadcast([PARTS, PARTS * HD, L]))\
                  .then_inc(op_loaded[b], 16)
                for c in range(PARTS):
                    k = scr["k"][bass.ds(h, 1), c:c + 1].rearrange("o a e t -> (o a e) t")
                    sp.dma_start(k_op[b][PARTS * HD * c:PARTS * HD * (c + 1), :],
                                 k.rearrange("(o e) t -> o e t", o=1).to_broadcast([PARTS, HD, L]))\
                      .then_inc(op_loaded[b], 16)

            def neg_rows(h, b):
                sp.wait_ge(neg_T_ready, h + 1)
                sp.dma_start(q_op[b][MROW:MROW + PARTS, :], neg_T[:, :]).then_inc(row_loaded, 16)

            def store(h, b):
                sp.wait_ge(o_taken, h + 2)
                for j in range(CHUNK):
                    sp.dma_start(scr["o"][bass.ds(h, 1), :, BANK * j:BANK * j + BANK].rearrange("o e q -> (o e) q"),
                                 o_out[b][32 * j:32 * j + HD + 1, :]).then_inc(o_stored[b], 16)

            def head(h, r, load_next):
                neg_rows(h + 1, (r + 1) % G)
                sp.wait_ge(score_ready, (h + 1) * (2 * NT))
                if load_next:
                    load(h + G, r)
                elif h == NH - G:
                    sp.nop().then_inc(op_loaded[NH % G], 16 * N_LOAD)
                store(h, r)

            sp.wait_ge(zeroed, 1)
            for b in range(G):
                load(b, b)
            neg_rows(0, 0)
            with sp.Fori(0, loops - 1) as it:
                for r in range(G):
                    head(it * G + r, r, True)
            for h in range((loops - 1) * G, NH - 1):
                head(h, h % G, h + G < NH)
            store(NH - 1, (NH - 1) % G)
            for b in range(G):
                sp.wait_ge(o_stored[b], 16 * CHUNK * (1 + len(range(b, NH, G))))

        @block.gpsimd
        def _(pool):
            link = chain(pool, pool_chain)
            for b in range(G):
                link(pool.memset(q_op[b][:, :].bitcast(F32), 0.0))
                link(pool.memset(k_op[b][:, :].bitcast(F32), 0.0))
                link(pool.memset(k_op[b][MROW:MROW + PARTS, :], 1.0))
                link(pool.memset(v_op[b][:, :, :], 0.0))
            link(pool.memset(neg_parts[:, :], 0.0))
            link(pool.tensor_copy(ident_b[:, :], ident[:, :]))
            pool.nop().then_inc(zeroed, 1)
            for h in range(G):
                pool.tensor_copy(v_op[h][:, :, 0:HD + 1], vs[:, h, :, :]).then_inc(v_ready, 1)
            with pool.Fori(0, loops - 1) as it:
                for r in range(G):
                    pool.wait_ge(pv_done, it * body + (FREE_PROB + (r + 1) * NT))
                    pool.tensor_copy(v_op[r][:, :, 0:HD + 1], vs[:, bass.ds(it * G + (G + r), 1), :, :]
                                     .rearrange("p o i e -> p (o i) e")).then_inc(v_ready, 1)
            pool.wait_ge(pv_done, FREE_PROB + (NH - G) * NT)
            pool.tensor_copy(v_op[(NH - 1) % G][:, :, 0:HD + 1], vs[:, NH - 1, :, :]).then_inc(v_ready, 1)

        @block.scalar
        def _(act):
            def exps(s, n):
                for half in range(2):
                    act.wait_ge(score_ready, s * 2 + (half + 1))
                    if half == 0:
                        act.wait_ge(pv_done, s + 1)
                    act.activation(prob[n % 3][:, 2 * BANK * half:2 * BANK * (half + 1)], ps_s[:, half, :], ACT.Exp)\
                       .then_inc(exp_done, 1)

            def take_neg(h, first=False):
                act.wait_ge(neg_turned, h + 1)
                if not first:
                    act.wait_ge(row_loaded, h * 16)
                act.activation(neg_T[:, :], ps_t[0:PARTS * NT, 0:P], ACT.Copy).then_inc(neg_T_ready, 1)

            def take_out(h, it, r):
                act.wait_ge(pv_done, h * NT + (FREE_PROB + NT))
                act.wait_ge(o_stored[r], it * (16 * CHUNK) + 16 * CHUNK)
                act.activation(o_out[r][:, :], ps_o[:, :], ACT.Copy).then_inc(o_taken, 1)

            act.nop().then_inc(exp_done, FREE_SCORE)
            act.nop().then_inc(o_taken, 1)
            for b in range(G):
                act.nop().then_inc(o_stored[b], 16 * CHUNK)
            take_neg(0, first=True)
            exps(0, 0)
            with act.Fori(0, loops) as it:
                for q in range(body):
                    if q % NT == TURN:
                        take_neg(it * G + (q // NT + 1))
                    exps(it * body + (q + 1), q + 1)
                    if q % NT == NT - 1:
                        take_out(it * G + q // NT, it, q // NT)
            for s in range(loops * body + 1, N_STEP):
                exps(s, s)
            take_out(NH - 1, loops, 0)

        @block.vector
        def _(dve):
            def maxima(t, n):
                for c in range(CHUNK):
                    dve.wait_ge(max_mm, t * CHUNK + (c + 1))
                    dve.tensor_reduce(maxes[:, n % NT, c:c + 1], ps_m[:, (n * CHUNK + c) % 3, :], AX.X, ALU.max)\
                       .then_inc(max_done, 1)

            def negate(h, first=False):
                dve.wait_ge(max_done, h * (NT * CHUNK) + (FREE_MAX + NT * CHUNK))
                dve.tensor_reduce(neg[:, :], maxes[:, :, :], AX.X, ALU.max, negate=True).then_inc(neg_chain, 1)
                dve.wait_ge(neg_chain, h * 4 + 1)
                if not first:
                    dve.wait_ge(neg_turned, h)
                part = [neg_parts[:, NT * i:NT * (i + 1)] for i in range(PARTS)]
                dve.tensor_copy(part[0], neg[:, :]).then_inc(neg_chain, 1)
                dve.wait_ge(neg_chain, h * 4 + 2)
                dve.tensor_tensor(neg[:, :], neg[:, :], part[0], ALU.subtract).then_inc(neg_chain, 1)
                dve.wait_ge(neg_chain, h * 4 + 3)
                dve.tensor_copy(part[1], neg[:, :]).then_inc(neg_chain, 1)
                dve.wait_ge(neg_chain, h * 4 + 4)
                dve.tensor_tensor(part[2], neg[:, :], part[1], ALU.subtract)\
                   .then_inc(neg_ready, 1)

            dve.nop().then_inc(max_done, FREE_MAX)
            dve.wait_ge(zeroed, 1)
            for t in range(AHEAD + 1):
                maxima(t, t)
                if t == NT - 1:
                    negate(0, first=True)
            with dve.Fori(0, loops) as it:
                for q in range(body):
                    n = q + 1 + AHEAD
                    maxima(it * body + n, n)
                    if n % NT == NT - 1:
                        negate(it * G + n // NT)

        @block.tensor
        def _(pe):
            def scores(s, n, halves=range(2)):
                b, k = n // NT % G, n % NT
                for half in halves:
                    pe.wait_ge(exp_done, s * 2 + (half + 1))
                    for c in range(2):
                        at = BANK * (2 * half + c)
                        ins = pe.matmul(ps_s[:, half, BANK * c:BANK * (c + 1)], k_op[b][:, P * k:P * (k + 1)],
                                        q_op[b][:, at:at + BANK], start=True, stop=True)
                    ins.then_inc(score_ready, 1)

            def max_scores(t, n, it, banks=range(CHUNK)):
                b, i = n // NT % G, n % NT
                if i == 0 and banks[0] == 0:
                    pe.wait_ge(op_loaded[b], (it + n // NT // G + 1) * (16 * N_LOAD))
                for c in banks:
                    pe.wait_ge(max_done, t * CHUNK + (c + 1))
                    pe.matmul(ps_m[:, (n * CHUNK + c) % 3, :], q_op[b][0:MROW, P * i:P * (i + 1)],
                              k_op[b][0:MROW, BANK * c:BANK * (c + 1)], start=True, stop=True).then_inc(max_mm, 1)

            def turn_neg(h, s):
                pe.wait_ge(neg_ready, h + 1)
                pe.wait_ge(exp_done, s * 2 + 2)
                pe.transpose(ps_t[:, 0:P], neg_parts[:, :], ident_b[:, :]).then_inc(neg_turned, 1)

            def outputs(s, n, h):
                b, k = n // NT % G, n % NT
                if k == 0:
                    pe.wait_ge(v_ready, h + 1)
                    pe.wait_ge(o_taken, h + 1)
                pe.wait_ge(exp_done, s * 2 + (FREE_SCORE + 2))
                for j in range(CHUNK):
                    ins = pe.matmul(ps_o[32 * j:32 * j + 32, :], v_op[b][:, k, :],
                                    prob[n % 3][:, BANK * j:BANK * (j + 1)], start=(k == 0), stop=(k == NT - 1))
                ins.then_inc(pv_done, 1)

            pe.nop().then_inc(pv_done, FREE_PROB)
            for t in range(AHEAD + 1):
                max_scores(t, t, 0)
                if t == NT + 1:
                    turn_neg(0, 0)
            pe.wait_ge(row_loaded, 16)
            scores(0, 0)
            with pe.Fori(0, loops) as it:
                for q in range(body):
                    n = q + 1
                    if n % NT == 0:
                        pe.wait_ge(row_loaded, it * (16 * G) + (n // NT + 1) * 16)
                    m = n + AHEAD
                    turned = q % NT == TURN
                    if turned:
                        turn_neg(it * G + (q // NT + 1), it * body + n)
                    max_scores(it * body + m, m, it, [0])
                    scores(it * body + n, n, [0])
                    max_scores(it * body + m, m, it, [1])
                    if turned:
                        pe.wait_ge(neg_T_ready, it * G + (q // NT + 2))
                    scores(it * body + n, n, [1])
                    max_scores(it * body + m, m, it, [2, 3])
                    outputs(it * body + q, q, it * G + q // NT)
            for s in range(loops * body + 1, N_STEP):
                scores(s, s)
                outputs(s - 1, s - 1, NH - 1)
            outputs(N_STEP - 1, N_STEP - 1, NH - 1)


def attention_output(nc, a, z, h_T, ident, scr):
    with ExitStack() as ctx:
        def sb(name, shape, dt=F32):
            return ctx.enter_context(nc.sbuf_tensor("ao_" + name, shape, dt))

        def sem(name):
            return ctx.enter_context(nc.semaphore("ao_" + name))

        ps = ctx.enter_context(nc.psum_tensor("ao_ps", [P, NB, BANK], F32))
        o_T = sb("o_T", [P, L])
        sums = sb("sums", [P, L])
        wo = sb("wo", [P, D])
        bo = sb("bo", [P, D])
        g2 = sb("g2", [P, 1])
        be2 = sb("be2", [P, 1])
        zn = sb("zn2", [P, NT, D])
        norm_3 = Norm(nc, sb, sem, "norm_3")
        loaded = sem("loaded")
        heads_loaded = sem("heads_loaded")
        chain_d = sem("chain")
        o_ready = sem("o_ready")
        pe_unit = sem("pe_unit")
        zn_ready = sem("zn2_ready")
        taken = sem("taken")
        col = lambda v: v.rearrange("(p o) -> p o", o=1)
        loads = [(wo[:, :], a["wo"]), (bo[:, :], bcast_rows(a["bo"], P)), (g2[:, :], col(a["ln2_g"])),
                 (be2[:, :], col(a["ln2_b"]))]
        block = ctx.enter_context(nc.Block())

        @block.sync
        def _(sp):
            sp.dma_start(sums[:, :], scr["o"][:, HD:HD + 1, :].to_broadcast([NH, HD, L])).then_inc(heads_loaded, 16)
            sp.dma_start(o_T[:, :], scr["o"][:, 0:HD, :]).then_inc(heads_loaded, 16)
            for dst, src in loads:
                sp.dma_start(dst, src).then_inc(loaded, 16)

        @block.scalar
        def _(act):
            norm_3.scalar_sqrt(act)

        @block.vector
        def _(dve):
            link = chain(dve, chain_d)
            dve.wait_ge(loaded, 16 * len(loads))
            dve.tensor_tensor(z[:, :, :], z[:, :, :],
                              bo[:, :].rearrange("p (o d) -> p o d", o=1).to_broadcast([P, NT, D]), ALU.add)
            dve.wait_ge(heads_loaded, 32)
            for n in range(4):
                c = slice(BANK * n, BANK * n + BANK)
                link(dve.reciprocal(sums[:, c], sums[:, c]))
                dve.tensor_tensor(o_T[:, c], o_T[:, c], sums[:, c], ALU.mult).then_inc(o_ready, 1)
            for n in range(4):
                dve.wait_ge(pe_unit, n + 1)
                ins = dve.tensor_tensor(z[:, 4 * n:4 * n + 4, :], ps[:, n, :].rearrange("p (i d) -> p i d", d=D),
                                        z[:, 4 * n:4 * n + 4, :], ALU.add)
            link(ins)
            norm_3.vector_stats(dve, link, z)
            norm_3.vector_apply(dve, link, zn, z).then_inc(zn_ready, 1)
            for n in range(4):
                dve.wait_ge(pe_unit, 4 + n + 1)
                dve.tensor_scalar(h_T[:, BANK * n:BANK * n + BANK], ps[:, 4 + n, :], g2[:, 0:1], be2[:, 0:1],
                                  ALU.mult, ALU.add).then_inc(taken, 1)

        @block.tensor
        def _(pe):
            for n in range(4):
                pe.wait_ge(o_ready, n + 1)
                if n == 0:
                    pe.wait_ge(loaded, 16 * len(loads))
                for i in range(4):
                    m = 4 * n + i
                    ins = pe.matmul(ps[:, n, P * i:P * i + P], o_T[:, P * m:P * m + P], wo[:, :], start=True, stop=True)
                ins.then_inc(pe_unit, 1)
            pe.wait_ge(zn_ready, 1)
            for n in range(4):
                for i in range(4):
                    ins = pe.transpose(ps[:, 4 + n, P * i:P * i + P], zn[:, 4 * n + i, :], ident[:, :])
                ins.then_inc(pe_unit, 1)


FT = FF // P


def experts(nc, a, x1, z, h_T, ident, out):
    steps = NE * CHUNK
    body = 2 * CHUNK
    loops = NE // 2 - 1
    with ExitStack() as ctx:
        def sb(name, shape, dt=F32):
            return ctx.enter_context(nc.sbuf_tensor("ex_" + name, shape, dt))

        def sem(name):
            return ctx.enter_context(nc.semaphore("ex_" + name))

        ps_h = ctx.enter_context(nc.psum_tensor("ps_h", [P, FT, BANK], F32))
        ps_y = ctx.enter_context(nc.psum_tensor("ps_y", [P, 2, BANK], F32))
        ps_r = ctx.enter_context(nc.psum_tensor("ps_r", [P, 2, BANK], F32))
        w1 = [sb(f"ew1_{b}", [P, FF]) for b in range(2)]
        w2 = [sb(f"ew2_{b}", [P, FT, D]) for b in range(2)]
        hid = [[sb(f"hid{b}_{f}", [P, BANK]) for f in range(FT)] for b in range(2)]
        b1_rows = sb("b1_rows", [NE * FT, P])
        b1_T = sb("b1_T", [P, NE * FT])
        b1_e = [sb(f"b1_e{b}", [P, FT]) for b in range(2)]
        b2 = sb("b2_rows", [NE, D])
        wr = sb("wr", [P, NE])
        order = sb("order", [P, 3, P])
        ones = sb("ones_p", [P, P])
        rank = sb("rank", [P, NE])
        logits = sb("logits", [P, NT, NE])
        masked = sb("masked", [P, NT, NE])
        probs = sb("probs", [P, NT, NE])
        cand = sb("cand", [P, NT, NE])
        peak = sb("peak", [P, NT])
        chosen = sb("chosen", [P, NT, 2, NE])
        upto = [sb(f"upto{b}", [P, NT, 2 * NE]) for b in range(2)]
        before = sb("before_tile", [P, NT, 2 * NE])
        kept = sb("kept", [P, NT, 2, NE])
        part = sb("part", [P, NT, 2, NE])
        share = sb("share", [P, NT, 2])
        total = sb("total", [P, NT])
        gate = sb("gate", [P, NE, NT])
        gate_e = [sb(f"gate_e{b}", [P, NT]) for b in range(2)]
        gate_T = sb("gate_T", [NE, L])
        norm_4 = Norm(nc, sb, sem, "norm_4")

        loaded = sem("loaded")
        w_loaded = [sem(f"w_loaded{b}") for b in range(2)]
        consts = sem("consts")
        pool_chain = sem("pool_chain")
        rank_chain = sem("rank_chain")
        chain_d = sem("chain")
        b1_turned = sem("b1_turned")
        b1_ready = sem("b1_ready")
        b1_e_ready = sem("b1_e_ready")
        logits_mm = sem("logits_mm")
        shifted_ready = sem("shifted_ready")
        exp_ready = sem("router_exp_ready")
        counts_ready = sem("counts_ready")
        count_mm = sem("count_mm")
        gate_ready = sem("gate_ready")
        gate_e_ready = sem("gate_e_ready")
        gate_turned = sem("gate_turned")
        gate_T_ready = sem("gate_T_ready")
        bias_mm = sem("bias_mm")
        hid_mm = sem("hid_mm")
        hid_ready = sem("hid_ready")
        y_mm = sem("y_mm")
        y_taken = sem("y_taken")
        out_ready = sem("out_ready")
        out_stored = sem("out_stored")

        block = ctx.enter_context(nc.Block())
        w1_v = a["w1"]
        w2_v = a["w2"].rearrange("e (f p) d -> e p f d", p=P)

        @block.sync
        def _(sp):
            def load(e, b):
                sp.dma_start(w1[b][:, :], w1_v[bass.ds(e, 1)].rearrange("o p f -> (o p) f")).then_inc(w_loaded[b], 16)
                sp.dma_start(w2[b][:, :, :], w2_v[bass.ds(e, 1)].rearrange("o p f d -> (o p) f d"))\
                  .then_inc(w_loaded[b], 16)

            loads = [(b1_rows[:, :], a["b1"].rearrange("e (f p) -> (e f) p", p=P)), (wr[:, :], a["wr"]),
                     (order[:, :, :].rearrange("p k q -> p (k q)"), a["c_before"]), (b2[:, :], a["b2"])]
            for dst, src in loads:
                sp.dma_start(dst, src).then_inc(loaded, 16)
            load(0, 0)
            load(1, 1)
            with sp.Fori(0, loops) as it:
                for b in range(2):
                    sp.wait_ge(y_mm, it * body + CHUNK * (b + 1))
                    load(it * 2 + (b + 2), b)
            sp.wait_ge(out_ready, 1)
            for j, v in enumerate(tiles_of(out)):
                sp.dma_start(v, x1[H1 * j:H1 * j + H1, :, :]).then_inc(out_stored, 16)
            sp.wait_ge(out_stored, 16 * NJ)

        @block.gpsimd
        def _(pool):
            link = chain(pool, pool_chain)
            link(pool.memset(ones[:, :], 1.0))
            for e in range(NE):
                link(pool.memset(rank[:, e:e + 1], float(NE - e)))
            pool.nop().then_inc(consts, 1)

        @block.scalar
        def _(act):
            act.wait_ge(shifted_ready, 1)
            act.activation(probs[:, :, :], cand[:, :, :], ACT.Exp).then_inc(exp_ready, 1)
            act.wait_ge(b1_turned, 1)
            act.activation(b1_T[:, :], ps_r[:, 1, 0:NE * FT], ACT.Copy).then_inc(b1_ready, 1)
            act.wait_ge(b1_ready, 1)

            def bias_of(e, b):
                act.activation(b1_e[b][:, :], b1_T[:, bass.ds(e * FT, FT)], ACT.Copy).then_inc(b1_e_ready, 1)
                act.wait_ge(b1_e_ready, e + 1)

            def hidden(s, n, e):
                b = n // CHUNK % 2
                if n % CHUNK == 0:
                    bias_of(e, b)
                for f in range(FT):
                    act.wait_ge(hid_mm, s * FT + (f + 1))
                    if f == 0 and not (isinstance(s, int) and s < 2):
                        act.wait_ge(y_mm, s - 1)
                    act.activation(hid[n % 2][f][:, :], ps_h[:, f, :], ACT.Relu, bias=b1_e[b][:, f:f + 1])\
                       .then_inc(hid_ready, 1)

            hidden(0, 0, 0)
            hidden(1, 1, 0)
            with act.Fori(0, loops) as it:
                for q in range(2, body + 2):
                    hidden(it * body + q, q, it * 2 + q // CHUNK)
            for s in range(loops * body + 2, steps):
                hidden(s, s, s // CHUNK)
            norm_4.scalar_sqrt(act)

        @block.vector
        def _(dve):
            link = chain(dve, chain_d)
            wide = lambda v: v.rearrange("p (i o) -> p i o", o=1).to_broadcast([P, NT, NE])
            rank_b = rank[:, :].rearrange("p (o e) -> p o e", o=1).to_broadcast([P, NT, NE])

            def choose(values, w):
                link(dve.tensor_reduce(peak[:, :], values[:, :, :], AX.X, ALU.max))
                link(dve.tensor_tensor(cand[:, :, :], values[:, :, :], wide(peak[:, :]), ALU.is_ge))
                link(dve.tensor_tensor(cand[:, :, :], cand[:, :, :], rank_b, ALU.mult))
                link(dve.tensor_reduce(peak[:, :], cand[:, :, :], AX.X, ALU.max))
                link(dve.tensor_tensor(chosen[:, :, w, :], rank_b, wide(peak[:, :]), ALU.is_equal))

            dve.wait_ge(logits_mm, 1)
            link(dve.tensor_copy(logits[:, :, :], ps_r[:, 0, 0:NT * NE].rearrange("p (i e) -> p i e", e=NE)))
            link(dve.tensor_reduce(peak[:, :], logits[:, :, :], AX.X, ALU.max))
            dve.tensor_tensor(cand[:, :, :], logits[:, :, :], wide(peak[:, :]), ALU.subtract).then_inc(shifted_ready, 1)
            dve.wait_ge(exp_ready, 1)
            link(dve.tensor_reduce(total[:, :], probs[:, :, :], AX.X, ALU.add))
            link(dve.reciprocal(total[:, :], total[:, :]))
            link(dve.tensor_tensor(probs[:, :, :], probs[:, :, :], wide(total[:, :]), ALU.mult))
            dve.wait_ge(consts, 1)
            choose(probs, 0)
            link(dve.scalar_tensor_tensor(out=masked[:, :, :], in0=chosen[:, :, 0, :], scalar=-3.0e38,
                                          in1=logits[:, :, :], op0=ALU.mult, op1=ALU.add))
            choose(masked, 1)
            now = chosen[:, :, :, :].rearrange("p i w e -> p i (w e)")
            for k in range(NT.bit_length() - 1):
                to = upto[k % 2]
                dist = 1 << k
                dve.tensor_copy(to[:, 0:dist, :], now[:, 0:dist, :])
                link(dve.tensor_tensor(to[:, dist:NT, :], now[:, dist:NT, :], now[:, 0:NT - dist, :], ALU.add))
                now = to[:, :, :]
            dve.tensor_tensor(before[:, :, :], now, chosen[:, :, :, :].rearrange("p i w e -> p i (w e)"),
                              ALU.subtract).then_inc(counts_ready, 1)
            dve.wait_ge(count_mm, 1)
            flat = lambda t: t[:, :, :, :].rearrange("p i w e -> p (i w e)")
            link(dve.scalar_tensor_tensor(out=flat(kept), in0=ps_r[:, 0, 0:2 * NT * NE], scalar=float(CAP),
                                          in1=flat(chosen), op0=ALU.is_le, op1=ALU.mult))
            for w in range(2):
                ins = dve.tensor_tensor(part[:, :, w, :], kept[:, :, w, :], probs[:, :, :], ALU.mult)
            link(ins)
            link(dve.tensor_reduce(share[:, :, :].rearrange("p i w -> p (i w)"),
                                   part[:, :, :, :].rearrange("p i w e -> p (i w) e"), AX.X, ALU.add))
            link(dve.tensor_tensor(total[:, :], share[:, :, 0], share[:, :, 1], ALU.add))
            link(dve.tensor_scalar(total[:, :], total[:, :], float(np.finfo(np.float32).eps), None, ALU.max))
            link(dve.reciprocal(total[:, :], total[:, :]))
            link(dve.tensor_scalar(total[:, :], total[:, :], KEEP, None, ALU.mult))
            link(dve.tensor_tensor(part[:, :, 0, :], part[:, :, 0, :], part[:, :, 1, :], ALU.add))
            link(dve.tensor_tensor(gate[:, :, :].rearrange("p e i -> p i e"), part[:, :, 0, :], wide(total[:, :]),
                                   ALU.mult))
            dve.nop().then_inc(gate_ready, 1)
            dve.nop().then_inc(y_taken, 2)

            def outputs(s, n, e):
                b = n // CHUNK % 2
                if n % CHUNK == 0:
                    dve.tensor_copy(gate_e[b][:, :], gate[:, bass.ds(e, 1), :].rearrange("p o i -> p (o i)"))\
                       .then_inc(gate_e_ready, 1)
                    dve.wait_ge(gate_e_ready, e + 1)
                dve.wait_ge(y_mm, s + 1)
                dve.wait_ge(y_taken, s + 2)
                for i in range(4):
                    m = 4 * (n % CHUNK) + i
                    ins = dve.scalar_tensor_tensor(out=z[:, m, :], in0=ps_y[:, n % 2, P * i:P * i + P],
                                                   scalar=gate_e[b][:, m:m + 1], in1=z[:, m, :],
                                                   op0=ALU.mult, op1=ALU.add)
                ins.then_inc(y_taken, 1)

            with dve.Fori(0, loops + 1) as it:
                for q in range(body):
                    outputs(it * body + q, q, it * 2 + q // CHUNK)
            for n in range(4):
                dve.wait_ge(gate_turned, n + 1)
                dve.tensor_copy(gate_T[:, BANK * n:BANK * n + BANK], ps_r[0:NE, n % 2, :]).then_inc(gate_T_ready, 1)
            dve.wait_ge(y_taken, steps + 2)
            for n in range(4):
                dve.wait_ge(bias_mm, n + 1)
                ins = dve.tensor_tensor(z[:, 4 * n:4 * n + 4, :], ps_h[:, n, :].rearrange("p (i d) -> p i d", d=D),
                                        z[:, 4 * n:4 * n + 4, :], ALU.add)
            link(ins)
            norm_4.vector_stats(dve, link, z)
            link(norm_4.vector_apply(dve, link, z, z))
            dve.tensor_tensor(x1[:, :, :], x1[:, :, :], z[:, :, :], ALU.add).then_inc(out_ready, 1)

        @block.tensor
        def _(pe):
            def hidden(s, n, it):
                b, c = n // CHUNK % 2, n % CHUNK
                if c == 0:
                    pe.wait_ge(w_loaded[b], (it + n // body + 1) * 32)
                for f in range(FT):
                    if not (isinstance(s, int) and s == 0):
                        pe.wait_ge(hid_ready, (s - 1) * FT + (f + 1))
                    pe.matmul(ps_h[:, f, :], w1[b][:, P * f:P * f + P], h_T[:, BANK * c:BANK * c + BANK],
                              start=True, stop=True).then_inc(hid_mm, 1)

            def second(s, n):
                b = n // CHUNK % 2
                pe.wait_ge(hid_ready, s * FT + FT)
                pe.wait_ge(y_taken, s + 1)
                for i in range(4):
                    for f in range(FT):
                        ins = pe.matmul(ps_y[:, n % 2, P * i:P * i + P], hid[n % 2][f][:, P * i:P * i + P],
                                        w2[b][:, f, :], start=(f == 0), stop=(f == FT - 1))
                ins.then_inc(y_mm, 1)

            pe.wait_ge(loaded, 64)
            for i in range(NT):
                ins = pe.matmul(ps_r[:, 0, NE * i:NE * i + NE], h_T[:, P * i:P * i + P], wr[:, :], start=True, stop=True)
            ins.then_inc(logits_mm, 1)
            pe.transpose(ps_r[:, 1, 0:NE * FT], b1_rows[:, :], ident[0:NE * FT, 0:NE * FT]).then_inc(b1_turned, 1)
            hidden(0, 0, 0)
            pe.wait_ge(counts_ready, 1)
            pe.wait_ge(consts, 1)
            w = 2 * NE
            last = upto[(NT.bit_length() - 2) % 2][:, NT - 1:NT, :]
            cnt = ps_r[:, 0, 0:NT * w]
            pe.matmul(cnt, order[:, 0, :], last.to_broadcast([P, NT, w]), start=True, stop=False)
            pe.matmul(cnt, order[:, 1, :], before[:, :, :], start=False, stop=False)
            pe.matmul(cnt.rearrange("p (i w) -> p i w", w=w)[:, :, NE:w], ones[:, :],
                      last[:, :, 0:NE].to_broadcast([P, NT, NE]), start=False, stop=False, skip_group_check=True)
            pe.matmul(cnt, order[:, 2, :], chosen[:, :, :, :].rearrange("p i w e -> p (i w e)"), start=False,
                      stop=True).then_inc(count_mm, 1)
            with pe.Fori(0, loops) as it:
                for q in range(body):
                    hidden(it * body + (q + 1), q + 1, it)
                    second(it * body + q, q)
            for s in range(loops * body, steps):
                if s + 1 < steps:
                    hidden(s + 1, s + 1, 0)
                second(s, s)
            pe.wait_ge(gate_ready, 1)
            for n in range(4):
                if n >= 2:
                    pe.wait_ge(gate_T_ready, n - 1)
                for i in range(4):
                    ins = pe.transpose(ps_r[0:NE, n % 2, P * i:P * i + P], gate[:, :, 4 * n + i], ident[:, :])
                ins.then_inc(gate_turned, 1)
            for n in range(4):
                pe.wait_ge(gate_T_ready, n + 1)
                for i in range(4):
                    m = 4 * n + i
                    ins = pe.matmul(ps_h[:, n, P * i:P * i + P], gate_T[:, P * m:P * m + P], b2[:, :], start=True, stop=True)
                ins.then_inc(bias_mm, 1)


def hyena_moe_layer(nc, a, out):
    with ExitStack() as ctx:
        x1 = ctx.enter_context(nc.sbuf_tensor("x1", [P, NT, D], F32))
        ident = ctx.enter_context(nc.sbuf_tensor("ident", [P, P], F32))
        scr = {n: nc.dram_tensor("scr_" + n, (NH, PARTS, HD, L), BF16).ap() for n in "qk"}
        scr["o"] = nc.dram_tensor("scr_o", (NH, HD + 1, L), F32).ap()
        hyena(nc, a["attn"] | a["const"], x1, ident)
        z = ctx.enter_context(nc.sbuf_tensor("z", [P, NT, D], F32))
        with ExitStack() as att:
            vs = att.enter_context(nc.sbuf_tensor("vs", [P, NH, NT, HD + 1], F32))
            attention_operands(nc, a["ffn"], x1, z, vs, ident, scr)
            attention(nc, vs, ident, scr)
        h_T = ctx.enter_context(nc.sbuf_tensor("h_T2", [P, L], F32))
        attention_output(nc, a["ffn"], z, h_T, ident, scr)
        experts(nc, a["ffn"] | a["const"], x1, z, h_T, ident, out)


def kernel(**inputs):
    import numpy as _np
    import concourse.bacc as _bacc
    from concourse import mybir as _mybir
    from concourse.bass_utils import run_bass_kernel_spmd as _run

    nc = _bacc.Bacc("TRN2", target_bir_lowering=False, num_devices=1)
    arrays, a = {}, {"attn": {}, "ffn": {}, "const": {}}
    named = [(k, _np.ascontiguousarray(v)) for k, v in inputs.items()] + list(shape_constants().items())
    for name, v in named:
        arrays[f"in_{name}_dram"] = v
        ap = nc.dram_tensor(f"in_{name}_dram", v.shape, _mybir.dt.from_np(v.dtype), kind="ExternalInput").ap()
        group = next((g for g in ("attn", "ffn") if name.startswith(f"L0_{g}_")), "const")
        a[group][name.removeprefix(f"L0_{group}_")] = ap
    out = nc.dram_tensor("out_0_dram", (1, L, D), F32, kind="ExternalOutput").ap()
    a["attn"]["u"] = a["attn"]["u"].rearrange("o l d -> (o l) d")
    hyena_moe_layer(nc, a, out.rearrange("o l d -> (o l) d"))
    r = _run(nc, [arrays], core_ids=[0])
    return r.results[0]["out_0_dram"]
```

```python
from contextlib import ExitStack

import numpy as np

import concourse.bass as bass
from concourse import mybir

ALU = mybir.AluOpType
ACT = mybir.ActivationFunctionType
AX = mybir.AxisListType
F32 = mybir.dt.float32
BF16 = mybir.dt.bfloat16
F32R = mybir.dt.float32r

P = 128
L, D = 2048, 128
NT = L // P
ORDER, EMB, HID = 2, 33, 64
FREQ = 10.0
LN_EPS = 1e-5
BANK = 512
NB = 8

R = 64
N_FFT = R * R
H1 = R // 2
NJ = P // H1
assert N_FFT == 2 * L and NT * NJ == R

TWO_PI_HI = 6.28125
TWO_PI_LO = float(2 * np.pi - TWO_PI_HI)
ROUND = 1.5 * 2.0 ** 23

NH, HD = 16, 8
NE, FF = 8, 512
CAP = L // 4
FT = FF // P
KEEP = 0.8


def shape_constants():
    f32 = np.float32
    i, p = np.meshgrid(np.arange(NT), np.arange(P), indexing="ij")
    tok = R * (p % H1) + NJ * i + p // H1
    lin = np.linspace(0.0, 1.0, L, dtype=f32)
    bands = np.linspace(0.0, EMB - 1.0, EMB, dtype=f32)
    pe = np.sin((lin[:, None] * bands[None, :] * f32(FREQ)).astype(np.float64)).astype(f32)
    c = {"c_pe": pe[tok.reshape(-1)].T, "c_negt": -lin[tok].T}
    n1, n2, k2 = np.arange(H1), np.arange(R), np.arange(R)
    f1 = np.zeros((H1, R))
    f1[:, 0], f1[:, 1] = 1.0, (-1.0) ** n1
    g = np.zeros((R, H1))
    g[0], g[1] = 1.0, (-1.0) ** n1
    for m in range(1, H1):
        a = 2 * np.pi * n1 * m / R
        f1[:, 2 * m], f1[:, 2 * m + 1] = np.cos(a), -np.sin(a)
        g[2 * m], g[2 * m + 1] = 2 * np.cos(a), -2 * np.sin(a)
    c["c_f1"] = np.kron(np.eye(NJ), f1)
    c["c_g"] = np.kron(np.eye(2), g / (N_FFT * L))
    m_fwd = np.zeros((2, R, H1 + 1, 2, R))
    m_inv = np.zeros((2, R, H1 + 1, 2, R))
    for k1 in range(H1 + 1):
        th = 2 * np.pi * n2[:, None] * (k1 + R * k2[None, :]) / N_FFT
        if k1 == 0 or k1 == H1:
            m_fwd[k1 // H1, :, k1, 0], m_fwd[k1 // H1, :, k1, 1] = np.cos(th), -np.sin(th)
        else:
            m_fwd[0, :, k1, 0], m_fwd[1, :, k1, 0] = np.cos(th), np.sin(th)
            m_fwd[0, :, k1, 1], m_fwd[1, :, k1, 1] = -np.sin(th), np.cos(th)
        m_inv[0, :, k1, 0], m_inv[1, :, k1, 0] = np.cos(th).T, -np.sin(th).T
        m_inv[0, :, k1, 1], m_inv[1, :, k1, 1] = np.sin(th).T, np.cos(th).T
    c["c_fwd"] = m_fwd.reshape(P, -1)
    inv = m_inv.reshape(2, R, -1)
    c["c_inv"] = np.concatenate([inv[0], inv[1], -inv[0]])
    edge = np.zeros((4, 2, P))
    edge[0, 0, 0] = edge[2, 1, P - 1] = -1.0
    c["c_edge"] = edge.reshape(4, -1)
    c["c_ident"] = np.eye(P)
    r = np.arange(P)
    c["c_sums"] = r[:, None] == r[None, :] // 32 * 32 + HD
    q = np.arange(P)
    jq, nq = q // H1, q % H1
    c["c_before"] = np.stack([
        nq[:, None] < nq[None, :],
        nq[:, None] == nq[None, :],
        (nq[:, None] == nq[None, :]) & (jq[:, None] <= jq[None, :]),
    ], axis=1).reshape(P, -1)
    return {k: np.ascontiguousarray(v, dtype=f32) for k, v in c.items()}


def tiles_of(dram):
    v = dram.rearrange("(n i j) d -> n i j d", i=NT, j=NJ)
    return [v[:, :, j, :] for j in range(NJ)]


def chain(eng, s):
    count = [0]

    def link(ins):
        count[0] += 1
        ins.then_inc(s, 1)
        eng.wait_ge(s, count[0])
    return link


class Norm:

    def __init__(self, nc, sb, sem, name):
        self.stats = sb(name + "_stats", [P, NT, 6], F32)
        self.mv = sb(name + "_mv", [P, NT, 2], F32)
        self.rstd = sb(name + "_rstd", [P, NT], F32)
        self.shift = sb(name + "_shift", [P, NT], F32)
        self.var_ready = sem(name + "_var_ready")
        self.std_ready = sem(name + "_std_ready")
        self.scales_ready = sem(name + "_scales_ready")

    def vector_stats(self, dve, link, x):
        link(self.vector_stats_of(dve, x, range(NT)))
        self.vector_var(dve, link)

    def vector_stats_of(self, dve, x, tiles):
        for i in tiles:
            ins = dve.bn_stats(self.stats[:, i, :], x[:, i, :])
        return ins

    def vector_var(self, dve, link):
        for i in range(NT):
            ins = dve.bn_aggr(self.mv[:, i, :], self.stats[:, i, :])
        link(ins)
        dve.tensor_scalar(self.rstd[:, :], self.mv[:, :, 1], LN_EPS, None, ALU.add).then_inc(self.var_ready, 1)

    def scalar_sqrt(self, act):
        act.wait_ge(self.var_ready, 1)
        act.activation(self.rstd[:, :], self.rstd[:, :], ACT.Sqrt).then_inc(self.std_ready, 1)

    def vector_scales(self, dve, link):
        dve.wait_ge(self.std_ready, 1)
        link(dve.reciprocal(self.rstd[:, :], self.rstd[:, :]))
        dve.scalar_tensor_tensor(out=self.shift[:, :], in0=self.mv[:, :, 0], scalar=-1.0, in1=self.rstd[:, :],
                                 op0=ALU.mult, op1=ALU.mult).then_inc(self.scales_ready, 1)

    def scalar_apply(self, act, out, x, tiles):
        act.wait_ge(self.scales_ready, 1)
        for i in tiles:
            ins = act.activation(out[:, i, :], x[:, i, :], ACT.Identity, bias=self.shift[:, i:i + 1],
                                 scale=self.rstd[:, i:i + 1])
        return ins

    def vector_apply(self, dve, link, out, x, tiles=range(NT)):
        for i in tiles:
            ins = dve.tensor_scalar(out[:, i, :], x[:, i, :], self.mv[:, i, 0:1], self.rstd[:, i:i + 1],
                                    ALU.subtract, ALU.mult)
        return ins


def bcast_rows(vec, n):
    return bass.AP(vec.tensor, vec.offset, [[0, n]] + [list(x) for x in vec.ap])


class Units:

    def __init__(self):
        self.who, self.base = [], {}

    def stage(self, name, who):
        self.base[name] = len(self.who)
        self.who += who

    def number(self, name, n=0):
        return self.base[name] + n

    def taken(self, who, below):
        return sum(x in (who, "B") for x in self.who[:below])


def hyena(nc, a, x1, ident):
    u = Units()
    alt = lambda n: ("AD" * n)[:n]
    u.stage("small_T", "D")
    u.stage("arg", "DDDD")
    u.stage("w_in_T", "ADA")
    u.stage("bias_T", "D")
    u.stage("bias_b", "D")
    u.stage("xn_T", alt(4))
    u.stage("filt", "D" * 8)
    u.stage("proj", "D" * NT)
    for o in range(ORDER):
        u.stage(f"h{o}_first", alt(8))
        u.stage(f"h{o}_turn", alt(8))
        u.stage(f"h{o}_spec", "B" * 9)
        u.stage(f"v{o}_first", alt(8))
        u.stage(f"v{o}_turn", alt(8))
        u.stage(f"v{o}_spec", "D" * 9)
        u.stage(f"v{o}_back", alt(8))
        u.stage(f"v{o}_return", alt(8))
        u.stage(f"v{o}_time", "D" * 4)
    u.stage("v_T", alt(4))
    u.stage("out", "D" * 4)

    with ExitStack() as ctx:
        def sb(name, shape, dt=F32):
            return ctx.enter_context(nc.sbuf_tensor("hy_" + name, shape, dt))

        def sem(name):
            return ctx.enter_context(nc.semaphore("hy_" + name))

        ps = ctx.enter_context(nc.psum_tensor("hy_ps", [P, NB, BANK], F32))
        branches = sb("branches", [P, NT, 3 * D])
        filt = sb("filt", [P, NT, ORDER * D])
        buf_a = sb("buf_a", [P, (H1 + 1) * P])
        buf_b = sb("buf_b", [P, (H1 + 1) * P])
        buf_c = sb("buf_c", [P, (H1 + 1) * P])
        spec_re = sb("spec_re", [P, H1 + 1, P])
        spec_im = sb("spec_im", [P, H1 + 1, P])
        m_fwd = sb("m_fwd", [P, H1 + 1, P])
        m_inv = sb("m_inv", [P, H1 + 1, P])
        m_inv_i = sb("m_inv_i", [P, H1 + 1, P])
        f1 = sb("f1", [P, NJ * R])
        gt = sb("gt", [P, 2 * H1])
        wk = sb("wk", [P, 3, 3 * D])
        w_in = buf_c[:, 0:384].rearrange("p (b d) -> p b d", b=3)
        ws = buf_c[:, 384:384 + 9 * 128].rearrange("p (t b d) -> p t b d", t=3, b=3)
        cw = sb("cw", [P, 3, 3])
        b_in = sb("b_in", [P, 3])
        bc = sb("bc", [P, 3, 4])
        bias_row = sb("bias_row", [4, 3 * D])
        ones4 = sb("ones4", [4, P])
        edge = sb("edge", [4, 2 * P])
        bias_b = sb("bias_b", [P, 3 * D])
        w1 = sb("w1", [HID, EMB])
        w2 = sb("w2", [P, 2, HID])
        b1 = sb("b1", [HID, 1])
        w1_T = sb("w1_T", [EMB, HID])
        w2_T = sb("w2_T", [P, ORDER * D])
        w_out = sb("w_out", [P, D])
        w_out_T = sb("w_out_T", [P, D])
        b_out = sb("b_out", [P, D])
        negt = sb("negt", [P, NT])
        rate = sb("rate", [P, ORDER * D])
        f_bias = sb("f_bias", [P, ORDER * D])
        xn_T = sb("xn_T", [P, (R + 2) * H1])
        pe_T = spec_im[0:EMB, :, :].rearrange("p a b -> p (a b)")[:, 2048:4096]
        arg = buf_a[0:HID, 0:L]
        turns = buf_a[0:HID, L:2 * L]
        sin_T = buf_b[:, 0:L]
        decay = spec_re[:, 0:H1, :].rearrange("p a b -> p (a b)").rearrange("p (i c) -> p i c", i=NT)
        xn = spec_im[:, 0:NT, :]
        norm_x = Norm(nc, sb, sem, "norm_x")
        norm_y = Norm(nc, sb, sem, "norm_y")
        y = buf_b[:, 0:L].rearrange("p (i d) -> p i d", i=NT)

        x_loaded = sem("x_loaded")
        small_loaded = sem("small_loaded")
        tables_loaded = sem("tables_loaded")
        fwd_loaded = sem("fwd_loaded")
        inv_loaded = sem("inv_loaded")
        row_loaded = sem("row_loaded")
        pe_unit = sem("pe_unit")
        act_taken = sem("act_taken")
        dve_taken = sem("dve_taken")
        dve_chain = sem("dve_chain")
        pool_chain = sem("pool_chain")
        zeroed = sem("zeroed")
        taps_ready = sem("taps_ready")
        arg_ready = sem("arg_ready")
        rate_ready = sem("rate_ready")
        sin_ready = sem("sin_ready")
        decay_ready = sem("decay_ready")
        xn_ready = sem("xn_ready")
        filt_ready = sem("filt_ready")
        halo_ready = sem("halo_ready")
        x1_ready = sem("x1_ready")
        spec_copied = sem("spec_copied")

        def taken(eng, below):
            if n := u.taken("A", below):
                eng.wait_ge(act_taken, n)
            if n := u.taken("D", below):
                eng.wait_ge(dve_taken, n)

        def bank(n):
            return ps[:, n % NB, :]

        def a_view(t):
            return t[:, 0:R * R].rearrange("p (c n) -> p n c", n=R)

        block = ctx.enter_context(nc.Block())

        small = [
            (w1[:, :], a["w1"]), (w2[:, :, :], a["w2"].rearrange("(b p) h -> p b h", p=P)),
            (w_out[:, :], a["w_out"]), (b1[:, :], a["b1"].rearrange("(p o) -> p o", o=1)),
            (ident[:, :], a["c_ident"]), (pe_T, a["c_pe"]),
            (rate[:, :], bcast_rows(a["filt_decay"].rearrange("o d -> (o d)"), P)),
            (negt[:, :], a["c_negt"]),
        ]
        tables = [
            (w_in, a["w_in"].rearrange("(b p) d -> p b d", p=P)),
            (cw[:, :, :], a["conv_w"].rearrange("(b p) k -> p b k", p=P)),
            (b_in[:, :], a["b_in"].rearrange("(b p) -> p b", p=P)),
            (bc[:, :, 3], a["conv_b"].rearrange("(b p) -> p b", p=P)),
            (edge[:, :], a["c_edge"]), (f1[:, :], a["c_f1"]), (gt[:, :], a["c_g"]),
            (f_bias[:, :], bcast_rows(a["filt_bias"].rearrange("o d -> (o d)"), P)),
            (b_out[:, :], bcast_rows(a["b_out"], P)),
        ]

        @block.sync
        def _(sp):
            for j, v in enumerate(tiles_of(a["u"])):
                sp.dma_start(x1[H1 * j:H1 * j + H1, :, :], v).then_inc(x_loaded, 16)
            sp.wait_ge(tables_loaded, 16 * len(tables))
            sp.dma_start(m_fwd[:, :, :].rearrange("p a b -> p (a b)"), a["c_fwd"]).then_inc(fwd_loaded, 16)
            sp.dma_start(m_inv[:, :, :].rearrange("p a b -> p (a b)"), a["c_inv"][0:P, :]).then_inc(inv_loaded, 16)
            sp.dma_start(m_inv_i[:, :, :].rearrange("p a b -> p (a b)"), a["c_inv"][R:R + P, :]).then_inc(inv_loaded, 16)
            for o in range(ORDER):
                taken(sp, u.number(f"h{o}_spec", 9))
                sp.dma_start(spec_re[R:P, :, :], spec_re[0:R, :, :]).then_inc(spec_copied, 16)
                sp.dma_start(spec_im[0:R, :, :], spec_im[R:P, :, :]).then_inc(spec_copied, 16)

        def mine(name, n, who):
            return u.who[u.number(name, n)] == who

        def take_weights(who, take):
            for k in range(3):
                if mine("w_in_T", k, who):
                    take("w_in_T", k, wk[:, k, :], bank(u.number("w_in_T", k))[:, 0:3 * D])

        def take_xn(who, take):
            for n in range(4):
                if mine("xn_T", n, who):
                    take("xn_T", n, xn_T[:, H1 + BANK * n:H1 + BANK * n + BANK], bank(u.number("xn_T", n)))

        def take_fft(name, who, take):
            for n in range(8):
                if mine(name + "_first", n, who):
                    src = bank(u.number(name + "_first", n)).rearrange("p (n c) -> p n c", c=R)
                    take(name + "_first", n, a_view(buf_a)[:, 8 * n:8 * n + 8, :], src)
            for n in range(8):
                if mine(name + "_turn", n, who):
                    take(name + "_turn", n, buf_b[:, BANK * n:BANK * n + BANK], bank(u.number(name + "_turn", n)))

        def spec_blocks(n):
            return slice(H1, H1 + 1) if n == 0 else slice(4 * n - 4, 4 * n)

        def take_spec(o, who, take):
            half, spec = (slice(0, R), spec_re) if who == "A" else (slice(R, P), spec_im)
            for n in range(9):
                dst = spec[half, spec_blocks(n), :].rearrange("p a b -> p (a b)")
                take(f"h{o}_spec", n, dst, bank(u.number(f"h{o}_spec", n))[half, 0:dst.shape[1]])

        def take_back(o, who, take):
            v = buf_b[:, 0:R * R].rearrange("p (n c) -> p c n", c=R)
            for n in range(8):
                if mine(f"v{o}_back", n, who):
                    src = bank(u.number(f"v{o}_back", n)).rearrange("p (c n) -> p c n", n=R)
                    take(f"v{o}_back", n, v[:, 8 * n:8 * n + 8, :], src)
            for n in range(8):
                if mine(f"v{o}_return", n, who):
                    take(f"v{o}_return", n, buf_a[:, BANK * n:BANK * n + BANK], bank(u.number(f"v{o}_return", n)))

        def take_v(who, take):
            for n in range(4):
                if mine("v_T", n, who):
                    take("v_T", n, buf_a[:, BANK * n:BANK * n + BANK], bank(u.number("v_T", n)))

        @block.gpsimd
        def _(pool):
            link = chain(pool, pool_chain)
            link(pool.memset(sin_T, 0.0))
            link(pool.memset(w2_T[:, :], 0.0))
            pool.dma_start(w2_T[HID:HID + 1, :], a["b2"].rearrange("(o d) -> o d", o=1)).then_inc(row_loaded, 16)
            link(pool.memset(sin_T[HID:HID + 1, :], 1.0))
            link(pool.memset(xn_T[:, 0:1], 0.0))
            link(pool.memset(xn_T[:, (R + 2) * H1 - 1:(R + 2) * H1], 0.0))
            pool.memset(ones4[:, :], 1.0).then_inc(zeroed, 1)
            pool.wait_ge(tables_loaded, 16 * len(tables))
            for k in range(3):
                for b in range(3):
                    pool.tensor_scalar(ws[:, k, b, :], w_in[:, b, :], cw[:, b, k:k + 1], None, ALU.mult)
            for k in range(3):
                ins = pool.tensor_tensor(bc[:, :, k], b_in[:, :], cw[:, :, k], ALU.mult)
            ins.then_inc(taps_ready, 1)
            for n in range(8):
                pool.wait_ge(dve_taken, u.taken("D", u.number("filt", n) + 1))
                for i in (2 * n, 2 * n + 1):
                    ins = pool.tensor_tensor(filt[:, i, :], filt[:, i, :], f_bias[:, :], ALU.add)
                ins.then_inc(filt_ready, 1)

        @block.scalar
        def _(act):
            for dst, src in small:
                act.dma_start(dst, src).then_inc(small_loaded, 16)
            for dst, src in tables:
                act.dma_start(dst, src, allow_slow_non_contiguous=True).then_inc(tables_loaded, 16)
            norm_x.scalar_sqrt(act)
            act.wait_ge(small_loaded, 16 * len(small))
            act.activation(rate[:, :], rate[:, :], ACT.Exp).then_inc(rate_ready, 1)
            act.wait_ge(rate_ready, 1)
            for i in range(NT):
                ins = act.activation(decay[:, i, :], rate[:, :], ACT.Exp, scale=negt[:, i:i + 1])
            ins.then_inc(decay_ready, 1)

            def take(name, n, dst, src):
                act.wait_ge(pe_unit, u.number(name, n) + 1)
                act.activation(dst, src, ACT.Copy).then_inc(act_taken, 1)

            take_weights("A", take)
            act.wait_ge(arg_ready, 1)
            act.wait_ge(zeroed, 1)
            act.activation(sin_T[0:HID, :], arg, ACT.Sin).then_inc(sin_ready, 1)
            take_xn("A", take)
            for o in range(ORDER):
                take_fft(f"h{o}", "A", take)
                take_spec(o, "A", take)
                take_fft(f"v{o}", "A", take)
                take_back(o, "A", take)
            take_v("A", take)
            norm_y.scalar_sqrt(act)

        @block.vector
        def _(dve):
            link = chain(dve, dve_chain)

            def take(name, n, dst, src):
                dve.wait_ge(pe_unit, u.number(name, n) + 1)
                dve.tensor_copy(dst, src).then_inc(dve_taken, 1)

            dve.wait_ge(x_loaded, 16 * NJ)
            norm_x.vector_stats(dve, link, x1)
            dve.wait_ge(pe_unit, u.number("small_T") + 1)
            dve.wait_ge(row_loaded, 16)
            b = bank(u.number("small_T"))
            dve.tensor_copy(w1_T[:, :], b[0:EMB, 0:HID])
            dve.tensor_copy(w2_T[0:HID, :], b[0:HID, D:D + 2 * D])
            dve.tensor_copy(w_out_T[:, :], b[:, 3 * D:4 * D]).then_inc(dve_taken, 1)
            for n in range(4):
                dve.wait_ge(pe_unit, u.number("arg", n) + 1)
                ins = dve.tensor_scalar(arg[:, BANK * n:BANK * n + BANK], bank(u.number("arg", n))[0:HID, :],
                                        b1[:, 0:1], FREQ, ALU.add, ALU.mult).then_inc(dve_taken, 1)
            dve.wait_ge(dve_taken, u.taken("D", u.number("arg", 3) + 1))
            link(dve.tensor_scalar(turns, arg, 1.0 / (2 * np.pi), ROUND, ALU.mult, ALU.add))
            link(dve.tensor_scalar(turns, turns, ROUND, None, ALU.subtract))
            link(dve.scalar_tensor_tensor(out=arg, in0=turns, scalar=-TWO_PI_HI, in1=arg, op0=ALU.mult, op1=ALU.add))
            link(dve.scalar_tensor_tensor(out=arg, in0=turns, scalar=-TWO_PI_LO, in1=arg, op0=ALU.mult, op1=ALU.add))
            dve.tensor_scalar(arg, arg, 3.1415925, -3.1415925, ALU.min, ALU.max).then_inc(arg_ready, 1)
            norm_x.vector_scales(dve, link)
            norm_x.vector_apply(dve, link, xn, x1).then_inc(xn_ready, 1)
            take_weights("D", take)
            take("bias_T", 0, bias_row[:, :], bank(u.number("bias_T"))[0:4, 0:3 * D])
            take("bias_b", 0, bias_b[:, :], bank(u.number("bias_b"))[:, 0:3 * D])
            take_xn("D", take)
            dve.wait_ge(dve_taken, u.taken("D", u.number("xn_T", 4)))
            dve.wait_ge(act_taken, u.taken("A", u.number("xn_T", 4)))
            dve.wait_ge(zeroed, 1)
            dve.tensor_copy(xn_T[:, 1:H1], xn_T[:, R * H1:R * H1 + H1 - 1])
            dve.tensor_copy(xn_T[:, (R + 1) * H1:(R + 2) * H1 - 1], xn_T[:, H1 + 1:2 * H1]).then_inc(halo_ready, 1)
            dve.wait_ge(decay_ready, 1)
            for n in range(8):
                dve.wait_ge(pe_unit, u.number("filt", n) + 1)
                dve.tensor_tensor(filt[:, 2 * n:2 * n + 2, :].rearrange("p i c -> p (i c)"),
                                  bank(u.number("filt", n)),
                                  decay[:, 2 * n:2 * n + 2, :].rearrange("p i c -> p (i c)"),
                                  ALU.mult).then_inc(dve_taken, 1)
            for i in range(NT):
                n = u.number("proj", i)
                dve.wait_ge(pe_unit, n + 1)
                dve.tensor_tensor(branches[:, i, :], bank(n)[:, 0:3 * D], bias_b[:, :], ALU.add)\
                   .then_inc(dve_taken, 1)
            for o in range(ORDER):
                take_fft(f"h{o}", "D", take)
                take_spec(o, "D", take)
                take_fft(f"v{o}", "D", take)
                dve.wait_ge(act_taken, u.taken("A", u.number(f"v{o}_turn")))
                dve.wait_ge(spec_copied, 32 * (o + 1))
                for n in range(9):
                    m = u.number(f"v{o}_spec", n)
                    s = spec_blocks(n)
                    w = (s.stop - s.start) * P
                    dve.wait_ge(pe_unit, m + 1)
                    for spec, dst in ((spec_re, buf_a), (spec_im, buf_c)):
                        ins = dve.tensor_tensor(dst[:, s.start * P:s.stop * P], bank(m)[:, 0:w],
                                                spec[:, s, :].rearrange("p a b -> p (a b)"), ALU.mult)
                    ins.then_inc(dve_taken, 1)
                take_back(o, "D", take)
                for n in range(4):
                    m = u.number(f"v{o}_time", n)
                    dve.wait_ge(pe_unit, m + 1)
                    dve.tensor_tensor(branches[:, 4 * n:4 * n + 4, 2 * D:3 * D],
                                      bank(m).rearrange("p (i d) -> p i d", d=D),
                                      branches[:, 4 * n:4 * n + 4, o * D:o * D + D], ALU.mult)\
                       .then_inc(dve_taken, 1)
            take_v("D", take)
            for n in range(4):
                m = u.number("out", n)
                dve.wait_ge(pe_unit, m + 1)
                dve.tensor_tensor(y[:, 4 * n:4 * n + 4, :], bank(m).rearrange("p (i d) -> p i d", d=D),
                                  b_out[:, :].rearrange("p (o d) -> p o d", o=1).to_broadcast([P, 4, D]),
                                  ALU.add).then_inc(dve_taken, 1)
            dve.wait_ge(dve_taken, u.taken("D", len(u.who)))
            norm_y.vector_stats(dve, link, y)
            norm_y.vector_scales(dve, link)
            link(norm_y.vector_apply(dve, link, y, y))
            dve.tensor_tensor(x1[:, :, :], x1[:, :, :], y, ALU.add).then_inc(x1_ready, 1)

        @block.tensor
        def _(pe):
            def start_unit(name, n=0):
                m = u.number(name, n)
                if m >= NB:
                    taken(pe, m - NB + 1)
                return bank(m)

            def shifted(i, k):
                return xn_T[:, (NJ * i + k) * H1:(NJ * i + k) * H1 + P]

            pe.wait_ge(small_loaded, 16 * len(small))
            b = start_unit("small_T")
            pe.transpose(b[0:EMB, 0:HID], w1[:, :], ident[0:HID, 0:HID])
            for k in range(2):
                pe.transpose(b[0:HID, D + D * k:2 * D + D * k], w2[:, k, :], ident[:, :])
            pe.transpose(b[:, 3 * D:4 * D], w_out[:, :], ident[:, :]).then_inc(pe_unit, 1)
            taken(pe, u.number("arg"))
            for n in range(4):
                b = start_unit("arg", n)
                pe.matmul(b[0:HID, :], w1_T[:, :], pe_T[:, BANK * n:BANK * n + BANK], start=True, stop=True)\
                  .then_inc(pe_unit, 1)
            pe.wait_ge(taps_ready, 1)
            for k in range(3):
                b = start_unit("w_in_T", k)
                for c in range(3):
                    ins = pe.transpose(b[:, D * c:D * c + D], ws[:, k, c, :], ident[:, :])
                ins.then_inc(pe_unit, 1)
            b = start_unit("bias_T")
            for c in range(3):
                ins = pe.transpose(b[0:4, D * c:D * c + D], bc[:, c, :], ident[:, :])
            ins.then_inc(pe_unit, 1)
            taken(pe, u.number("bias_b"))
            pe.wait_ge(zeroed, 1)
            b = start_unit("bias_b")
            pe.matmul(b[:, 0:3 * D], ones4[:, :], bias_row[:, :], start=True, stop=True).then_inc(pe_unit, 1)
            pe.wait_ge(xn_ready, 1)
            for n in range(4):
                b = start_unit("xn_T", n)
                for i in range(4):
                    ins = pe.transpose(b[:, P * i:P * i + P], xn[:, 4 * n + i, :], ident[:, :])
                ins.then_inc(pe_unit, 1)
            pe.wait_ge(sin_ready, 1)
            for n in range(8):
                b = start_unit("filt", n)
                for i in (2 * n, 2 * n + 1):
                    ins = pe.matmul(b[:, 256 * (i % 2):256 * (i % 2) + 256], sin_T[:, P * i:P * i + P], w2_T[:, :],
                                    start=True, stop=True)
                ins.then_inc(pe_unit, 1)

            def fft(name, x):
                for n in range(8):
                    b = start_unit(name + "_first", n)
                    for i in (2 * n, 2 * n + 1):
                        ins = pe.matmul(b[:, 256 * (i % 2):256 * (i % 2) + 256], x[:, i, :], f1[:, :],
                                        start=True, stop=True)
                    ins.then_inc(pe_unit, 1)
                taken(pe, u.number(name + "_turn"))
                for n in range(8):
                    b = start_unit(name + "_turn", n)
                    for i in range(4):
                        m = 4 * n + i
                        ins = pe.transpose(b[:, P * i:P * i + P], buf_a[:, P * m:P * m + P], ident[:, :])
                    ins.then_inc(pe_unit, 1)
                taken(pe, u.number(name + "_spec"))

            def spec_unit(b, n):
                s = spec_blocks(n)
                for q, k1 in enumerate(range(s.start, s.stop)):
                    m = k1 % H1
                    ins = pe.matmul(b[:, P * q:P * q + P], m_fwd[:, k1, :], buf_b[:, P * m:P * m + P], start=True, stop=True)
                ins.then_inc(pe_unit, 1)

            pe.wait_ge(halo_ready, 1)
            for i in range(NT):
                b = start_unit("proj", i)
                edges = {0: 0, NT - 1: 1}
                for k in range(3):
                    lhs = shifted(i, k)
                    ins = pe.matmul(b[:, 0:3 * D], lhs, wk[:, k, :], start=(k == 0),
                                    stop=(k == 2 and i not in edges))
                if i in edges:
                    e = edges[i]
                    ins = pe.matmul(b[:, 0:3 * D], edge[:, e * P:e * P + P], bias_row[:, :], start=False, stop=True)
                ins.then_inc(pe_unit, 1)
            taken(pe, u.number("h0_first"))
            pe.wait_ge(filt_ready, 8)
            for o in range(ORDER):
                fft(f"h{o}", filt[:, :, o * D:o * D + D])
                pe.wait_ge(fwd_loaded, 16)
                for n in range(9):
                    spec_unit(start_unit(f"h{o}_spec", n), n)
                fft(f"v{o}", branches[:, :, 2 * D:3 * D])
                for n in range(9):
                    spec_unit(start_unit(f"v{o}_spec", n), n)
                pe.wait_ge(inv_loaded, 32)
                for n in range(8):
                    taken(pe, u.number(f"v{o}_spec", n + 2))
                    b = start_unit(f"v{o}_back", n)
                    for q in range(4):
                        k1 = 4 * n + q
                        parts = [(0, 0, R), (H1, R, R)] if k1 == 0 else [(k1, 0, P)]
                        for k, at, w in parts:
                            dst = b[:, P * q + at:P * q + at + w]
                            pe.matmul(dst, buf_a[:, P * k:P * k + P], m_inv[:, k, 0:w], start=True, stop=False)
                            ins = pe.matmul(dst, buf_c[:, P * k:P * k + P], m_inv_i[:, k, 0:w], start=False, stop=True)
                    ins.then_inc(pe_unit, 1)
                taken(pe, u.number(f"v{o}_return"))
                for n in range(8):
                    b = start_unit(f"v{o}_return", n)
                    for i in range(4):
                        m = 4 * n + i
                        ins = pe.transpose(b[:, P * i:P * i + P], buf_b[:, P * m:P * m + P], ident[:, :])
                    ins.then_inc(pe_unit, 1)
                taken(pe, u.number(f"v{o}_time"))
                for n in range(4):
                    b = start_unit(f"v{o}_time", n)
                    for jh in range(2):
                        rhs = buf_a[:, 8 * n * P:8 * (n + 1) * P].rearrange("p (i q c) -> p q i c", q=2, c=P)[:, jh]
                        ins = pe.matmul(b[R * jh:R * jh + R, :], gt[:, :], rhs, start=True, stop=True)
                    ins.then_inc(pe_unit, 1)
                taken(pe, u.number(f"v{o}_time", 4))
            for n in range(4):
                b = start_unit("v_T", n)
                for i in range(4):
                    ins = pe.transpose(b[:, P * i:P * i + P], branches[:, 4 * n + i, 2 * D:3 * D], ident[:, :])
                ins.then_inc(pe_unit, 1)
            taken(pe, u.number("out"))
            for n in range(4):
                b = start_unit("out", n)
                for i in range(4):
                    m = 4 * n + i
                    ins = pe.matmul(b[:, P * i:P * i + P], buf_a[:, P * m:P * m + P], w_out_T[:, :], start=True, stop=True)
                ins.then_inc(pe_unit, 1)




def attention_operands(nc, a, x1, z, vs, ident, scr):
    u = Units()
    u.stage("h_T", "DDDD")
    u.stage("q", "DDDD")
    u.stage("k", "DDDD")
    u.stage("v", "DDDD")
    with ExitStack() as ctx:
        def sb(name, shape, dt=F32):
            return ctx.enter_context(nc.sbuf_tensor("op_" + name, shape, dt))

        def sem(name):
            return ctx.enter_context(nc.semaphore("op_" + name))

        ps = ctx.enter_context(nc.psum_tensor("op_ps", [P, NB, BANK], F32))
        zn = sb("zn", [P, NT, D])
        h_T = sb("h_T", [P, L])
        w = {n: sb("w" + n, [P, D]) for n in "qkv"}
        bias = {n: sb("bias_" + n, [P, 1]) for n in "qk"}
        bias_v = sb("bias_v", [P, D])
        g1 = sb("g1", [P, 1])
        be1 = sb("be1", [P, 1])
        full = {n: sb("full_" + n, [P, L]) for n in "qk"}
        parts = {n: [sb(f"part_{n}{i}", [P, L], BF16) for i in range(3)] for n in "qk"}
        norm_1 = Norm(nc, sb, sem, "norm_1")
        norm_2 = Norm(nc, sb, sem, "norm_2")

        loaded = sem("loaded")
        chain_d = sem("chain")
        pe_unit = sem("pe_unit")
        taken = sem("taken")
        zn_ready = sem("zn_ready")
        full_ready = sem("full_ready")
        part1_ready = sem("part1_ready")
        part2_ready = sem("part2_ready")
        rest1_ready = sem("rest1_ready")
        part3_ready = sem("part3_ready")
        stored = sem("parts_stored")
        col = lambda v: v.rearrange("(p o) -> p o", o=1)
        loads = [(w[n][:, :], a["w" + n]) for n in "qkv"]
        loads += [(bias[n][:, :], col(a["b" + n])) for n in "qk"]
        loads += [(bias_v[:, :], bcast_rows(a["bv"], P)), (g1[:, :], col(a["ln1_g"])), (be1[:, :], col(a["ln1_b"]))]

        def bank(name, n):
            return ps[:, u.number(name, n) % NB, :]

        block = ctx.enter_context(nc.Block())

        @block.sync
        def _(sp):
            for dst, src in loads:
                sp.dma_start(dst, src).then_inc(loaded, 16)
            for m, n in enumerate("qk"):
                for i, s in enumerate((part1_ready, part2_ready, part3_ready)):
                    sp.wait_ge(s, m + 1)
                    sp.dma_start(scr[n][:, i, :, :], parts[n][i][:, :]).then_inc(stored, 16)
            sp.wait_ge(stored, 96)

        @block.scalar
        def _(act):
            norm_1.scalar_sqrt(act)
            norm_2.scalar_sqrt(act)
            for m, n in enumerate("qk"):
                act.wait_ge(full_ready, m + 1)
                act.activation(parts[n][0][:, :], full[n][:, :], ACT.Copy).then_inc(part1_ready, 1)
                act.wait_ge(rest1_ready, m + 1)
                act.activation(parts[n][1][:, :], full[n][:, :], ACT.Copy).then_inc(part2_ready, 1)

        @block.vector
        def _(dve):
            link = chain(dve, chain_d)
            norm_1.vector_stats(dve, link, x1)
            norm_1.vector_scales(dve, link)
            link(norm_1.vector_apply(dve, link, z, x1))
            norm_2.vector_stats(dve, link, z)
            norm_2.vector_scales(dve, link)
            norm_2.vector_apply(dve, link, zn, z).then_inc(zn_ready, 1)
            dve.wait_ge(loaded, 16 * len(loads))
            for n in range(4):
                dve.wait_ge(pe_unit, u.number("h_T", n) + 1)
                dve.tensor_scalar(h_T[:, BANK * n:BANK * n + BANK], bank("h_T", n), g1[:, 0:1], be1[:, 0:1],
                                  ALU.mult, ALU.add).then_inc(taken, 1)
            for m, name in enumerate("qk"):
                scale = HD ** -0.5 if name == "q" else 1.0
                for n in range(4):
                    dve.wait_ge(pe_unit, u.number(name, n) + 1)
                    dve.tensor_scalar(full[name][:, BANK * n:BANK * n + BANK], bank(name, n),
                                      bias[name][:, 0:1], scale, ALU.add, ALU.mult).then_inc(taken, 1)
                dve.wait_ge(taken, u.number(name, 4))
                dve.nop().then_inc(full_ready, 1)
            for m, name in enumerate("qk"):
                dve.wait_ge(part1_ready, m + 1)
                dve.tensor_tensor(full[name][:, :], full[name][:, :], parts[name][0][:, :], ALU.subtract)\
                   .then_inc(rest1_ready, 1)
            for n in range(4):
                dve.wait_ge(pe_unit, u.number("v", n) + 1)
                dve.tensor_tensor(
                    vs[:, :, 4 * n:4 * n + 4, 0:HD].rearrange("p h i e -> p i h e"),
                    bank("v", n).rearrange("p (i h e) -> p i h e", i=4, h=NH),
                    bias_v[:, :].rearrange("p (o h e) -> p o h e", o=1, h=NH).to_broadcast([P, 4, NH, HD]),
                    ALU.add).then_inc(taken, 1)
            for m, name in enumerate("qk"):
                dve.wait_ge(part2_ready, m + 1)
                dve.tensor_tensor(parts[name][2][:, :], full[name][:, :], parts[name][1][:, :], ALU.subtract)\
                   .then_inc(part3_ready, 1)

        @block.tensor
        def _(pe):
            pe.wait_ge(zn_ready, 1)
            for n in range(4):
                for i in range(4):
                    ins = pe.transpose(bank("h_T", n)[:, P * i:P * i + P], zn[:, 4 * n + i, :], ident[:, :])
                ins.then_inc(pe_unit, 1)
            pe.wait_ge(loaded, 16 * len(loads))
            for name in "qk":
                for n in range(4):
                    pe.wait_ge(taken, n + 1 if name == "q" else 4)
                    pe.matmul(bank(name, n), w[name][:, :], h_T[:, BANK * n:BANK * n + BANK], start=True, stop=True)\
                      .then_inc(pe_unit, 1)
            for n in range(4):
                pe.wait_ge(taken, u.number("v", n) - NB + 1)
                for i in range(4):
                    m = 4 * n + i
                    ins = pe.matmul(bank("v", n)[:, P * i:P * i + P], h_T[:, P * m:P * m + P], w["v"][:, :],
                                    start=True, stop=True)
                ins.then_inc(pe_unit, 1)


PARTS = 3
ROWS = PARTS * PARTS * HD
MROW = 96
assert ROWS <= MROW
G = 3
AHEAD = NT + 4
CHUNK = L // BANK
N_STEP = NH * NT


class HeadOutputs:

    def __init__(self, nc, ctx):
        def sb(name, shape):
            return ctx.enter_context(nc.sbuf_tensor("ho_" + name, shape, F32))
        self.rows = (NH - 1) * HD
        self.o_T = sb("o_T", [self.rows, L])
        self.sums = sb("sums", [self.rows, L])
        self.last_o = sb("last_o", [P, BANK])
        self.last_scale = sb("last_scale", [P, BANK])
        self.sum_rows = sb("sum_rows", [P, P])
        self.wo = sb("wo", [self.rows, D])
        self.wo_last = sb("wo_last", [P, D])
        self.bo = sb("bo", [P, D])


def attention(nc, a, z, vs, ho, ew, ident, scr):
    loops = (NH - 1) // G
    assert loops * G == NH - 1
    body = G * NT
    with ExitStack() as ctx:
        def sb(name, shape, dt=F32):
            return ctx.enter_context(nc.sbuf_tensor("at_" + name, shape, dt))

        def sem(name):
            return ctx.enter_context(nc.semaphore("at_" + name))

        ps_s = ctx.enter_context(nc.psum_tensor("ps_s", [P, 2, 2 * BANK], F32))
        ps_m = ctx.enter_context(nc.psum_tensor("ps_m", [P, 3, BANK], F32))
        ps_o = ctx.enter_context(nc.psum_tensor("ps_o", [P, BANK], F32))
        ps_t = ps_s[:, 1, 0:P // 2].bitcast(BF16)
        q_op = [sb(f"q_op{b}", [P, L], BF16) for b in range(G)]
        k_op = [sb(f"k_op{b}", [P, L], BF16) for b in range(G)]
        v_op = [sb(f"v_op{b}", [P, NT, 32]) for b in range(G)]
        prob = [sb(f"prob{b}", [P, L]) for b in range(3)]
        o_out = [sb(f"o_out{b}", [P, BANK]) for b in range(G)]
        ident_b = sb("ident_b", [P, P], BF16)
        maxes = sb("maxes", [P, NT, CHUNK])
        neg = sb("neg", [P, NT])
        neg_parts = sb("neg_parts", [P, P], BF16)
        neg_T = sb("neg_T", [PARTS * NT, P], BF16)

        zeroed = sem("zeroed")
        pool_chain = sem("pool_chain")
        op_loaded = [sem(f"op_loaded{b}") for b in range(G)]
        score_ready = sem("score_ready")
        exp_done = sem("exp_done")
        max_mm = sem("max_mm")
        max_done = sem("max_done")
        pv_done = sem("pv_done")
        neg_chain = sem("neg_chain")
        neg_ready = sem("neg_ready")
        neg_turned = sem("neg_turned")
        neg_T_ready = sem("neg_T_ready")
        row_loaded = sem("neg_row_loaded")
        v_ready = sem("v_ready")
        o_taken = sem("o_taken")
        o_stored = [sem(f"o_stored{b}") for b in range(G)]

        ho_loaded = sem("ho_loaded")
        heads_loaded = sem("heads_loaded")
        sums_chain = sem("sums_chain")
        w_loaded = [sem(f"w_loaded{b}") for b in range(2)]
        w_hi_ready = sem("w_hi_ready")
        ho_loads = [(ho.wo[:, :], a["wo"][0:ho.rows, :]), (ho.bo[:, :], bcast_rows(a["bo"], P)),
                    (ho.sum_rows[:, :], a["c_sums"])]
        ho_loads += [(ho.wo_last[32 * j:32 * j + HD, :], a["wo"][ho.rows:D, :]) for j in range(CHUNK)]

        N_LOAD = 4
        TURN = 12
        FREE_SCORE, FREE_MAX, FREE_PROB = 2, 3, 3

        block = ctx.enter_context(nc.Block())

        @block.sync
        def _(sp):
            def load(h, b):
                q = scr["q"][bass.ds(h, 1)].rearrange("o a e t -> (o a e) t")
                sp.dma_start(q_op[b][0:ROWS, :],
                             q.rearrange("(o r) t -> o r t", o=1).to_broadcast([PARTS, PARTS * HD, L]))\
                  .then_inc(op_loaded[b], 16)
                for c in range(PARTS):
                    k = scr["k"][bass.ds(h, 1), c:c + 1].rearrange("o a e t -> (o a e) t")
                    sp.dma_start(k_op[b][PARTS * HD * c:PARTS * HD * (c + 1), :],
                                 k.rearrange("(o e) t -> o e t", o=1).to_broadcast([PARTS, HD, L]))\
                      .then_inc(op_loaded[b], 16)

            def neg_rows(h, b):
                sp.wait_ge(neg_T_ready, h + 1)
                sp.dma_start(q_op[b][MROW:MROW + PARTS, :], neg_T[:, :]).then_inc(row_loaded, 16)

            def store(h, b):
                sp.wait_ge(o_taken, h + 2)
                for j in range(CHUNK):
                    sp.dma_start(scr["o"][bass.ds(h, 1), :, BANK * j:BANK * j + BANK].rearrange("o e q -> (o e) q"),
                                 o_out[b][32 * j:32 * j + HD + 1, :]).then_inc(o_stored[b], 16)

            def head(h, r, load_next):
                neg_rows(h + 1, (r + 1) % G)
                sp.wait_ge(score_ready, (h + 1) * (2 * NT))
                if load_next:
                    load(h + G, r)
                elif h == NH - G:
                    sp.nop().then_inc(op_loaded[NH % G], 16 * N_LOAD)
                store(h, r)

            sp.wait_ge(zeroed, 1)
            for b in range(G):
                load(b, b)
            for e in range(2):
                ew.load(sp, a, e, e, w_loaded[e])
            for dst, src in ho_loads:
                sp.dma_start(dst, src).then_inc(ho_loaded, 16)
            neg_rows(0, 0)
            with sp.Fori(0, loops - 1) as it:
                for r in range(G):
                    head(it * G + r, r, True)
            for h in range((loops - 1) * G, NH - 1):
                head(h, h % G, h + G < NH)
            for b in range(G):
                sp.wait_ge(o_stored[b], 16 * CHUNK * (1 + len(range(b, NH - 1, G))))
            sp.dma_start(ho.sums[:, :], scr["o"][0:NH - 1, HD:HD + 1, :].to_broadcast([NH - 1, HD, L]))\
              .then_inc(heads_loaded, 16)
            sp.dma_start(ho.o_T[:, :], scr["o"][0:NH - 1, 0:HD, :]).then_inc(heads_loaded, 16)

        @block.gpsimd
        def _(pool):
            link = chain(pool, pool_chain)
            for b in range(G):
                link(pool.memset(q_op[b][:, :].bitcast(F32), 0.0))
                link(pool.memset(k_op[b][:, :].bitcast(F32), 0.0))
                link(pool.memset(k_op[b][MROW:MROW + PARTS, :], 1.0))
                link(pool.memset(v_op[b][:, :, :], 0.0))
                link(pool.memset(v_op[b][:, :, HD:2 * HD], 1.0))
            link(pool.memset(neg_parts[:, :], 0.0))
            link(pool.tensor_copy(ident_b[:, :], ident[:, :]))
            pool.nop().then_inc(zeroed, 1)
            for h in range(G):
                pool.tensor_copy(v_op[h][:, :, 0:HD], vs[:, h, :, :]).then_inc(v_ready, 1)
            for e in range(2):
                pool.wait_ge(w_hi_ready, e + 1)
                ew.pool_lo(pool, e)
            with pool.Fori(0, loops - 1) as it:
                for r in range(G):
                    pool.wait_ge(pv_done, it * body + (FREE_PROB + (r + 1) * NT))
                    pool.tensor_copy(v_op[r][:, :, 0:HD], vs[:, bass.ds(it * G + (G + r), 1), :, :]
                                     .rearrange("p o i e -> p (o i) e")).then_inc(v_ready, 1)
            pool.wait_ge(pv_done, FREE_PROB + (NH - G) * NT)
            pool.tensor_copy(v_op[(NH - 1) % G][:, :, 0:HD], vs[:, NH - 1, :, :]).then_inc(v_ready, 1)

        @block.scalar
        def _(act):
            def exps(s, n):
                for half in range(2):
                    act.wait_ge(score_ready, s * 2 + (half + 1))
                    if half == 0:
                        act.wait_ge(pv_done, s + 1)
                    act.activation(prob[n % 3][:, 2 * BANK * half:2 * BANK * (half + 1)], ps_s[:, half, :], ACT.Exp)\
                       .then_inc(exp_done, 1)

            def take_neg(h, first=False):
                act.wait_ge(neg_turned, h + 1)
                if not first:
                    act.wait_ge(row_loaded, h * 16)
                act.activation(neg_T[:, :], ps_t[0:PARTS * NT, 0:P], ACT.Copy).then_inc(neg_T_ready, 1)

            def take_out(h, it, r):
                act.wait_ge(pv_done, h * NT + (FREE_PROB + NT))
                act.wait_ge(o_stored[r], it * (16 * CHUNK) + 16 * CHUNK)
                act.activation(o_out[r][:, :], ps_o[:, :], ACT.Copy).then_inc(o_taken, 1)

            for e in range(2):
                act.wait_ge(w_loaded[e], 32)
                ew.scalar_hi(act, e).then_inc(w_hi_ready, 1)
            act.nop().then_inc(exp_done, FREE_SCORE)
            act.nop().then_inc(o_taken, 1)
            for b in range(G):
                act.nop().then_inc(o_stored[b], 16 * CHUNK)
            take_neg(0, first=True)
            exps(0, 0)
            with act.Fori(0, loops) as it:
                for q in range(body):
                    if q % NT == TURN:
                        take_neg(it * G + (q // NT + 1))
                    exps(it * body + (q + 1), q + 1)
                    if q % NT == NT - 1:
                        take_out(it * G + q // NT, it, q // NT)
            for s in range(loops * body + 1, N_STEP):
                exps(s, s)
            act.wait_ge(pv_done, FREE_PROB + NH * NT)
            act.activation(ho.last_o[:, :], ps_o[:, :], ACT.Copy)

        @block.vector
        def _(dve):
            def maxima(t, n):
                for c in range(CHUNK):
                    dve.wait_ge(max_mm, t * CHUNK + (c + 1))
                    dve.tensor_reduce(maxes[:, n % NT, c:c + 1], ps_m[:, (n * CHUNK + c) % 3, :], AX.X, ALU.max)\
                       .then_inc(max_done, 1)

            def negate(h, first=False):
                dve.wait_ge(max_done, h * (NT * CHUNK) + (FREE_MAX + NT * CHUNK))
                dve.tensor_reduce(neg[:, :], maxes[:, :, :], AX.X, ALU.max, negate=True).then_inc(neg_chain, 1)
                dve.wait_ge(neg_chain, h * 4 + 1)
                if not first:
                    dve.wait_ge(neg_turned, h)
                part = [neg_parts[:, NT * i:NT * (i + 1)] for i in range(PARTS)]
                dve.tensor_copy(part[0], neg[:, :]).then_inc(neg_chain, 1)
                dve.wait_ge(neg_chain, h * 4 + 2)
                dve.tensor_tensor(neg[:, :], neg[:, :], part[0], ALU.subtract).then_inc(neg_chain, 1)
                dve.wait_ge(neg_chain, h * 4 + 3)
                dve.tensor_copy(part[1], neg[:, :]).then_inc(neg_chain, 1)
                dve.wait_ge(neg_chain, h * 4 + 4)
                dve.tensor_tensor(part[2], neg[:, :], part[1], ALU.subtract)\
                   .then_inc(neg_ready, 1)

            dve.nop().then_inc(max_done, FREE_MAX)
            dve.wait_ge(zeroed, 1)
            for t in range(AHEAD + 1):
                maxima(t, t)
                if t == NT - 1:
                    negate(0, first=True)
            with dve.Fori(0, loops) as it:
                for q in range(body):
                    n = q + 1 + AHEAD
                    maxima(it * body + n, n)
                    if n % NT == NT - 1:
                        negate(it * G + n // NT)
            dve.wait_ge(ho_loaded, 16 * len(ho_loads))
            dve.tensor_tensor(z[:, :, :], z[:, :, :],
                              ho.bo[:, :].rearrange("p (o d) -> p o d", o=1).to_broadcast([P, NT, D]), ALU.add)
            dve.wait_ge(heads_loaded, 32)
            dve.reciprocal(ho.sums[:, :], ho.sums[:, :]).then_inc(sums_chain, 1)
            dve.wait_ge(sums_chain, 1)
            dve.tensor_tensor(ho.o_T[:, :], ho.o_T[:, :], ho.sums[:, :], ALU.mult)

        @block.tensor
        def _(pe):
            def scores(s, n, halves=range(2)):
                b, k = n // NT % G, n % NT
                for half in halves:
                    pe.wait_ge(exp_done, s * 2 + (half + 1))
                    for c in range(2):
                        at = BANK * (2 * half + c)
                        ins = pe.matmul(ps_s[:, half, BANK * c:BANK * (c + 1)], k_op[b][:, P * k:P * (k + 1)],
                                        q_op[b][:, at:at + BANK], start=True, stop=True)
                    ins.then_inc(score_ready, 1)

            def max_scores(t, n, it, banks=range(CHUNK)):
                b, i = n // NT % G, n % NT
                if i == 0 and banks[0] == 0:
                    pe.wait_ge(op_loaded[b], (it + n // NT // G + 1) * (16 * N_LOAD))
                for c in banks:
                    pe.wait_ge(max_done, t * CHUNK + (c + 1))
                    pe.matmul(ps_m[:, (n * CHUNK + c) % 3, :], q_op[b][0:MROW, P * i:P * (i + 1)],
                              k_op[b][0:MROW, BANK * c:BANK * (c + 1)], start=True, stop=True).then_inc(max_mm, 1)

            def turn_neg(h, s):
                pe.wait_ge(neg_ready, h + 1)
                pe.wait_ge(exp_done, s * 2 + 2)
                pe.transpose(ps_t[:, 0:P], neg_parts[:, :], ident_b[:, :]).then_inc(neg_turned, 1)

            def outputs(s, n, h):
                b, k = n // NT % G, n % NT
                if k == 0:
                    pe.wait_ge(v_ready, h + 1)
                    pe.wait_ge(o_taken, h + 1)
                pe.wait_ge(exp_done, s * 2 + (FREE_SCORE + 2))
                for j in range(CHUNK):
                    ins = pe.matmul(ps_o[32 * j:32 * j + 32, :], v_op[b][:, k, :],
                                    prob[n % 3][:, BANK * j:BANK * (j + 1)], start=(k == 0), stop=(k == NT - 1))
                ins.then_inc(pv_done, 1)

            pe.nop().then_inc(pv_done, FREE_PROB)
            for t in range(AHEAD + 1):
                max_scores(t, t, 0)
                if t == NT + 1:
                    turn_neg(0, 0)
            pe.wait_ge(row_loaded, 16)
            scores(0, 0)
            with pe.Fori(0, loops) as it:
                for q in range(body):
                    n = q + 1
                    if n % NT == 0:
                        pe.wait_ge(row_loaded, it * (16 * G) + (n // NT + 1) * 16)
                    m = n + AHEAD
                    turned = q % NT == TURN
                    if turned:
                        turn_neg(it * G + (q // NT + 1), it * body + n)
                    max_scores(it * body + m, m, it, [0])
                    scores(it * body + n, n, [0])
                    max_scores(it * body + m, m, it, [1])
                    if turned:
                        pe.wait_ge(neg_T_ready, it * G + (q // NT + 2))
                    scores(it * body + n, n, [1])
                    max_scores(it * body + m, m, it, [2, 3])
                    outputs(it * body + q, q, it * G + q // NT)
            for s in range(loops * body + 1, N_STEP):
                scores(s, s)
                outputs(s - 1, s - 1, NH - 1)
            outputs(N_STEP - 1, N_STEP - 1, NH - 1)


class Router:

    def __init__(self, nc, ctx):
        def sb(name, shape):
            return ctx.enter_context(nc.sbuf_tensor("ro_" + name, shape, F32))
        self.logits = sb("logits", [P, NT, NE])
        self.b1_T = sb("b1_T", [P, NE * FT])
        self.b2 = sb("b2_rows", [NE, D])
        self.order = sb("order", [P, 3, P])


def attention_output(nc, a, z, ho, h_T, h_part, ro, ident):
    with ExitStack() as ctx:
        def sb(name, shape, dt=F32):
            return ctx.enter_context(nc.sbuf_tensor("ao_" + name, shape, dt))

        def sem(name):
            return ctx.enter_context(nc.semaphore("ao_" + name))

        ps = ctx.enter_context(nc.psum_tensor("ao_ps", [P, NB, BANK], F32))
        g2 = sb("g2", [P, 1])
        be2 = sb("be2", [P, 1])
        zn = sb("zn2", [P, NT, D])
        wr = sb("wr", [P, 32])
        logits_T = sb("logits_T", [P, BANK])
        b1_rows = sb("b1_rows", [NE * FT, P])
        norm_3 = Norm(nc, sb, sem, "norm_3")
        sums_mm = sem("sums_mm")
        loaded = sem("loaded")
        chain_d = sem("chain")
        last_ready = sem("last_ready")
        pe_unit = sem("pe_unit")
        zn_ready = sem("zn2_ready")
        zn_ready_act = sem("zn2_ready_act")
        full_ready = sem("full_ready")
        hi_ready = sem("hi_ready")
        logits_mm = sem("logits_mm")
        b1_turned = sem("b1_turned")
        wr_zeroed = sem("wr_zeroed")
        logits_T_ready = sem("logits_T_ready")
        logits_turned = sem("logits_turned")
        col = lambda v: v.rearrange("(p o) -> p o", o=1)
        loads = [(g2[:, :], col(a["ln2_g"])), (be2[:, :], col(a["ln2_b"])), (wr[:, 0:NE], a["wr"]),
                 (b1_rows[:, :], a["b1"].rearrange("e (f p) -> (e f) p", p=P)), (ro.b2[:, :], a["b2"]),
                 (ro.order[:, :, :].rearrange("p k q -> p (k q)"), a["c_before"])]
        block = ctx.enter_context(nc.Block())

        def bank_cols(n):
            return slice(BANK * n, BANK * n + BANK)

        @block.sync
        def _(sp):
            for dst, src in loads:
                sp.dma_start(dst, src).then_inc(loaded, 16)

        @block.gpsimd
        def _(pool):
            pool.memset(wr[:, NE:32], 0.0).then_inc(wr_zeroed, 1)
            for n in (1, 3):
                pool.wait_ge(hi_ready, n + 1)
                pool.tensor_tensor(h_part["lo"][:, bank_cols(n)], h_T[:, bank_cols(n)],
                                   h_part["hi"][:, bank_cols(n)].bitcast(F32), ALU.subtract)

        @block.scalar
        def _(act):
            norm_3.scalar_sqrt(act)
            norm_3.scalar_apply(act, zn, z, range(NT // 2, NT)).then_inc(zn_ready_act, 1)
            act.wait_ge(b1_turned, 1)
            act.activation(ro.b1_T[:, :], ps[:, 1, 0:NE * FT], ACT.Copy)
            for n in range(4):
                act.wait_ge(full_ready, n + 1)
                act.activation(h_part["hi"][:, bank_cols(n)], h_T[:, bank_cols(n)], ACT.Copy).then_inc(hi_ready, 1)

        @block.vector
        def _(dve):
            link = chain(dve, chain_d)
            dve.wait_ge(sums_mm, 1)
            link(dve.reciprocal(ho.last_scale[:, :], ps[:, 4, :]))
            dve.tensor_tensor(ho.last_o[:, :], ho.last_o[:, :], ho.last_scale[:, :], ALU.mult).then_inc(last_ready, 1)
            for n in range(4):
                dve.wait_ge(pe_unit, n + 1)
                link(dve.tensor_tensor(z[:, 4 * n:4 * n + 4, :], ps[:, n, :].rearrange("p (i d) -> p i d", d=D),
                                       z[:, 4 * n:4 * n + 4, :], ALU.add))
                ins = norm_3.vector_stats_of(dve, z, range(4 * n, 4 * n + 4))
            link(ins)
            norm_3.vector_var(dve, link)
            norm_3.vector_scales(dve, link)
            norm_3.vector_apply(dve, link, zn, z, range(0, NT // 2)).then_inc(zn_ready, 1)
            dve.wait_ge(loaded, 16 * len(loads))
            for n in range(4):
                dve.wait_ge(pe_unit, 4 + n + 1)
                dve.tensor_scalar(h_T[:, bank_cols(n)], ps[:, 4 + n, :], g2[:, 0:1], be2[:, 0:1],
                                  ALU.mult, ALU.add).then_inc(full_ready, 1)
            dve.wait_ge(logits_mm, 1)
            dve.tensor_copy(logits_T[:, :], ps[:, 2, :]).then_inc(logits_T_ready, 1)
            for n in (0, 2):
                dve.wait_ge(hi_ready, n + 1)
                dve.tensor_tensor(h_part["lo"][:, bank_cols(n)], h_T[:, bank_cols(n)],
                                  h_part["hi"][:, bank_cols(n)].bitcast(F32), ALU.subtract)
            dve.wait_ge(logits_turned, 1)
            dve.tensor_copy(ro.logits[:, :, :].rearrange("p (n i) e -> p n i e", i=4),
                            ps[:, 3, :].rearrange("p (i n x) -> p n i x", n=CHUNK, x=32)[:, :, :, 0:NE])

        @block.tensor
        def _(pe):
            pe.matmul(ps[:, 4, :], ho.sum_rows[:, :], ho.last_o[:, :], start=True, stop=True).then_inc(sums_mm, 1)
            dst = lambda m: ps[:, m // 4, P * (m % 4):P * (m % 4) + P]
            for m in range(NT):
                pe.matmul(dst(m), ho.o_T[:, P * m:P * m + P], ho.wo[:, :], start=(m % 4 == 0), stop=False,
                          skip_group_check=(m % 4 != 0))
            pe.wait_ge(last_ready, 1)
            for n in range(4):
                rows = slice(32 * n, 32 * n + HD)
                for i in range(4):
                    ins = pe.matmul(dst(4 * n + i), ho.last_o[rows, P * i:P * i + P], ho.wo_last[rows, :],
                                    start=False, stop=True, skip_group_check=(i != 0))
                ins.then_inc(pe_unit, 1)
            pe.wait_ge(zn_ready, 1)
            for n in range(4):
                if n == 2:
                    pe.wait_ge(zn_ready_act, 1)
                for i in range(4):
                    ins = pe.transpose(ps[:, 4 + n, P * i:P * i + P], zn[:, 4 * n + i, :], ident[:, :])
                ins.then_inc(pe_unit, 1)
            pe.wait_ge(loaded, 16 * len(loads))
            pe.transpose(ps[:, 1, 0:NE * FT], b1_rows[:, :], ident[0:NE * FT, 0:NE * FT]).then_inc(b1_turned, 1)
            pe.wait_ge(wr_zeroed, 1)
            for n in range(CHUNK):
                pe.wait_ge(full_ready, n + 1)
                ins = pe.matmul(ps[32 * n:32 * n + 32, 2, :], wr[:, :], h_T[:, bank_cols(n)], start=True, stop=True)
            ins.then_inc(logits_mm, 1)
            pe.wait_ge(logits_T_ready, 1)
            for i in range(4):
                ins = pe.transpose(ps[:, 3, P * i:P * i + P], logits_T[:, P * i:P * i + P], ident[:, :])
            ins.then_inc(logits_turned, 1)


W_PARTS = ("hi", "lo")


class ExpertWeights:

    def __init__(self, nc, ctx):
        def sb(name, shape, dt=F32):
            return ctx.enter_context(nc.sbuf_tensor("ew_" + name, shape, dt))
        self.w1 = [sb(f"w1_{b}", [P, FF]) for b in range(2)]
        self.w2 = [sb(f"w2_{b}", [P, FT, D]) for b in range(2)]
        self.w1_part = [{p: sb(f"w1_{p}{b}", [P, FF], F32R) for p in W_PARTS} for b in range(2)]
        self.w2_part = [{p: sb(f"w2_{p}{b}", [P, FT, D], F32R) for p in W_PARTS} for b in range(2)]

    def load(self, sp, a, e, b, loaded):
        w1 = a["w1"][bass.ds(e, 1)].rearrange("o p f -> (o p) f")
        w2 = a["w2"].rearrange("e (f p) d -> e p f d", p=P)[bass.ds(e, 1)].rearrange("o p f d -> (o p) f d")
        sp.dma_start(self.w1[b][:, :], w1).then_inc(loaded, 16)
        sp.dma_start(self.w2[b][:, :, :], w2).then_inc(loaded, 16)

    def scalar_hi(self, act, b):
        act.activation(self.w1_part[b]["hi"][:, :], self.w1[b][:, :], ACT.Copy)
        return act.activation(self.w2_part[b]["hi"][:, :, :], self.w2[b][:, :, :], ACT.Copy)

    def pool_lo(self, pool, b):
        pool.tensor_tensor(self.w1_part[b]["lo"][:, :], self.w1[b][:, :], self.w1_part[b]["hi"][:, :].bitcast(F32),
                           ALU.subtract)
        return pool.tensor_tensor(self.w2_part[b]["lo"][:, :, :], self.w2[b][:, :, :],
                                  self.w2_part[b]["hi"][:, :, :].bitcast(F32), ALU.subtract)


def experts(nc, a, x1, z, h_part, ew, ro, ident, scr, out):
    steps = NE * CHUNK
    body = 2 * CHUNK
    loops = (NE - 2) // 2
    with ExitStack() as ctx:
        def sb(name, shape, dt=F32):
            return ctx.enter_context(nc.sbuf_tensor("ex_" + name, shape, dt))

        def sem(name):
            return ctx.enter_context(nc.semaphore("ex_" + name))

        ps_h = ctx.enter_context(nc.psum_tensor("ps_h", [P, FT, BANK], F32))
        ps_y = ctx.enter_context(nc.psum_tensor("ps_y", [P, 2, BANK], F32))
        ps_r = ctx.enter_context(nc.psum_tensor("ps_r", [P, 2, BANK], F32))
        hid = [[sb(f"hid{b}_{f}", [P, BANK]) for f in range(FT)] for b in range(2)]
        hid_hi = [[sb(f"hid_hi{b}_{f}", [P, BANK], F32R) for f in range(FT)] for b in range(2)]
        hid_lo = [[sb(f"hid_lo{b}_{f}", [P, BANK], F32R) for f in range(FT)] for b in range(2)]
        y_0 = sb("y_0", [P, L])
        y_gated = [sb(f"y_gated{b}", [P, BANK]) for b in range(2)]
        y_T = sb("y_T", [P, L])
        gate_b = [sb(f"gate_b{b}", [P, L]) for b in range(2)]
        b1_e = [sb(f"b1_e{b}", [P, FT]) for b in range(2)]
        ones = sb("ones_p", [P, P])
        rank = sb("rank", [P, NE])
        masked = sb("masked", [P, NT, NE])
        probs = sb("probs", [P, NT, NE])
        cand = sb("cand", [P, NT, NE])
        peak = sb("peak", [P, NT])
        chosen = sb("chosen", [P, NT, 2, NE])
        upto = [sb(f"upto{b}", [P, NT, 2 * NE]) for b in range(2)]
        before = sb("before_tile", [P, NT, 2 * NE])
        kept = sb("kept", [P, NT, 2, NE])
        part = sb("part", [P, NT, 2, NE])
        share = sb("share", [P, NT, 2])
        total = sb("total", [P, NT])
        gate = sb("gate", [P, NE, NT])
        gate_T = sb("gate_T", [NE, L])
        norm_4 = Norm(nc, sb, sem, "norm_4")

        w_loaded = [sem(f"w_loaded{b}") for b in range(2)]
        w_hi_ready = sem("w_hi_ready")
        w_split = sem("w_split")
        consts = sem("consts")
        pool_chain = sem("pool_chain")
        chain_d = sem("chain")
        b1_e_ready = sem("b1_e_ready")
        shifted_ready = sem("shifted_ready")
        exp_ready = sem("router_exp_ready")
        counts_ready = sem("counts_ready")
        count_mm = sem("count_mm")
        gate_ready = sem("gate_ready")
        gate_turned = sem("gate_turned")
        gate_T_ready = sem("gate_T_ready")
        gate_stored = sem("gate_stored")
        gate_loaded = [sem(f"gate_loaded{b}") for b in range(2)]
        bias_mm = sem("bias_mm")
        bias_added = sem("bias_added")
        hid_mm = sem("hid_mm")
        hi_ready = sem("hi_ready")
        lo_ready = sem("lo_ready")
        y_mm = sem("y_mm")
        y_taken = sem("y_taken")
        y_added = sem("y_added")
        y_turned = sem("y_turned")
        z_ready_act = sem("z_ready_act")
        out_ready = sem("out_ready")
        out_stored = sem("out_stored")

        block = ctx.enter_context(nc.Block())

        @block.sync
        def _(sp):
            for e in (2, 3):
                ew.load(sp, a, e, e % 2, w_loaded[e % 2])

            def load_gates(e, b):
                sp.dma_start(gate_b[b][:, :], scr["gate"][bass.ds(e, 1), :].to_broadcast([P, L]))\
                  .then_inc(gate_loaded[b], 16)

            sp.wait_ge(gate_T_ready, CHUNK)
            sp.dma_start(scr["gate"][:, :], gate_T[:, :]).then_inc(gate_stored, 16)
            sp.wait_ge(gate_stored, 16)
            load_gates(0, 0)
            load_gates(1, 1)

            def after(it, b):
                sp.wait_ge(y_taken, it * body + (b + 1) * CHUNK)
                sp.wait_ge(y_added, it * body + (b + 1) * CHUNK)
                load_gates(it * 2 + (2 + b), b)

            with sp.Fori(0, loops - 1) as it:
                for b in range(2):
                    after(it, b)
                    sp.wait_ge(w_split, it * 2 + (b + 1))
                    ew.load(sp, a, it * 2 + (4 + b), b, w_loaded[b])
            for b in range(2):
                after(loops - 1, b)
            for half in range(2):
                sp.wait_ge(out_ready, half + 1)
                t = slice(NT // 2 * half, NT // 2 * (half + 1))
                for j, v in enumerate(tiles_of(out)):
                    sp.dma_start(v[:, t, :], x1[H1 * j:H1 * j + H1, t, :]).then_inc(out_stored, 16)
            sp.wait_ge(out_stored, 32 * NJ)

        def split(eng, n, f):
            return eng.tensor_tensor(hid_lo[n % 2][f][:, :], hid[n % 2][f][:, :],
                                     hid_hi[n % 2][f][:, :].bitcast(F32), ALU.subtract)

        @block.gpsimd
        def _(pool):
            link = chain(pool, pool_chain)
            link(pool.memset(ones[:, :], 1.0))
            for e in range(NE):
                link(pool.memset(rank[:, e:e + 1], float(NE - e)))
            pool.nop().then_inc(consts, 1)
            for s in range(CHUNK):
                for f in range(FT):
                    pool.wait_ge(hi_ready, s * FT + f + 1)
                    split(pool, s, f).then_inc(lo_ready, 1)
            with pool.Fori(0, loops) as it:
                for b in range(2):
                    pool.wait_ge(w_hi_ready, it * 2 + (b + 1))
                    ew.pool_lo(pool, b).then_inc(w_split, 1)

        @block.scalar
        def _(act):
            act.wait_ge(shifted_ready, 1)
            act.activation(probs[:, :, :], cand[:, :, :], ACT.Exp).then_inc(exp_ready, 1)

            def bias_of(e, b):
                act.activation(b1_e[b][:, :], ro.b1_T[:, bass.ds(e * FT, FT)], ACT.Copy).then_inc(b1_e_ready, 1)
                act.wait_ge(b1_e_ready, e + 1)

            def hidden(s, n, e):
                b = n // CHUNK % 2
                if n % CHUNK == 0:
                    bias_of(e, b)
                for f in range(FT):
                    act.wait_ge(hid_mm, s * FT + (f + 1))
                    if f == 0 and not (isinstance(s, int) and s < 2):
                        act.wait_ge(y_mm, s - 1)
                    act.activation(hid[n % 2][f][:, :], ps_h[:, f, :], ACT.Relu, bias=b1_e[b][:, f:f + 1])
                    act.activation(hid_hi[n % 2][f][:, :], ps_h[:, f, :], ACT.Relu, bias=b1_e[b][:, f:f + 1])\
                       .then_inc(hi_ready, 1)

            def keep_y_0(s):
                act.wait_ge(y_mm, s + 1)
                act.activation(y_0[:, BANK * s:BANK * s + BANK], ps_y[:, s % 2, :], ACT.Copy).then_inc(y_taken, 1)

            hidden(0, 0, 0)
            for s in range(1, CHUNK + 1):
                hidden(s, s, s // CHUNK)
                keep_y_0(s - 1)
            with act.Fori(0, loops) as it:
                for q in range(body):
                    n = q + CHUNK + 1
                    if n % CHUNK == 1:
                        act.wait_ge(y_mm, it * body + (n - 1))
                        act.wait_ge(w_loaded[(n // CHUNK + 1) % 2], it * 32 + 32)
                        ew.scalar_hi(act, (n // CHUNK + 1) % 2).then_inc(w_hi_ready, 1)
                    hidden(it * body + n, n, it * 2 + n // CHUNK)
            for s in range(loops * body + CHUNK + 1, steps):
                hidden(s, s, s // CHUNK)
            norm_4.scalar_sqrt(act)
            norm_4.scalar_apply(act, z, z, range(NT // 2, NT)).then_inc(z_ready_act, 1)

        @block.vector
        def _(dve):
            link = chain(dve, chain_d)
            wide = lambda v: v.rearrange("p (i o) -> p i o", o=1).to_broadcast([P, NT, NE])
            rank_b = rank[:, :].rearrange("p (o e) -> p o e", o=1).to_broadcast([P, NT, NE])

            def choose(values, w):
                link(dve.tensor_reduce(peak[:, :], values[:, :, :], AX.X, ALU.max))
                link(dve.tensor_tensor(cand[:, :, :], values[:, :, :], wide(peak[:, :]), ALU.is_ge))
                link(dve.tensor_tensor(cand[:, :, :], cand[:, :, :], rank_b, ALU.mult))
                link(dve.tensor_reduce(peak[:, :], cand[:, :, :], AX.X, ALU.max))
                link(dve.tensor_tensor(chosen[:, :, w, :], rank_b, wide(peak[:, :]), ALU.is_equal))

            link(dve.tensor_reduce(peak[:, :], ro.logits[:, :, :], AX.X, ALU.max))
            dve.tensor_tensor(cand[:, :, :], ro.logits[:, :, :], wide(peak[:, :]), ALU.subtract).then_inc(shifted_ready, 1)
            dve.wait_ge(exp_ready, 1)
            link(dve.tensor_reduce(total[:, :], probs[:, :, :], AX.X, ALU.add))
            link(dve.reciprocal(total[:, :], total[:, :]))
            link(dve.tensor_tensor(probs[:, :, :], probs[:, :, :], wide(total[:, :]), ALU.mult))
            dve.wait_ge(consts, 1)
            choose(probs, 0)
            link(dve.scalar_tensor_tensor(out=masked[:, :, :], in0=chosen[:, :, 0, :], scalar=-3.0e38,
                                          in1=ro.logits[:, :, :], op0=ALU.mult, op1=ALU.add))
            choose(masked, 1)
            now = chosen[:, :, :, :].rearrange("p i w e -> p i (w e)")
            for k in range(NT.bit_length() - 1):
                to = upto[k % 2]
                dist = 1 << k
                dve.tensor_copy(to[:, 0:dist, :], now[:, 0:dist, :])
                link(dve.tensor_tensor(to[:, dist:NT, :], now[:, dist:NT, :], now[:, 0:NT - dist, :], ALU.add))
                now = to[:, :, :]
            dve.tensor_tensor(before[:, :, :], now, chosen[:, :, :, :].rearrange("p i w e -> p i (w e)"),
                              ALU.subtract).then_inc(counts_ready, 1)
            dve.wait_ge(count_mm, 1)
            flat = lambda t: t[:, :, :, :].rearrange("p i w e -> p (i w e)")
            link(dve.scalar_tensor_tensor(out=flat(kept), in0=ps_r[:, 0, 0:2 * NT * NE], scalar=float(CAP),
                                          in1=flat(chosen), op0=ALU.is_le, op1=ALU.mult))
            for w in range(2):
                ins = dve.tensor_tensor(part[:, :, w, :], kept[:, :, w, :], probs[:, :, :], ALU.mult)
            link(ins)
            link(dve.tensor_reduce(share[:, :, :].rearrange("p i w -> p (i w)"),
                                   part[:, :, :, :].rearrange("p i w e -> p (i w) e"), AX.X, ALU.add))
            link(dve.tensor_tensor(total[:, :], share[:, :, 0], share[:, :, 1], ALU.add))
            link(dve.tensor_scalar(total[:, :], total[:, :], float(np.finfo(np.float32).eps), None, ALU.max))
            link(dve.reciprocal(total[:, :], total[:, :]))
            link(dve.tensor_scalar(total[:, :], total[:, :], KEEP, None, ALU.mult))
            link(dve.tensor_tensor(part[:, :, 0, :], part[:, :, 0, :], part[:, :, 1, :], ALU.add))
            dve.tensor_tensor(gate[:, :, :].rearrange("p e i -> p i e"), part[:, :, 0, :], wide(total[:, :]),
                              ALU.mult).then_inc(gate_ready, 1)
            for n in range(CHUNK):
                dve.wait_ge(gate_turned, n + 1)
                dve.tensor_copy(gate_T[:, BANK * n:BANK * n + BANK], ps_r[0:NE, n % 2, :]).then_inc(gate_T_ready, 1)

            def lows(s, n, tiles):
                for f in tiles:
                    dve.wait_ge(hi_ready, s * FT + (f + 1))
                    if f == 0:
                        dve.wait_ge(y_mm, s - 1)
                    split(dve, n, f).then_inc(lo_ready, 1)

            def add_bias(n):
                dve.wait_ge(bias_mm, n + 1)
                return dve.tensor_tensor(z[:, 4 * n:4 * n + 4, :], ps_r[:, n % 2, :].rearrange("p (i d) -> p i d", d=D),
                                         z[:, 4 * n:4 * n + 4, :], ALU.add).then_inc(bias_added, 1)

            def gated(s, n):
                b, c = n // CHUNK % 2, n % CHUNK
                if c == 0:
                    k = n // CHUNK
                    dve.wait_ge(gate_loaded[b], (s - c) * 2 + (16 if b == 0 else 8))
                dve.wait_ge(y_mm, s + 1)
                dve.tensor_tensor(y_gated[n % 2][:, :], ps_y[:, n % 2, :], gate_b[b][:, BANK * c:BANK * c + BANK],
                                  ALU.mult).then_inc(y_taken, 1)

            def summed(s, n):
                c = slice(BANK * (n % CHUNK), BANK * (n % CHUNK) + BANK)
                dve.wait_ge(y_taken, s + 1)
                dve.wait_ge(y_added, s - (CHUNK - 1))
                return dve.tensor_tensor(y_T[:, c], y_T[:, c], y_gated[n % 2][:, :], ALU.add).then_inc(y_added, 1)

            for n in range(2):
                add_bias(n)
            lows(CHUNK, CHUNK, range(FT))
            dve.wait_ge(gate_loaded[0], 16)
            for c in range(CHUNK):
                dve.wait_ge(y_taken, c + 1)
                at = slice(BANK * c, BANK * c + BANK)
                dve.tensor_tensor(y_T[:, at], y_0[:, at], gate_b[0][:, at], ALU.mult).then_inc(y_added, 1)
            with dve.Fori(0, loops) as it:
                for q in range(body):
                    n = q + CHUNK
                    s = it * body + n
                    gated(s, n)
                    lows(s + 1, n + 1, [0])
                    summed(s, n)
                    lows(s + 1, n + 1, range(1, FT))
            for n in range(2, CHUNK):
                add_bias(n)
            last = steps - 1
            for s in range(steps - CHUNK, last):
                gated(s, s)
                lows(s + 1, s + 1, [0])
                summed(s, s)
                lows(s + 1, s + 1, range(1, FT))

            def from_turned(n):
                dve.wait_ge(y_turned, n + 1)
                dve.wait_ge(bias_added, CHUNK)
                return dve.tensor_tensor(z[:, 4 * n:4 * n + 4, :], ps_h[:, n, :].rearrange("p (i d) -> p i d", d=D),
                                         z[:, 4 * n:4 * n + 4, :], ALU.add)
            from_turned(0)
            link(from_turned(1))
            norm_4.vector_stats_of(dve, z, range(0, NT // 2))
            gated(last, last)
            summed(last, last)
            from_turned(2)
            link(from_turned(3))
            link(norm_4.vector_stats_of(dve, z, range(NT // 2, NT)))
            norm_4.vector_var(dve, link)
            norm_4.vector_scales(dve, link)
            link(norm_4.vector_apply(dve, link, z, z, range(0, NT // 2)))
            for half in range(2):
                if half:
                    dve.wait_ge(z_ready_act, 1)
                t = slice(NT // 2 * half, NT // 2 * (half + 1))
                dve.tensor_tensor(x1[:, t, :], x1[:, t, :], z[:, t, :], ALU.add).then_inc(out_ready, 1)

        @block.tensor
        def _(pe):
            def products(dst, terms):
                for i, (lhs, rhs) in enumerate(terms):
                    ins = pe.matmul(dst, lhs, rhs, start=(i == 0), stop=(i == len(terms) - 1))
                return ins

            def hidden(s, n):
                b, c = n // CHUNK % 2, n % CHUNK
                for f in range(FT):
                    if not (isinstance(s, int) and s == 0):
                        pe.wait_ge(hi_ready, (s - 1) * FT + (f + 1))
                    w = {p: ew.w1_part[b][p][:, P * f:P * f + P] for p in W_PARTS}
                    h = {p: h_part[p][:, BANK * c:BANK * c + BANK] for p in W_PARTS}
                    products(ps_h[:, f, :], [(w["hi"], h["hi"]), (w["hi"], h["lo"]), (w["lo"], h["hi"])])\
                        .then_inc(hid_mm, 1)

            def second(s, n):
                b = n // CHUNK % 2
                dst = ps_y[:, n % 2, :]
                w = ew.w2_part[b]
                pe.wait_ge(hi_ready, s * FT + FT)
                if not (isinstance(s, int) and s < 2):
                    pe.wait_ge(y_taken, s - 1)
                for f in range(FT):
                    for p in W_PARTS:
                        pe.matmul(dst, w[p][:, f, :], hid_hi[n % 2][f][:, :], start=(f == 0 and p == "hi"), stop=False)
                for f in range(FT):
                    pe.wait_ge(lo_ready, s * FT + (f + 1))
                    ins = pe.matmul(dst, w["hi"][:, f, :], hid_lo[n % 2][f][:, :], start=False, stop=(f == FT - 1))
                ins.then_inc(y_mm, 1)

            def turn_gates(n):
                if n >= 2:
                    pe.wait_ge(gate_T_ready, n - 1)
                for i in range(4):
                    ins = pe.transpose(ps_r[0:NE, n % 2, P * i:P * i + P], gate[:, :, 4 * n + i], ident[:, :])
                ins.then_inc(gate_turned, 1)

            def biases(n):
                if n >= 2:
                    pe.wait_ge(bias_added, n - 1)
                pe.wait_ge(gate_T_ready, CHUNK)
                for i in range(4):
                    m = 4 * n + i
                    ins = pe.matmul(ps_r[:, n % 2, P * i:P * i + P], gate_T[:, P * m:P * m + P], ro.b2[:, :],
                                    start=True, stop=True)
                ins.then_inc(bias_mm, 1)

            hidden(0, 0)
            for s in range(2):
                hidden(s + 1, s + 1)
                second(s, s)
            pe.wait_ge(counts_ready, 1)
            pe.wait_ge(consts, 1)
            w = 2 * NE
            last = upto[(NT.bit_length() - 2) % 2][:, NT - 1:NT, :]
            cnt = ps_r[:, 0, 0:NT * w]
            pe.matmul(cnt, ro.order[:, 0, :], last.to_broadcast([P, NT, w]), start=True, stop=False)
            pe.matmul(cnt, ro.order[:, 1, :], before[:, :, :], start=False, stop=False)
            pe.matmul(cnt.rearrange("p (i w) -> p i w", w=w)[:, :, NE:w], ones[:, :],
                      last[:, :, 0:NE].to_broadcast([P, NT, NE]), start=False, stop=False, skip_group_check=True)
            pe.matmul(cnt, ro.order[:, 2, :], chosen[:, :, :, :].rearrange("p i w e -> p (i w e)"), start=False,
                      stop=True).then_inc(count_mm, 1)
            hidden(3, 3)
            second(2, 2)
            pe.wait_ge(gate_ready, 1)
            for n in range(CHUNK):
                turn_gates(n)
            hidden(4, 4)
            second(3, 3)
            for n in range(2):
                biases(n)
            with pe.Fori(0, loops) as it:
                for q in range(body):
                    n = q + CHUNK
                    s = it * body + n
                    if (n + 1) % CHUNK == 0:
                        pe.wait_ge(w_split, it * 2 + (n + 1) // CHUNK - 1)
                    hidden(s + 1, n + 1)
                    second(s, n)
            for n in range(2, CHUNK):
                biases(n)
            for s in range(steps - CHUNK, steps - 1):
                hidden(s + 1, s + 1)
                second(s, s)

            def turn_y(n):
                pe.wait_ge(y_added, steps - CHUNK + n + 1)
                pe.wait_ge(hi_ready, steps * FT)
                for i in range(4):
                    m = 4 * n + i
                    ins = pe.transpose(ps_h[:, n, P * i:P * i + P], y_T[:, P * m:P * m + P], ident[:, :])
                ins.then_inc(y_turned, 1)

            for n in range(2):
                turn_y(n)
            second(steps - 1, steps - 1)
            for n in range(2, CHUNK):
                turn_y(n)


def hyena_moe_layer(nc, a, out):
    with ExitStack() as ctx:
        x1 = ctx.enter_context(nc.sbuf_tensor("x1", [P, NT, D], F32))
        ident = ctx.enter_context(nc.sbuf_tensor("ident", [P, P], F32))
        scr = {n: nc.dram_tensor("scr_" + n, (NH, PARTS, HD, L), BF16).ap() for n in "qk"}
        scr["o"] = nc.dram_tensor("scr_o", (NH, HD + 1, L), F32).ap()
        scr["gate"] = nc.dram_tensor("scr_gate", (NE, L), F32).ap()
        hyena(nc, a["attn"] | a["const"], x1, ident)
        z = ctx.enter_context(nc.sbuf_tensor("z", [P, NT, D], F32))
        ew = ExpertWeights(nc, ctx)
        ho = HeadOutputs(nc, ctx)
        with ExitStack() as att:
            vs = att.enter_context(nc.sbuf_tensor("vs", [P, NH, NT, HD], F32))
            attention_operands(nc, a["ffn"], x1, z, vs, ident, scr)
            attention(nc, a["ffn"] | a["const"], z, vs, ho, ew, ident, scr)
        h_part = {p: ctx.enter_context(nc.sbuf_tensor("h_T2_" + p, [P, L], F32R)) for p in W_PARTS}
        ro = Router(nc, ctx)
        with ExitStack() as full:
            h_T = full.enter_context(nc.sbuf_tensor("h_T2", [P, L], F32))
            attention_output(nc, a["ffn"] | a["const"], z, ho, h_T, h_part, ro, ident)
        experts(nc, a["ffn"] | a["const"], x1, z, h_part, ew, ro, ident, scr, out)


def kernel(**inputs):
    import numpy as _np
    import concourse.bacc as _bacc
    from concourse import mybir as _mybir
    from concourse.bass_utils import run_bass_kernel_spmd as _run

    nc = _bacc.Bacc("TRN2", target_bir_lowering=False, num_devices=1)
    arrays, a = {}, {"attn": {}, "ffn": {}, "const": {}}
    named = [(k, _np.ascontiguousarray(v)) for k, v in inputs.items()] + list(shape_constants().items())
    for name, v in named:
        arrays[f"in_{name}_dram"] = v
        ap = nc.dram_tensor(f"in_{name}_dram", v.shape, _mybir.dt.from_np(v.dtype), kind="ExternalInput").ap()
        group = next((g for g in ("attn", "ffn") if name.startswith(f"L0_{g}_")), "const")
        a[group][name.removeprefix(f"L0_{group}_")] = ap
    out = nc.dram_tensor("out_0_dram", (1, L, D), F32, kind="ExternalOutput").ap()
    a["attn"]["u"] = a["attn"]["u"].rearrange("o l d -> (o l) d")
    hyena_moe_layer(nc, a, out.rearrange("o l d -> (o l) d"))
    r = _run(nc, [arrays], core_ids=[0])
    return r.results[0]["out_0_dram"]
```

```python
from contextlib import ExitStack

import numpy as np

import concourse.bass as bass
from concourse import mybir

ALU = mybir.AluOpType
ACT = mybir.ActivationFunctionType
AX = mybir.AxisListType
F32 = mybir.dt.float32
BF16 = mybir.dt.bfloat16
F32R = mybir.dt.float32r

P = 128
L, D = 2048, 128
NT = L // P
ORDER, EMB, HID = 2, 33, 64
FREQ = 10.0
LN_EPS = 1e-5
BANK = 512
NB = 8

R = 64
N_FFT = R * R
H1 = R // 2
NJ = P // H1
assert N_FFT == 2 * L and NT * NJ == R

TWO_PI_HI = 6.28125
TWO_PI_LO = float(2 * np.pi - TWO_PI_HI)
ROUND = 1.5 * 2.0 ** 23

NH, HD = 16, 8
NE, FF = 8, 512
CAP = L // 4
FT = FF // P
KEEP = 0.8


def shape_constants():
    f32 = np.float32
    i, p = np.meshgrid(np.arange(NT), np.arange(P), indexing="ij")
    tok = R * (p % H1) + NJ * i + p // H1
    lin = np.linspace(0.0, 1.0, L, dtype=f32)
    bands = np.linspace(0.0, EMB - 1.0, EMB, dtype=f32)
    pe = np.sin((lin[:, None] * bands[None, :] * f32(FREQ)).astype(np.float64)).astype(f32)
    c = {"c_pe": pe[tok.reshape(-1)].T, "c_negt": -lin[tok].T}
    n1, n2, k2 = np.arange(H1), np.arange(R), np.arange(R)
    f1 = np.zeros((H1, R))
    f1[:, 0], f1[:, 1] = 1.0, (-1.0) ** n1
    g = np.zeros((R, H1))
    g[0], g[1] = 1.0, (-1.0) ** n1
    for m in range(1, H1):
        a = 2 * np.pi * n1 * m / R
        f1[:, 2 * m], f1[:, 2 * m + 1] = np.cos(a), -np.sin(a)
        g[2 * m], g[2 * m + 1] = 2 * np.cos(a), -2 * np.sin(a)
    c["c_f1"] = np.kron(np.eye(NJ), f1)
    c["c_g"] = np.kron(np.eye(2), g / (N_FFT * L))
    m_fwd = np.zeros((2, R, H1 + 1, 2, R))
    m_inv = np.zeros((2, R, H1 + 1, 2, R))
    for k1 in range(H1 + 1):
        th = 2 * np.pi * n2[:, None] * (k1 + R * k2[None, :]) / N_FFT
        if k1 == 0 or k1 == H1:
            m_fwd[k1 // H1, :, k1, 0], m_fwd[k1 // H1, :, k1, 1] = np.cos(th), -np.sin(th)
        else:
            m_fwd[0, :, k1, 0], m_fwd[1, :, k1, 0] = np.cos(th), np.sin(th)
            m_fwd[0, :, k1, 1], m_fwd[1, :, k1, 1] = -np.sin(th), np.cos(th)
        m_inv[0, :, k1, 0], m_inv[1, :, k1, 0] = np.cos(th).T, -np.sin(th).T
        m_inv[0, :, k1, 1], m_inv[1, :, k1, 1] = np.sin(th).T, np.cos(th).T
    c["c_fwd"] = m_fwd.reshape(P, -1)
    inv = m_inv.reshape(2, R, -1)
    c["c_inv"] = np.concatenate([inv[0], inv[1], -inv[0]])
    c["c_ident"] = np.eye(P)
    r = np.arange(P)
    c["c_sums"] = r[:, None] == r[None, :] // 32 * 32 + HD
    q = np.arange(P)
    jq, nq = q // H1, q % H1
    c["c_before"] = np.stack([
        nq[:, None] < nq[None, :],
        nq[:, None] == nq[None, :],
        (nq[:, None] == nq[None, :]) & (jq[:, None] <= jq[None, :]),
    ], axis=1).reshape(P, -1)
    return {k: np.ascontiguousarray(v, dtype=f32) for k, v in c.items()}


def tiles_of(dram):
    v = dram.rearrange("(n i j) d -> n i j d", i=NT, j=NJ)
    return [v[:, :, j, :] for j in range(NJ)]


def chain(eng, s):
    count = [0]

    def link(ins):
        count[0] += 1
        ins.then_inc(s, 1)
        eng.wait_ge(s, count[0])
    return link


class Norm:

    def __init__(self, nc, sb, sem, name):
        self.stats = sb(name + "_stats", [P, NT, 6], F32)
        self.mv = sb(name + "_mv", [P, NT, 2], F32)
        self.rstd = sb(name + "_rstd", [P, NT], F32)
        self.shift = sb(name + "_shift", [P, NT], F32)
        self.var_ready = sem(name + "_var_ready")
        self.std_ready = sem(name + "_std_ready")
        self.scales_ready = sem(name + "_scales_ready")

    def vector_stats(self, dve, link, x):
        link(self.vector_stats_of(dve, x, range(NT)))
        self.vector_var(dve, link)

    def vector_stats_of(self, dve, x, tiles):
        for i in tiles:
            ins = dve.bn_stats(self.stats[:, i, :], x[:, i, :])
        return ins

    def vector_mv(self, dve, tiles):
        for i in tiles:
            ins = dve.bn_aggr(self.mv[:, i, :], self.stats[:, i, :])
        return ins

    def vector_var(self, dve, link):
        link(self.vector_mv(dve, range(NT)))
        self.vector_var_only(dve)

    def vector_var_only(self, dve, tiles=range(NT)):
        t = slice(tiles.start, tiles.stop)
        dve.tensor_scalar(self.rstd[:, t], self.mv[:, t, 1], LN_EPS, None, ALU.add).then_inc(self.var_ready, 1)

    def scalar_sqrt(self, act, tiles=range(NT)):
        t = slice(tiles.start, tiles.stop)
        act.wait_ge(self.var_ready, 1)
        act.activation(self.rstd[:, t], self.rstd[:, t], ACT.Sqrt).then_inc(self.std_ready, 1)

    def vector_scales(self, dve, link, tiles=range(NT)):
        dve.wait_ge(self.std_ready, 1)
        t = slice(tiles.start, tiles.stop)
        link(dve.reciprocal(self.rstd[:, t], self.rstd[:, t]))
        dve.scalar_tensor_tensor(out=self.shift[:, t], in0=self.mv[:, t, 0], scalar=-1.0, in1=self.rstd[:, t],
                                 op0=ALU.mult, op1=ALU.mult).then_inc(self.scales_ready, 1)

    def scalar_apply(self, act, out, x, tiles):
        act.wait_ge(self.scales_ready, 1)
        for i in tiles:
            ins = act.activation(out[:, i, :], x[:, i, :], ACT.Identity, bias=self.shift[:, i:i + 1],
                                 scale=self.rstd[:, i:i + 1])
        return ins

    def vector_apply(self, dve, link, out, x, tiles=range(NT)):
        for i in tiles:
            ins = dve.tensor_scalar(out[:, i, :], x[:, i, :], self.mv[:, i, 0:1], self.rstd[:, i:i + 1],
                                    ALU.subtract, ALU.mult)
        return ins


def bcast_rows(vec, n):
    return bass.AP(vec.tensor, vec.offset, [[0, n]] + [list(x) for x in vec.ap])


class Units:

    def __init__(self):
        self.who, self.base = [], {}

    def stage(self, name, who):
        self.base[name] = len(self.who)
        self.who += who

    def number(self, name, n=0):
        return self.base[name] + n

    def taken(self, who, below):
        return sum(x in (who, "B") for x in self.who[:below])


def hyena(nc, a, x1, y, norm_y, ident):
    u = Units()
    alt = lambda n: ("AD" * n)[:n]
    u.stage("small_T", "D")
    u.stage("arg", "DDDD")
    u.stage("w_in_T", "A")
    u.stage("xn_T", alt(4))
    u.stage("proj", "A" * 12)
    u.stage("filt", "D" * 8)
    u.stage("branch_T0", alt(4))
    for o in range(ORDER):
        u.stage(f"h{o}_first", alt(8))
        u.stage(f"h{o}_turn", alt(8))
        if o == 0:
            u.stage("branch_T1", alt(4))
        u.stage(f"h{o}_spec", "B" * 9)
        u.stage(f"v{o}_first", alt(8))
        u.stage(f"v{o}_turn", alt(8))
        if o == 0:
            u.stage("branch_T2", alt(4))
        u.stage(f"v{o}_spec", "D" * 9)
        u.stage(f"v{o}_back", alt(8))
        u.stage(f"v{o}_return", alt(8))
        u.stage(f"v{o}_time", "D" * 4)
    u.stage("v_T", alt(4))
    u.stage("out", "D" * 4)

    with ExitStack() as ctx:
        def sb(name, shape, dt=F32):
            return ctx.enter_context(nc.sbuf_tensor("hy_" + name, shape, dt))

        def sem(name):
            return ctx.enter_context(nc.semaphore("hy_" + name))

        ps = ctx.enter_context(nc.psum_tensor("hy_ps", [P, NB, BANK], F32))
        branches = sb("branches", [P, NT, 3 * D])
        filt = [y, sb("filt", [P, NT, D])]
        buf_a = sb("buf_a", [P, (H1 + 1) * P])
        buf_b = sb("buf_b", [P, (H1 + 1) * P])
        buf_c = sb("buf_c", [P, (H1 + 1) * P])
        spec_re = sb("spec_re", [P, H1 + 1, P])
        spec_im = sb("spec_im", [P, H1 + 1, P])
        m_fwd = sb("m_fwd", [P, H1 + 1, P])
        m_inv = sb("m_inv", [P, H1 + 1, P])
        m_inv_i = sb("m_inv_i", [P, H1 + 1, P])
        f1 = sb("f1", [P, NJ * R])
        gt = sb("gt", [P, 2 * H1])
        w_in = sb("w_in", [P, 3, D])
        w_in_T = sb("w_in_T", [P, 3 * D])
        cw = sb("cw", [P, 3, 3])
        b_in = sb("b_in", [P, 3])
        conv_b = sb("conv_b", [P, 3])
        w1 = sb("w1", [HID, EMB])
        w2 = sb("w2", [P, 2, HID])
        b1 = sb("b1", [HID, 1])
        w1_T = sb("w1_T", [EMB, HID])
        w2_T = sb("w2_T", [P, ORDER * D])
        w_out = sb("w_out", [P, D])
        w_out_T = sb("w_out_T", [P, D])
        b_out = sb("b_out", [P, D])
        negt = sb("negt", [P, NT])
        rate = sb("rate", [P, ORDER * D])
        f_bias = sb("f_bias", [P, ORDER * D])
        xn_T = sb("xn_T", [P, L])
        PAD = (R + 2) * H1
        flat = lambda t: t[:, :, :].rearrange("p a b -> p (a b)")
        raw = [flat(m_inv)[:, 0:PAD], flat(m_inv)[:, PAD:2 * PAD], flat(m_inv_i)[:, 0:PAD]]
        conv = [buf_c[:, 0:L], buf_c[:, L:2 * L], flat(m_inv_i)[:, PAD:PAD + L]]
        pe_T = spec_im[0:EMB, :, :].rearrange("p a b -> p (a b)")[:, 2048:4096]
        arg = buf_a[0:HID, 0:L]
        turns = buf_a[0:HID, L:2 * L]
        sin_T = buf_b[:, 0:L]
        decay = spec_re[:, 0:H1, :].rearrange("p a b -> p (a b)").rearrange("p (i c) -> p i c", i=NT)
        xn = spec_im[:, 0:NT, :]
        norm_x = Norm(nc, sb, sem, "norm_x")

        x_loaded = sem("x_loaded")
        small_loaded = sem("small_loaded")
        tables_loaded = sem("tables_loaded")
        fwd_loaded = sem("fwd_loaded")
        inv_loaded = sem("inv_loaded")
        row_loaded = sem("row_loaded")
        pe_unit = sem("pe_unit")
        act_taken = sem("act_taken")
        dve_taken = sem("dve_taken")
        dve_chain = sem("dve_chain")
        pool_chain = sem("pool_chain")
        zeroed = sem("zeroed")
        middle_ready = sem("middle_ready")
        conv_ready = sem("conv_ready")
        arg_ready = sem("arg_ready")
        rate_ready = sem("rate_ready")
        sin_ready = sem("sin_ready")
        decay_ready = sem("decay_ready")
        xn_ready = sem("xn_ready")
        filt_ready = sem("filt_ready")
        spec_copied = sem("spec_copied")

        def taken(eng, below):
            if n := u.taken("A", below):
                eng.wait_ge(act_taken, n)
            if n := u.taken("D", below):
                eng.wait_ge(dve_taken, n)

        def bank(n):
            return ps[:, n % NB, :]

        def a_view(t):
            return t[:, 0:R * R].rearrange("p (c n) -> p n c", n=R)

        block = ctx.enter_context(nc.Block())

        small = [
            (w1[:, :], a["w1"]), (w2[:, :, :], a["w2"].rearrange("(b p) h -> p b h", p=P)),
            (w_out[:, :], a["w_out"]), (b1[:, :], a["b1"].rearrange("(p o) -> p o", o=1)),
            (ident[:, :], a["c_ident"]), (pe_T, a["c_pe"]),
            (rate[:, :], bcast_rows(a["filt_decay"].rearrange("o d -> (o d)"), P)),
            (negt[:, :], a["c_negt"]),
        ]
        tables = [
            (w_in[:, :, :], a["w_in"].rearrange("(b p) d -> p b d", p=P)),
            (cw[:, :, :], a["conv_w"].rearrange("(b p) k -> p b k", p=P)),
            (b_in[:, :], a["b_in"].rearrange("(b p) -> p b", p=P)),
            (conv_b[:, :], a["conv_b"].rearrange("(b p) -> p b", p=P)),
            (f1[:, :], a["c_f1"]), (gt[:, :], a["c_g"]),
            (f_bias[:, :], bcast_rows(a["filt_bias"].rearrange("o d -> (o d)"), P)),
            (b_out[:, :], bcast_rows(a["b_out"], P)),
        ]

        @block.sync
        def _(sp):
            for j, v in enumerate(tiles_of(a["u"])):
                sp.dma_start(x1[H1 * j:H1 * j + H1, :, :], v).then_inc(x_loaded, 16)
            sp.wait_ge(tables_loaded, 16 * len(tables))
            sp.dma_start(m_fwd[:, :, :].rearrange("p a b -> p (a b)"), a["c_fwd"]).then_inc(fwd_loaded, 16)
            sp.wait_ge(pe_unit, u.number("branch_T0", 4))
            sp.dma_start(m_inv_i[:, :, :].rearrange("p a b -> p (a b)"), a["c_inv"][R:R + P, :]).then_inc(inv_loaded, 16)
            for o in range(ORDER):
                taken(sp, u.number(f"h{o}_spec", 9))
                sp.dma_start(spec_re[R:P, :, :], spec_re[0:R, :, :]).then_inc(spec_copied, 16)
                sp.dma_start(spec_im[0:R, :, :], spec_im[R:P, :, :]).then_inc(spec_copied, 16)
                if o == 0:
                    sp.wait_ge(conv_ready, 3)
                    sp.dma_start(m_inv[:, :, :].rearrange("p a b -> p (a b)"), a["c_inv"][0:P, :])\
                      .then_inc(inv_loaded, 16)

        def mine(name, n, who):
            return u.who[u.number(name, n)] == who

        BRANCHES = (2, 0, 1)

        def take_xn(who, take):
            for n in range(4):
                if mine("xn_T", n, who):
                    take("xn_T", n, xn_T[:, BANK * n:BANK * n + BANK], bank(u.number("xn_T", n)))

        def take_branch(k, who, take):
            b, name = BRANCHES[k], f"branch_T{k}"
            for n in range(4):
                if mine(name, n, who):
                    take(name, n, branches[:, 4 * n:4 * n + 4, D * b:D * b + D],
                         bank(u.number(name, n)).rearrange("p (i d) -> p i d", d=D))

        def take_fft(name, who, take):
            for n in range(8):
                if mine(name + "_first", n, who):
                    src = bank(u.number(name + "_first", n)).rearrange("p (n c) -> p n c", c=R)
                    take(name + "_first", n, a_view(buf_a)[:, 8 * n:8 * n + 8, :], src)
            for n in range(8):
                if mine(name + "_turn", n, who):
                    take(name + "_turn", n, buf_b[:, BANK * n:BANK * n + BANK], bank(u.number(name + "_turn", n)))

        def spec_blocks(n):
            return slice(H1, H1 + 1) if n == 0 else slice(4 * n - 4, 4 * n)

        def take_spec(o, who, take):
            half, spec = (slice(0, R), spec_re) if who == "A" else (slice(R, P), spec_im)
            for n in range(9):
                dst = spec[half, spec_blocks(n), :].rearrange("p a b -> p (a b)")
                take(f"h{o}_spec", n, dst, bank(u.number(f"h{o}_spec", n))[half, 0:dst.shape[1]])

        def take_back(o, who, take):
            v = buf_b[:, 0:R * R].rearrange("p (n c) -> p c n", c=R)
            for n in range(8):
                if mine(f"v{o}_back", n, who):
                    src = bank(u.number(f"v{o}_back", n)).rearrange("p (c n) -> p c n", n=R)
                    take(f"v{o}_back", n, v[:, 8 * n:8 * n + 8, :], src)
            for n in range(8):
                if mine(f"v{o}_return", n, who):
                    take(f"v{o}_return", n, buf_a[:, BANK * n:BANK * n + BANK], bank(u.number(f"v{o}_return", n)))

        def take_v(who, take):
            for n in range(4):
                if mine("v_T", n, who):
                    take("v_T", n, buf_a[:, BANK * n:BANK * n + BANK], bank(u.number("v_T", n)))

        @block.gpsimd
        def _(pool):
            link = chain(pool, pool_chain)
            link(pool.memset(sin_T, 0.0))
            link(pool.memset(w2_T[:, :], 0.0))
            pool.dma_start(w2_T[HID:HID + 1, :], a["b2"].rearrange("(o d) -> o d", o=1)).then_inc(row_loaded, 16)
            link(pool.memset(sin_T[HID:HID + 1, :], 1.0))
            for b in range(3):
                link(pool.memset(raw[b][:, 0:1], 0.0))
                link(pool.memset(raw[b][:, PAD - 1:PAD], 0.0))
            pool.nop().then_inc(zeroed, 1)
            pool.wait_ge(tables_loaded, 16 * len(tables))
            for n in range(8):
                pool.wait_ge(dve_taken, u.taken("D", u.number("filt", n) + 1))
                for o in range(ORDER):
                    f = filt[o][:, 2 * n:2 * n + 2, :]
                    b = f_bias[:, o * D:o * D + D].rearrange("p (o d) -> p o d", o=1).to_broadcast([P, 2, D])
                    ins = pool.tensor_tensor(f, f, b, ALU.add)
                ins.then_inc(filt_ready, 1)

        @block.scalar
        def _(act):
            for dst, src in small:
                act.dma_start(dst, src).then_inc(small_loaded, 16)
            for dst, src in tables:
                act.dma_start(dst, src, allow_slow_non_contiguous=True).then_inc(tables_loaded, 16)
            norm_x.scalar_sqrt(act)
            act.wait_ge(small_loaded, 16 * len(small))
            act.activation(rate[:, :], rate[:, :], ACT.Exp).then_inc(rate_ready, 1)
            act.wait_ge(rate_ready, 1)
            for i in range(NT):
                ins = act.activation(decay[:, i, :], rate[:, :], ACT.Exp, scale=negt[:, i:i + 1])
            ins.then_inc(decay_ready, 1)

            def take(name, n, dst, src):
                act.wait_ge(pe_unit, u.number(name, n) + 1)
                act.activation(dst, src, ACT.Copy).then_inc(act_taken, 1)

            take("w_in_T", 0, w_in_T[:, :], bank(u.number("w_in_T"))[:, 0:3 * D])
            take_xn("A", take)
            act.wait_ge(zeroed, 1)
            for k, b in enumerate(BRANCHES):
                if k == 2:
                    act.wait_ge(arg_ready, 1)
                    act.activation(sin_T[0:HID, :], arg, ACT.Sin).then_inc(sin_ready, 1)
                for n in range(4):
                    m = u.number("proj", 4 * k + n)
                    act.wait_ge(pe_unit, m + 1)
                    act.activation(raw[b][:, H1 + BANK * n:H1 + BANK * n + BANK], bank(m), ACT.Identity,
                                   bias=b_in[:, b:b + 1]).then_inc(act_taken, 1)
                act.wait_ge(act_taken, u.taken("A", m + 1))
                act.activation(conv[b], raw[b][:, H1:H1 + L], ACT.Identity, bias=conv_b[:, b:b + 1],
                               scale=cw[:, b, 1:2]).then_inc(middle_ready, 1)
            take_branch(0, "A", take)
            for o in range(ORDER):
                take_fft(f"h{o}", "A", take)
                if o == 0:
                    take_branch(1, "A", take)
                take_spec(o, "A", take)
                take_fft(f"v{o}", "A", take)
                if o == 0:
                    take_branch(2, "A", take)
                take_back(o, "A", take)
            take_v("A", take)

        @block.vector
        def _(dve):
            link = chain(dve, dve_chain)

            def take(name, n, dst, src):
                dve.wait_ge(pe_unit, u.number(name, n) + 1)
                dve.tensor_copy(dst, src).then_inc(dve_taken, 1)

            dve.wait_ge(x_loaded, 16 * NJ)
            norm_x.vector_stats(dve, link, x1)
            dve.wait_ge(pe_unit, u.number("small_T") + 1)
            dve.wait_ge(row_loaded, 16)
            b = bank(u.number("small_T"))
            dve.tensor_copy(w1_T[:, :], b[0:EMB, 0:HID])
            dve.tensor_copy(w2_T[0:HID, :], b[0:HID, D:D + 2 * D])
            dve.tensor_copy(w_out_T[:, :], b[:, 3 * D:4 * D]).then_inc(dve_taken, 1)
            norm_x.vector_scales(dve, link)
            norm_x.vector_apply(dve, link, xn, x1).then_inc(xn_ready, 1)
            for n in range(4):
                dve.wait_ge(pe_unit, u.number("arg", n) + 1)
                dve.tensor_scalar(arg[:, BANK * n:BANK * n + BANK], bank(u.number("arg", n))[0:HID, :],
                                  b1[:, 0:1], FREQ, ALU.add, ALU.mult).then_inc(dve_taken, 1)
            take_xn("D", take)
            dve.wait_ge(dve_taken, u.taken("D", u.number("arg", 4)))
            link(dve.tensor_scalar(turns, arg, 1.0 / (2 * np.pi), ROUND, ALU.mult, ALU.add))
            link(dve.tensor_scalar(turns, turns, ROUND, None, ALU.subtract))
            link(dve.scalar_tensor_tensor(out=arg, in0=turns, scalar=-TWO_PI_HI, in1=arg, op0=ALU.mult, op1=ALU.add))
            link(dve.scalar_tensor_tensor(out=arg, in0=turns, scalar=-TWO_PI_LO, in1=arg, op0=ALU.mult, op1=ALU.add))
            dve.tensor_scalar(arg, arg, 3.1415925, -3.1415925, ALU.min, ALU.max).then_inc(arg_ready, 1)

            def convolve(k):
                b = BRANCHES[k]
                r = raw[b]
                dve.wait_ge(act_taken, u.taken("A", u.number("proj", 4 * k + 4)))
                dve.wait_ge(zeroed, 1)
                dve.tensor_copy(r[:, 1:H1], r[:, R * H1:R * H1 + H1 - 1])
                link(dve.tensor_copy(r[:, (R + 1) * H1:(R + 2) * H1 - 1], r[:, H1 + 1:2 * H1]))
                dve.wait_ge(middle_ready, k + 1)
                link(dve.scalar_tensor_tensor(out=conv[b], in0=r[:, 0:L], scalar=cw[:, b, 0:1], in1=conv[b],
                                              op0=ALU.mult, op1=ALU.add))
                dve.scalar_tensor_tensor(out=conv[b], in0=r[:, 2 * H1:2 * H1 + L], scalar=cw[:, b, 2:3],
                                         in1=conv[b], op0=ALU.mult, op1=ALU.add).then_inc(conv_ready, 1)

            convolve(0)
            dve.wait_ge(decay_ready, 1)
            for n in range(8):
                dve.wait_ge(pe_unit, u.number("filt", n) + 1)
                for o in range(ORDER):
                    c = slice(o * D, o * D + D)
                    ins = dve.tensor_tensor(filt[o][:, 2 * n:2 * n + 2, :],
                                            bank(u.number("filt", n)).rearrange("p (i c) -> p i c", i=2)[:, :, c],
                                            decay[:, 2 * n:2 * n + 2, c], ALU.mult)
                ins.then_inc(dve_taken, 1)
            take_branch(0, "D", take)
            convolve(1)
            for o in range(ORDER):
                take_fft(f"h{o}", "D", take)
                if o == 0:
                    take_branch(1, "D", take)
                take_spec(o, "D", take)
                if o == 0:
                    convolve(2)
                take_fft(f"v{o}", "D", take)
                if o == 0:
                    take_branch(2, "D", take)
                dve.wait_ge(act_taken, u.taken("A", u.number(f"v{o}_turn")))
                dve.wait_ge(spec_copied, 32 * (o + 1))
                for n in range(9):
                    m = u.number(f"v{o}_spec", n)
                    s = spec_blocks(n)
                    w = (s.stop - s.start) * P
                    dve.wait_ge(pe_unit, m + 1)
                    for spec, dst in ((spec_re, buf_a), (spec_im, buf_c)):
                        ins = dve.tensor_tensor(dst[:, s.start * P:s.stop * P], bank(m)[:, 0:w],
                                                spec[:, s, :].rearrange("p a b -> p (a b)"), ALU.mult)
                    ins.then_inc(dve_taken, 1)
                take_back(o, "D", take)
                for n in range(4):
                    m = u.number(f"v{o}_time", n)
                    dve.wait_ge(pe_unit, m + 1)
                    dve.tensor_tensor(branches[:, 4 * n:4 * n + 4, 2 * D:3 * D],
                                      bank(m).rearrange("p (i d) -> p i d", d=D),
                                      branches[:, 4 * n:4 * n + 4, o * D:o * D + D], ALU.mult)\
                       .then_inc(dve_taken, 1)
            take_v("D", take)
            for n in range(4):
                m = u.number("out", n)
                dve.wait_ge(pe_unit, m + 1)
                dve.tensor_tensor(y[:, 4 * n:4 * n + 4, :], bank(m).rearrange("p (i d) -> p i d", d=D),
                                  b_out[:, :].rearrange("p (o d) -> p o d", o=1).to_broadcast([P, 4, D]),
                                  ALU.add).then_inc(dve_taken, 1)
                dve.wait_ge(dve_taken, u.taken("D", m + 1))
                tiles = range(4 * n, 4 * n + 4)
                link(norm_y.vector_stats_of(dve, y, tiles))
                norm_y.vector_mv(dve, tiles)

        @block.tensor
        def _(pe):
            def start_unit(name, n=0):
                m = u.number(name, n)
                if m >= NB:
                    taken(pe, m - NB + 1)
                return bank(m)

            pe.wait_ge(small_loaded, 16 * len(small))
            b = start_unit("small_T")
            pe.transpose(b[0:EMB, 0:HID], w1[:, :], ident[0:HID, 0:HID])
            for k in range(2):
                pe.transpose(b[0:HID, D + D * k:2 * D + D * k], w2[:, k, :], ident[:, :])
            pe.transpose(b[:, 3 * D:4 * D], w_out[:, :], ident[:, :]).then_inc(pe_unit, 1)
            taken(pe, u.number("arg"))
            for n in range(4):
                b = start_unit("arg", n)
                pe.matmul(b[0:HID, :], w1_T[:, :], pe_T[:, BANK * n:BANK * n + BANK], start=True, stop=True)\
                  .then_inc(pe_unit, 1)
            pe.wait_ge(tables_loaded, 16 * len(tables))
            b = start_unit("w_in_T")
            for c in range(3):
                ins = pe.transpose(b[:, D * c:D * c + D], w_in[:, c, :], ident[:, :])
            ins.then_inc(pe_unit, 1)
            pe.wait_ge(xn_ready, 1)
            for n in range(4):
                b = start_unit("xn_T", n)
                for i in range(4):
                    ins = pe.transpose(b[:, P * i:P * i + P], xn[:, 4 * n + i, :], ident[:, :])
                ins.then_inc(pe_unit, 1)
            def fft(name, x):
                for n in range(8):
                    if name == "h0":
                        pe.wait_ge(filt_ready, n + 1)
                    elif name == "v0":
                        taken(pe, u.number("branch_T0", n // 2 + 1))
                    b = start_unit(name + "_first", n)
                    for i in (2 * n, 2 * n + 1):
                        ins = pe.matmul(b[:, 256 * (i % 2):256 * (i % 2) + 256], x[:, i, :], f1[:, :],
                                        start=True, stop=True)
                    ins.then_inc(pe_unit, 1)
                taken(pe, u.number(name + "_turn"))
                for n in range(8):
                    b = start_unit(name + "_turn", n)
                    for i in range(4):
                        m = 4 * n + i
                        ins = pe.transpose(b[:, P * i:P * i + P], buf_a[:, P * m:P * m + P], ident[:, :])
                    ins.then_inc(pe_unit, 1)

            def spec_unit(name, n):
                s = spec_blocks(n)
                taken(pe, u.number(name + "_turn", max(n - 1, 0) + 1))
                b = start_unit(name + "_spec", n)
                for q, k1 in enumerate(range(s.start, s.stop)):
                    m = k1 % H1
                    ins = pe.matmul(b[:, P * q:P * q + P], m_fwd[:, k1, :], buf_b[:, P * m:P * m + P], start=True, stop=True)
                ins.then_inc(pe_unit, 1)

            for k, c in enumerate(BRANCHES):
                for n in range(4):
                    taken(pe, u.number("xn_T", n + 1))
                    b = start_unit("proj", 4 * k + n)
                    pe.matmul(b, w_in_T[:, D * c:D * c + D], xn_T[:, BANK * n:BANK * n + BANK], start=True, stop=True)\
                      .then_inc(pe_unit, 1)
            pe.wait_ge(sin_ready, 1)
            for n in range(8):
                b = start_unit("filt", n)
                for i in (2 * n, 2 * n + 1):
                    ins = pe.matmul(b[:, 256 * (i % 2):256 * (i % 2) + 256], sin_T[:, P * i:P * i + P], w2_T[:, :],
                                    start=True, stop=True)
                ins.then_inc(pe_unit, 1)
            def turn_branch(k):
                pe.wait_ge(conv_ready, k + 1)
                for n in range(4):
                    b = start_unit(f"branch_T{k}", n)
                    for i in range(4):
                        m = 4 * n + i
                        ins = pe.transpose(b[:, P * i:P * i + P], conv[BRANCHES[k]][:, P * m:P * m + P], ident[:, :])
                    ins.then_inc(pe_unit, 1)

            turn_branch(0)
            for o in range(ORDER):
                fft(f"h{o}", filt[o])
                if o == 0:
                    turn_branch(1)
                pe.wait_ge(fwd_loaded, 16)
                for n in range(9):
                    spec_unit(f"h{o}", n)
                if o:
                    taken(pe, u.number(f"v{o - 1}_time", 4))
                fft(f"v{o}", branches[:, :, 2 * D:3 * D])
                if o == 0:
                    turn_branch(2)
                for n in range(9):
                    spec_unit(f"v{o}", n)
                pe.wait_ge(inv_loaded, 32)
                for n in range(8):
                    taken(pe, u.number(f"v{o}_spec", n + 2))
                    b = start_unit(f"v{o}_back", n)
                    for q in range(4):
                        k1 = 4 * n + q
                        parts = [(0, 0, R), (H1, R, R)] if k1 == 0 else [(k1, 0, P)]
                        for k, at, w in parts:
                            dst = b[:, P * q + at:P * q + at + w]
                            pe.matmul(dst, buf_a[:, P * k:P * k + P], m_inv[:, k, 0:w], start=True, stop=False)
                            ins = pe.matmul(dst, buf_c[:, P * k:P * k + P], m_inv_i[:, k, 0:w], start=False, stop=True)
                    ins.then_inc(pe_unit, 1)
                taken(pe, u.number(f"v{o}_return"))
                for n in range(8):
                    b = start_unit(f"v{o}_return", n)
                    for i in range(4):
                        m = 4 * n + i
                        ins = pe.transpose(b[:, P * i:P * i + P], buf_b[:, P * m:P * m + P], ident[:, :])
                    ins.then_inc(pe_unit, 1)
                for n in range(4):
                    taken(pe, u.number(f"v{o}_return", 2 * n + 2))
                    b = start_unit(f"v{o}_time", n)
                    for jh in range(2):
                        rhs = buf_a[:, 8 * n * P:8 * (n + 1) * P].rearrange("p (i q c) -> p q i c", q=2, c=P)[:, jh]
                        ins = pe.matmul(b[R * jh:R * jh + R, :], gt[:, :], rhs, start=True, stop=True)
                    ins.then_inc(pe_unit, 1)
            for n in range(4):
                taken(pe, u.number(f"v{ORDER - 1}_time", n + 1))
                b = start_unit("v_T", n)
                for i in range(4):
                    ins = pe.transpose(b[:, P * i:P * i + P], branches[:, 4 * n + i, 2 * D:3 * D], ident[:, :])
                ins.then_inc(pe_unit, 1)
            for n in range(4):
                taken(pe, u.number("v_T", n + 1))
                b = start_unit("out", n)
                for i in range(4):
                    m = 4 * n + i
                    ins = pe.matmul(b[:, P * i:P * i + P], buf_a[:, P * m:P * m + P], w_out_T[:, :], start=True, stop=True)
                ins.then_inc(pe_unit, 1)




class ScoreOperands:

    def __init__(self, nc, ctx):
        def sb(name, shape, dt):
            return ctx.enter_context(nc.sbuf_tensor("so_" + name, shape, dt))
        self.q = [sb(f"q{b}", [P, L], BF16) for b in range(G)]
        self.k = [sb(f"k{b}", [P, L], BF16) for b in range(G)]
        self.v = [sb(f"v{b}", [P, NT, 32], F32) for b in range(G)]
        self.neg_parts = sb("neg_parts", [P, P], BF16)
        self.ident_b = sb("ident_b", [P, P], BF16)

    def fill(self, pool, link, ident):
        for b in range(G):
            link(pool.memset(self.q[b][:, :].bitcast(F32), 0.0))
            link(pool.memset(self.k[b][:, :].bitcast(F32), 0.0))
            link(pool.memset(self.k[b][MROW:MROW + PARTS, :], 1.0))
            link(pool.memset(self.v[b][:, :, :], 0.0))
            link(pool.memset(self.v[b][:, :, HD:2 * HD], 1.0))
        link(pool.memset(self.neg_parts[:, :], 0.0))
        link(pool.tensor_copy(self.ident_b[:, :], ident[:, :]))


class Norm2:

    def __init__(self, nc, sb, sem, name):
        self.one = Norm(nc, sb, sem, name)
        self.scale = sb(name + "_scale2", [P, 2, NT], F32)
        self.shift = sb(name + "_shift2", [P, 2, NT], F32)

    def vector_var(self, dve):
        v = self.one.mv[:, :, 1]
        dve.tensor_scalar(self.scale[:, 0, :], v, LN_EPS, None, ALU.add)
        dve.tensor_scalar(self.scale[:, 1, :], v, 1.0 + LN_EPS, LN_EPS ** 2, ALU.mult, ALU.add)\
            .then_inc(self.one.var_ready, 1)

    def scalar_sqrt(self, act):
        act.wait_ge(self.one.var_ready, 1)
        act.activation(self.scale[:, :, :], self.scale[:, :, :], ACT.Sqrt).then_inc(self.one.std_ready, 1)

    def vector_scales(self, dve, link):
        dve.wait_ge(self.one.std_ready, 1)
        link(dve.reciprocal(self.scale[:, :, :], self.scale[:, :, :]))
        for i in range(2):
            ins = dve.scalar_tensor_tensor(out=self.shift[:, i, :], in0=self.one.mv[:, :, 0], scalar=-1.0,
                                           in1=self.scale[:, i, :], op0=ALU.mult, op1=ALU.mult)
        ins.then_inc(self.one.scales_ready, 1)


def attention_operands(nc, a, x, y, norm_y, norm_12, vs, so, ident, scr):
    u = Units()
    u.stage("h_T", "DDDD")
    for n in range(CHUNK):
        u.stage(f"q{n}", "D")
        u.stage(f"k{n}", "A")
    u.stage("v", "DDDD")
    with ExitStack() as ctx:
        def sb(name, shape, dt=F32):
            return ctx.enter_context(nc.sbuf_tensor("op_" + name, shape, dt))

        def sem(name):
            return ctx.enter_context(nc.semaphore("op_" + name))

        ps = ctx.enter_context(nc.psum_tensor("op_ps", [P, NB, BANK], F32))
        zn = sb("zn", [P, NT, D])
        h_T = sb("h_T", [P, L])
        w = {n: sb("w" + n, [P, D]) for n in "qkv"}
        bias = {n: sb("bias_" + n, [P, 1]) for n in "qk"}
        bias_v = sb("bias_v", [P, D])
        g1 = sb("g1", [P, 1])
        be1 = sb("be1", [P, 1])
        full = {n: sb("full_" + n, [P, L]) for n in "qk"}
        part = {n: sb("part_" + n, [P, PARTS, L], BF16) for n in "qk"}

        loaded = sem("loaded")
        chain_d = sem("chain")
        pool_chain = sem("pool_chain")
        pe_unit = sem("pe_unit")
        dve_taken = sem("dve_taken")
        act_taken = sem("act_taken")
        zn_ready = {e: sem("zn_ready_" + e) for e in ("dve", "act")}
        first_ready = sem("first_ready")
        second_ready = sem("second_ready")
        rest_ready = sem("rest_ready")
        third_ready = sem("third_ready")
        stored = sem("parts_stored")
        col = lambda v: v.rearrange("(p o) -> p o", o=1)
        loads = [(g1[:, :], col(a["ln1_g"])), (be1[:, :], col(a["ln1_b"]))]
        loads += [(w[n][:, :], a["w" + n]) for n in "qkv"]
        loads += [(bias[n][:, :], col(a["b" + n])) for n in "qk"]
        loads += [(bias_v[:, :], bcast_rows(a["bv"], P))]
        names = [(n, name) for n in range(CHUNK) for name in "qk"]

        def bank(name, n=0):
            return ps[:, u.number(name, n) % NB, :]

        def cols(n):
            return slice(BANK * n, BANK * n + BANK)

        block = ctx.enter_context(nc.Block())

        @block.sync
        def _(sp):
            for dst, src in loads:
                sp.dma_start(dst, src).then_inc(loaded, 16)
            for m, (n, name) in enumerate(names):
                sp.wait_ge(third_ready, m + 1)
                sp.dma_start(scr[name].rearrange("h e a t -> (h e) a t")[:, :, cols(n)], part[name][:, :, cols(n)])\
                  .then_inc(stored, 16)
            sp.wait_ge(stored, 16 * len(names))

        @block.gpsimd
        def _(pool):
            so.fill(pool, chain(pool, pool_chain), ident)
            for m, (n, name) in enumerate(names):
                pool.wait_ge(second_ready, m + 1)
                pool.tensor_tensor(part[name][:, 2, cols(n)], full[name][:, cols(n)], part[name][:, 1, cols(n)],
                                   ALU.subtract).then_inc(third_ready, 1)

        @block.scalar
        def _(act):
            norm_y.scalar_sqrt(act)
            norm_12.scalar_sqrt(act)
            act.wait_ge(norm_12.one.scales_ready, 1)
            for c in (1, 3):
                for i in range(4 * c, 4 * c + 4):
                    ins = act.activation(zn[:, i, :], y[:, i, :], ACT.Identity, bias=norm_12.shift[:, 1, i:i + 1],
                                         scale=norm_12.scale[:, 1, i:i + 1])
                ins.then_inc(zn_ready["act"], 1)

            def second(m):
                n, name = names[m]
                act.wait_ge(rest_ready, m + 1)
                act.activation(part[name][:, 1, cols(n)], full[name][:, cols(n)], ACT.Copy).then_inc(second_ready, 1)

            for m, (n, name) in enumerate(names):
                if name == "q":
                    act.wait_ge(dve_taken, u.taken("D", u.number(f"q{n}") + 1))
                else:
                    act.wait_ge(pe_unit, u.number(f"k{n}") + 1)
                    act.activation(full["k"][:, cols(n)], bank(f"k{n}"), ACT.Identity, bias=bias["k"][:, 0:1])\
                       .then_inc(act_taken, 1)
                    act.wait_ge(act_taken, u.taken("A", u.number(f"k{n}") + 1))
                act.activation(part[name][:, 0, cols(n)], full[name][:, cols(n)], ACT.Copy).then_inc(first_ready, 1)
                if m >= 2:
                    second(m - 2)
            for m in range(len(names) - 2, len(names)):
                second(m)

        @block.vector
        def _(dve):
            link = chain(dve, chain_d)
            norm_y.vector_var_only(dve)
            norm_y.vector_scales(dve, link)
            for c in range(4):
                tiles = range(4 * c, 4 * c + 4)
                for i in tiles:
                    ins = dve.scalar_tensor_tensor(out=y[:, i, :], in0=y[:, i, :], scalar=norm_y.rstd[:, i:i + 1],
                                                   in1=x[:, i, :], op0=ALU.mult, op1=ALU.add)
                link(ins)
                link(norm_12.one.vector_stats_of(dve, y, tiles))
                ins = norm_12.one.vector_mv(dve, tiles)
            link(ins)
            norm_12.vector_var(dve)
            norm_12.vector_scales(dve, link)
            dve.wait_ge(norm_12.one.scales_ready, 1)
            for c in (0, 2):
                for i in range(4 * c, 4 * c + 4):
                    ins = dve.tensor_scalar(zn[:, i, :], y[:, i, :], norm_12.scale[:, 1, i:i + 1],
                                            norm_12.shift[:, 1, i:i + 1], ALU.mult, ALU.add)
                ins.then_inc(zn_ready["dve"], 1)
            dve.wait_ge(loaded, 16 * len(loads))
            for n in range(4):
                dve.wait_ge(pe_unit, u.number("h_T", n) + 1)
                dve.tensor_scalar(h_T[:, cols(n)], bank("h_T", n), g1[:, 0:1], be1[:, 0:1],
                                  ALU.mult, ALU.add).then_inc(dve_taken, 1)

            def rest(m):
                n, name = names[m]
                dve.wait_ge(first_ready, m + 1)
                dve.tensor_tensor(full[name][:, cols(n)], full[name][:, cols(n)], part[name][:, 0, cols(n)],
                                  ALU.subtract).then_inc(rest_ready, 1)

            for n in range(CHUNK):
                dve.wait_ge(pe_unit, u.number(f"q{n}") + 1)
                dve.tensor_scalar(full["q"][:, cols(n)], bank(f"q{n}"), bias["q"][:, 0:1], HD ** -0.5,
                                  ALU.add, ALU.mult).then_inc(dve_taken, 1)
                if n:
                    rest(2 * n - 2)
                    rest(2 * n - 1)
            rest(2 * CHUNK - 2)
            rest(2 * CHUNK - 1)
            for n in range(4):
                dve.wait_ge(pe_unit, u.number("v", n) + 1)
                dve.tensor_tensor(
                    vs[:, :, 4 * n:4 * n + 4, :].rearrange("p h i e -> p i h e"),
                    bank("v", n).rearrange("p (i h e) -> p i h e", i=4, h=NH),
                    bias_v[:, :].rearrange("p (o h e) -> p o h e", o=1, h=NH).to_broadcast([P, 4, NH, HD]),
                    ALU.add).then_inc(dve_taken, 1)

        @block.tensor
        def _(pe):
            for n in range(4):
                pe.wait_ge(zn_ready["act" if n % 2 else "dve"], n // 2 + 1)
                for i in range(4):
                    ins = pe.transpose(bank("h_T", n)[:, P * i:P * i + P], zn[:, 4 * n + i, :], ident[:, :])
                ins.then_inc(pe_unit, 1)
            pe.wait_ge(loaded, 16 * len(loads))
            for n in range(CHUNK):
                pe.wait_ge(dve_taken, u.taken("D", u.number("h_T", n) + 1))
                for name in "qk":
                    m = u.number(f"{name}{n}")
                    if m >= NB:
                        pe.wait_ge(dve_taken, u.taken("D", m - NB + 1))
                    pe.matmul(bank(f"{name}{n}"), w[name][:, :], h_T[:, cols(n)], start=True, stop=True)\
                      .then_inc(pe_unit, 1)
            for n in range(4):
                m = u.number("v", n) - NB + 1
                pe.wait_ge(dve_taken, u.taken("D", m))
                pe.wait_ge(act_taken, max(1, u.taken("A", m)))
                for i in range(4):
                    t = P * (4 * n + i)
                    ins = pe.matmul(bank("v", n)[:, P * i:P * i + P], h_T[:, t:t + P], w["v"][:, :],
                                    start=True, stop=True)
                ins.then_inc(pe_unit, 1)


PARTS = 3
ROWS = PARTS * PARTS * HD
MROW = 96
assert ROWS <= MROW
G = 3
AHEAD = NT + 3
CHUNK = L // BANK
N_STEP = NH * NT


class HeadOutputs:

    def __init__(self, nc, ctx):
        def sb(name, shape):
            return ctx.enter_context(nc.sbuf_tensor("ho_" + name, shape, F32))
        self.rows = (NH - 1) * HD
        self.o_T = sb("o_T", [self.rows, L])
        self.sums = sb("sums", [self.rows, L])
        self.last_o = sb("last_o", [P, BANK])
        self.last_scale = sb("last_scale", [P, BANK])
        self.sum_rows = sb("sum_rows", [P, P])
        self.wo = sb("wo", [self.rows, D])
        self.wo_last = sb("wo_last", [P, D])
        self.bo = sb("bo", [P, D])


def attention(nc, a, x1, z, norm_y, norm_12, vs, so, ho, ew, scr):
    loops = (NH - 1) // G
    assert loops * G == NH - 1
    body = G * NT
    with ExitStack() as ctx:
        def sb(name, shape, dt=F32):
            return ctx.enter_context(nc.sbuf_tensor("at_" + name, shape, dt))

        def sem(name):
            return ctx.enter_context(nc.semaphore("at_" + name))

        ps_s = ctx.enter_context(nc.psum_tensor("ps_s", [P, 2, 2 * BANK], F32))
        ps_m = ctx.enter_context(nc.psum_tensor("ps_m", [P, 3, BANK], F32))
        ps_o = ctx.enter_context(nc.psum_tensor("ps_o", [P, BANK], F32))
        ps_t = ps_s[:, 1, 0:P // 2].bitcast(BF16)
        q_op, k_op, v_op, neg_parts, ident_b = so.q, so.k, so.v, so.neg_parts, so.ident_b
        prob = [sb(f"prob{b}", [P, L]) for b in range(3)]
        o_out = [sb(f"o_out{b}", [P, BANK]) for b in range(G)]
        maxes = sb("maxes", [P, NT, CHUNK])
        neg = sb("neg", [P, NT])
        zeros = sb("zeros", [P, NT])
        neg_T = sb("neg_T", [PARTS * NT, P], BF16)

        z_ready = sem("z_ready")
        pool_chain = sem("pool_chain")
        op_loaded = [sem(f"op_loaded{b}") for b in range(G)]
        score_ready = sem("score_ready")
        exp_done = sem("exp_done")
        max_mm = sem("max_mm")
        max_done = sem("max_done")
        pv_done = sem("pv_done")
        neg_max = sem("neg_max")
        neg_chain = sem("neg_chain")
        neg_ready = sem("neg_ready")
        neg_turned = sem("neg_turned")
        neg_T_ready = sem("neg_T_ready")
        row_loaded = sem("neg_row_loaded")
        v_ready = sem("v_ready")
        o_taken = sem("o_taken")
        o_stored = [sem(f"o_stored{b}") for b in range(G)]

        ho_loaded = sem("ho_loaded")
        heads_loaded = sem("heads_loaded")
        sums_chain = sem("sums_chain")
        w_loaded = [sem(f"w_loaded{b}") for b in range(2)]
        w_hi_ready = sem("w_hi_ready")
        ho_loads = [(ho.wo[:, :], a["wo"][0:ho.rows, :]), (ho.bo[:, :], bcast_rows(a["bo"], P)),
                    (ho.sum_rows[:, :], a["c_sums"])]
        ho_loads += [(ho.wo_last[32 * j:32 * j + HD, :], a["wo"][ho.rows:D, :]) for j in range(CHUNK)]

        N_LOAD = 4
        TURN = 13
        FREE_SCORE, FREE_MAX, FREE_PROB = 2, 3, 3

        block = ctx.enter_context(nc.Block())

        @block.sync
        def _(sp):
            def load(h, b):
                q = scr["q"][bass.ds(h, 1)].rearrange("o e a t -> (o e a) t")
                sp.dma_start(q_op[b][0:ROWS, :],
                             q.rearrange("(o r) t -> o r t", o=1).to_broadcast([PARTS, PARTS * HD, L]))\
                  .then_inc(op_loaded[b], 16)
                for c in range(PARTS):
                    k = scr["k"][bass.ds(h, 1), :, c:c + 1].rearrange("o e c t -> (o e) c t")
                    sp.dma_start(k_op[b][PARTS * HD * c:PARTS * HD * (c + 1), :],
                                 k.to_broadcast([HD, PARTS, L]))\
                      .then_inc(op_loaded[b], 16)

            def neg_rows(h, b):
                sp.wait_ge(neg_T_ready, h + 1)
                sp.dma_start(q_op[b][MROW:MROW + PARTS, :], neg_T[:, :]).then_inc(row_loaded, 16)

            def store(h, b):
                sp.wait_ge(o_taken, h + 2)
                for j in range(CHUNK):
                    sp.dma_start(scr["o"][bass.ds(h, 1), :, BANK * j:BANK * j + BANK].rearrange("o e q -> (o e) q"),
                                 o_out[b][32 * j:32 * j + HD + 1, :]).then_inc(o_stored[b], 16)

            def head(h, r, load_next):
                neg_rows(h + 1, (r + 1) % G)
                sp.wait_ge(score_ready, (h + 1) * (2 * NT))
                if load_next:
                    load(h + G, r)
                elif h == NH - G:
                    sp.nop().then_inc(op_loaded[NH % G], 16 * N_LOAD)
                store(h, r)

            for b in range(G):
                load(b, b)
            for e in range(2):
                ew.load(sp, a, e, e, w_loaded[e])
            for dst, src in ho_loads:
                sp.dma_start(dst, src).then_inc(ho_loaded, 16)
            neg_rows(0, 0)
            with sp.Fori(0, loops - 1) as it:
                for r in range(G):
                    head(it * G + r, r, True)
            for h in range((loops - 1) * G, NH - 1):
                head(h, h % G, h + G < NH)
            for b in range(G):
                sp.wait_ge(o_stored[b], 16 * CHUNK * (1 + len(range(b, NH - 1, G))))
            sp.dma_start(ho.sums[:, :], scr["o"][0:NH - 1, HD:HD + 1, :].to_broadcast([NH - 1, HD, L]))\
              .then_inc(heads_loaded, 16)
            sp.dma_start(ho.o_T[:, :], scr["o"][0:NH - 1, 0:HD, :]).then_inc(heads_loaded, 16)

        @block.gpsimd
        def _(pool):
            link = chain(pool, pool_chain)
            for h in range(G):
                pool.tensor_copy(v_op[h][:, :, 0:HD], vs[:, h, :, :]).then_inc(v_ready, 1)
            link(pool.memset(zeros[:, :], 0.0))
            for i in range(NT):
                link(pool.tensor_scalar(x1[:, i, :], z[:, i, :], norm_y.shift[:, i:i + 1], None, ALU.add))
            for i in range(NT):
                link(pool.tensor_scalar(z[:, i, :], z[:, i, :], norm_12.scale[:, 0, i:i + 1],
                                        norm_12.shift[:, 0, i:i + 1], ALU.mult, ALU.add))
            pool.nop().then_inc(z_ready, 1)

            def split_neg(h):
                pool.wait_ge(neg_max, h + 1)
                part = [neg_parts[:, NT * i:NT * (i + 1)] for i in range(PARTS)]
                pool.tensor_tensor(part[0], neg[:, :], zeros[:, :], ALU.add).then_inc(neg_chain, 1)
                pool.wait_ge(neg_chain, h * 3 + 1)
                pool.tensor_tensor(neg[:, :], neg[:, :], part[0], ALU.subtract).then_inc(neg_chain, 1)
                pool.wait_ge(neg_chain, h * 3 + 2)
                pool.tensor_tensor(part[1], neg[:, :], zeros[:, :], ALU.add).then_inc(neg_chain, 1)
                pool.wait_ge(neg_chain, h * 3 + 3)
                pool.tensor_tensor(part[2], neg[:, :], part[1], ALU.subtract).then_inc(neg_ready, 1)

            split_neg(0)
            for e in range(2):
                pool.wait_ge(w_hi_ready, e + 1)
                ew.pool_lo(pool, e)
            with pool.Fori(0, loops - 1) as it:
                for r in range(G):
                    split_neg(it * G + (r + 1))
                    pool.wait_ge(pv_done, it * body + (FREE_PROB + (r + 1) * NT))
                    pool.tensor_copy(v_op[r][:, :, 0:HD], vs[:, bass.ds(it * G + (G + r), 1), :, :]
                                     .rearrange("p o i e -> p (o i) e")).then_inc(v_ready, 1)
            for h in range(NH - G, NH):
                split_neg(h)
                if h == NH - G:
                    pool.wait_ge(pv_done, FREE_PROB + (NH - G) * NT)
                    pool.tensor_copy(v_op[(NH - 1) % G][:, :, 0:HD], vs[:, NH - 1, :, :]).then_inc(v_ready, 1)

        @block.scalar
        def _(act):
            def exps(s, n):
                for half in range(2):
                    act.wait_ge(score_ready, s * 2 + (half + 1))
                    if half == 0:
                        act.wait_ge(pv_done, s + 1)
                    act.activation(prob[n % 3][:, 2 * BANK * half:2 * BANK * (half + 1)], ps_s[:, half, :], ACT.Exp)\
                       .then_inc(exp_done, 1)

            def take_neg(h, first=False):
                act.wait_ge(neg_turned, h + 1)
                if not first:
                    act.wait_ge(row_loaded, h * 16)
                act.activation(neg_T[:, :], ps_t[0:PARTS * NT, 0:P], ACT.Copy).then_inc(neg_T_ready, 1)

            def take_out(h, it, r):
                act.wait_ge(pv_done, h * NT + (FREE_PROB + NT))
                act.wait_ge(o_stored[r], it * (16 * CHUNK) + 16 * CHUNK)
                act.activation(o_out[r][:, :], ps_o[:, :], ACT.Copy).then_inc(o_taken, 1)

            for e in range(2):
                act.wait_ge(w_loaded[e], 32)
                ew.scalar_hi(act, e).then_inc(w_hi_ready, 1)
            act.nop().then_inc(exp_done, FREE_SCORE)
            act.nop().then_inc(o_taken, 1)
            for b in range(G):
                act.nop().then_inc(o_stored[b], 16 * CHUNK)
            take_neg(0, first=True)
            exps(0, 0)
            with act.Fori(0, loops) as it:
                for q in range(body):
                    if q % NT == TURN:
                        take_neg(it * G + (q // NT + 1))
                    exps(it * body + (q + 1), q + 1)
                    if q % NT == NT - 1:
                        take_out(it * G + q // NT, it, q // NT)
            for s in range(loops * body + 1, N_STEP):
                exps(s, s)
            act.wait_ge(pv_done, FREE_PROB + NH * NT)
            act.activation(ho.last_o[:, :], ps_o[:, :], ACT.Copy)

        @block.vector
        def _(dve):
            def maxima(t, n):
                for c in range(CHUNK):
                    dve.wait_ge(max_mm, t * CHUNK + (c + 1))
                    dve.tensor_reduce(maxes[:, n % NT, c:c + 1], ps_m[:, (n * CHUNK + c) % 3, :], AX.X, ALU.max)\
                       .then_inc(max_done, 1)

            def negate(h, first=False):
                dve.wait_ge(max_done, h * (NT * CHUNK) + (FREE_MAX + NT * CHUNK))
                if not first:
                    dve.wait_ge(neg_turned, h)
                dve.tensor_reduce(neg[:, :], maxes[:, :, :], AX.X, ALU.max, negate=True).then_inc(neg_max, 1)
                dve.wait_ge(neg_max, h + 1)

            dve.nop().then_inc(max_done, FREE_MAX)
            for t in range(AHEAD + 1):
                maxima(t, t)
                if t == NT - 1:
                    negate(0, first=True)
            with dve.Fori(0, loops) as it:
                for q in range(body):
                    n = q + 1 + AHEAD
                    maxima(it * body + n, n)
                    if n % NT == NT - 1:
                        negate(it * G + n // NT)
            dve.wait_ge(ho_loaded, 16 * len(ho_loads))
            dve.wait_ge(z_ready, 1)
            dve.tensor_tensor(z[:, :, :], z[:, :, :],
                              ho.bo[:, :].rearrange("p (o d) -> p o d", o=1).to_broadcast([P, NT, D]), ALU.add)
            dve.wait_ge(heads_loaded, 32)
            dve.reciprocal(ho.sums[:, :], ho.sums[:, :]).then_inc(sums_chain, 1)
            dve.wait_ge(sums_chain, 1)
            dve.tensor_tensor(ho.o_T[:, :], ho.o_T[:, :], ho.sums[:, :], ALU.mult)

        @block.tensor
        def _(pe):
            def scores(s, n, halves=range(2)):
                b, k = n // NT % G, n % NT
                for half in halves:
                    pe.wait_ge(exp_done, s * 2 + (half + 1))
                    for c in range(2):
                        at = BANK * (2 * half + c)
                        ins = pe.matmul(ps_s[:, half, BANK * c:BANK * (c + 1)], k_op[b][:, P * k:P * (k + 1)],
                                        q_op[b][:, at:at + BANK], start=True, stop=True)
                    ins.then_inc(score_ready, 1)

            def max_scores(t, n, it, banks=range(CHUNK)):
                b, i = n // NT % G, n % NT
                if i == 0 and banks[0] == 0:
                    pe.wait_ge(op_loaded[b], (it + n // NT // G + 1) * (16 * N_LOAD))
                for c in banks:
                    pe.wait_ge(max_done, t * CHUNK + (c + 1))
                    pe.matmul(ps_m[:, (n * CHUNK + c) % 3, :], q_op[b][0:MROW, P * i:P * (i + 1)],
                              k_op[b][0:MROW, BANK * c:BANK * (c + 1)], start=True, stop=True).then_inc(max_mm, 1)

            def turn_neg(h, s):
                pe.wait_ge(neg_ready, h + 1)
                pe.wait_ge(exp_done, s * 2 + 2)
                pe.transpose(ps_t[:, 0:P], neg_parts[:, :], ident_b[:, :]).then_inc(neg_turned, 1)

            def outputs(s, n, h):
                b, k = n // NT % G, n % NT
                if k == 0:
                    pe.wait_ge(v_ready, h + 1)
                    pe.wait_ge(o_taken, h + 1)
                pe.wait_ge(exp_done, s * 2 + (FREE_SCORE + 2))
                for j in range(CHUNK):
                    ins = pe.matmul(ps_o[32 * j:32 * j + 32, :], v_op[b][:, k, :],
                                    prob[n % 3][:, BANK * j:BANK * (j + 1)], start=(k == 0), stop=(k == NT - 1))
                ins.then_inc(pv_done, 1)

            pe.nop().then_inc(pv_done, FREE_PROB)
            for t in range(AHEAD + 1):
                max_scores(t, t, 0)
                if t == NT + 1:
                    turn_neg(0, 0)
            pe.wait_ge(row_loaded, 16)
            scores(0, 0)
            with pe.Fori(0, loops) as it:
                for q in range(body):
                    n = q + 1
                    if n % NT == 0:
                        pe.wait_ge(row_loaded, it * (16 * G) + (n // NT + 1) * 16)
                    m = n + AHEAD
                    turned = q % NT == TURN
                    if turned:
                        turn_neg(it * G + (q // NT + 1), it * body + n)
                    max_scores(it * body + m, m, it, [0])
                    scores(it * body + n, n, [0])
                    max_scores(it * body + m, m, it, [1])
                    if turned:
                        pe.wait_ge(neg_T_ready, it * G + (q // NT + 2))
                    scores(it * body + n, n, [1])
                    max_scores(it * body + m, m, it, [2, 3])
                    outputs(it * body + q, q, it * G + q // NT)
            for s in range(loops * body + 1, N_STEP):
                scores(s, s)
                outputs(s - 1, s - 1, NH - 1)
            outputs(N_STEP - 1, N_STEP - 1, NH - 1)


class Router:

    def __init__(self, nc, ctx):
        def sb(name, shape):
            return ctx.enter_context(nc.sbuf_tensor("ro_" + name, shape, F32))
        self.logits = sb("logits", [P, NT, NE])
        self.b1_T = sb("b1_T", [P, NE * FT])
        self.b2 = sb("b2_rows", [NE, D])
        self.order = sb("order", [P, 3, P])


def attention_output(nc, a, z, ho, h_T, h_part, ro, ident):
    with ExitStack() as ctx:
        def sb(name, shape, dt=F32):
            return ctx.enter_context(nc.sbuf_tensor("ao_" + name, shape, dt))

        def sem(name):
            return ctx.enter_context(nc.semaphore("ao_" + name))

        ps = ctx.enter_context(nc.psum_tensor("ao_ps", [P, NB, BANK], F32))
        g2 = sb("g2", [P, 1])
        be2 = sb("be2", [P, 1])
        zn = sb("zn2", [P, NT, D])
        wr = sb("wr", [P, 32])
        logits_T = sb("logits_T", [P, BANK])
        b1_rows = sb("b1_rows", [NE * FT, P])
        norm_3 = Norm(nc, sb, sem, "norm_3")
        sums_mm = sem("sums_mm")
        loaded = sem("loaded")
        chain_d = sem("chain")
        last_ready = sem("last_ready")
        pe_unit = sem("pe_unit")
        zn_ready = sem("zn2_ready")
        zn_ready_act = sem("zn2_ready_act")
        full_ready = sem("full_ready")
        hi_ready = sem("hi_ready")
        logits_mm = sem("logits_mm")
        b1_turned = sem("b1_turned")
        wr_zeroed = sem("wr_zeroed")
        logits_T_ready = sem("logits_T_ready")
        logits_turned = sem("logits_turned")
        col = lambda v: v.rearrange("(p o) -> p o", o=1)
        loads = [(g2[:, :], col(a["ln2_g"])), (be2[:, :], col(a["ln2_b"])), (wr[:, 0:NE], a["wr"]),
                 (b1_rows[:, :], a["b1"].rearrange("e (f p) -> (e f) p", p=P)), (ro.b2[:, :], a["b2"]),
                 (ro.order[:, :, :].rearrange("p k q -> p (k q)"), a["c_before"])]
        block = ctx.enter_context(nc.Block())

        def bank_cols(n):
            return slice(BANK * n, BANK * n + BANK)

        @block.sync
        def _(sp):
            for dst, src in loads:
                sp.dma_start(dst, src).then_inc(loaded, 16)

        @block.gpsimd
        def _(pool):
            pool.memset(wr[:, NE:32], 0.0).then_inc(wr_zeroed, 1)
            for n in (1, 3):
                pool.wait_ge(hi_ready, n + 1)
                pool.tensor_tensor(h_part["lo"][:, bank_cols(n)], h_T[:, bank_cols(n)],
                                   h_part["hi"][:, bank_cols(n)].bitcast(F32), ALU.subtract)

        @block.scalar
        def _(act):
            norm_3.scalar_sqrt(act)
            norm_3.scalar_apply(act, zn, z, range(NT // 2, NT)).then_inc(zn_ready_act, 1)
            act.wait_ge(b1_turned, 1)
            act.activation(ro.b1_T[:, :], ps[:, 1, 0:NE * FT], ACT.Copy)
            for n in range(4):
                act.wait_ge(full_ready, n + 1)
                act.activation(h_part["hi"][:, bank_cols(n)], h_T[:, bank_cols(n)], ACT.Copy).then_inc(hi_ready, 1)

        @block.vector
        def _(dve):
            link = chain(dve, chain_d)
            dve.wait_ge(sums_mm, 1)
            link(dve.reciprocal(ho.last_scale[:, :], ps[:, 4, :]))
            dve.tensor_tensor(ho.last_o[:, :], ho.last_o[:, :], ho.last_scale[:, :], ALU.mult).then_inc(last_ready, 1)
            for n in range(4):
                dve.wait_ge(pe_unit, n + 1)
                link(dve.tensor_tensor(z[:, 4 * n:4 * n + 4, :], ps[:, n, :].rearrange("p (i d) -> p i d", d=D),
                                       z[:, 4 * n:4 * n + 4, :], ALU.add))
                ins = norm_3.vector_stats_of(dve, z, range(4 * n, 4 * n + 4))
            link(ins)
            norm_3.vector_var(dve, link)
            norm_3.vector_scales(dve, link)
            norm_3.vector_apply(dve, link, zn, z, range(0, NT // 2)).then_inc(zn_ready, 1)
            dve.wait_ge(loaded, 16 * len(loads))
            for n in range(4):
                dve.wait_ge(pe_unit, 4 + n + 1)
                dve.tensor_scalar(h_T[:, bank_cols(n)], ps[:, 4 + n, :], g2[:, 0:1], be2[:, 0:1],
                                  ALU.mult, ALU.add).then_inc(full_ready, 1)
            dve.wait_ge(logits_mm, 1)
            dve.tensor_copy(logits_T[:, :], ps[:, 2, :]).then_inc(logits_T_ready, 1)
            for n in (0, 2):
                dve.wait_ge(hi_ready, n + 1)
                dve.tensor_tensor(h_part["lo"][:, bank_cols(n)], h_T[:, bank_cols(n)],
                                  h_part["hi"][:, bank_cols(n)].bitcast(F32), ALU.subtract)
            dve.wait_ge(logits_turned, 1)
            dve.tensor_copy(ro.logits[:, :, :].rearrange("p (n i) e -> p n i e", i=4),
                            ps[:, 3, :].rearrange("p (i n x) -> p n i x", n=CHUNK, x=32)[:, :, :, 0:NE])

        @block.tensor
        def _(pe):
            pe.matmul(ps[:, 4, :], ho.sum_rows[:, :], ho.last_o[:, :], start=True, stop=True).then_inc(sums_mm, 1)
            dst = lambda m: ps[:, m // 4, P * (m % 4):P * (m % 4) + P]
            for m in range(NT):
                pe.matmul(dst(m), ho.o_T[:, P * m:P * m + P], ho.wo[:, :], start=(m % 4 == 0), stop=False,
                          skip_group_check=(m % 4 != 0))
            pe.wait_ge(last_ready, 1)
            for n in range(4):
                rows = slice(32 * n, 32 * n + HD)
                for i in range(4):
                    ins = pe.matmul(dst(4 * n + i), ho.last_o[rows, P * i:P * i + P], ho.wo_last[rows, :],
                                    start=False, stop=True, skip_group_check=(i != 0))
                ins.then_inc(pe_unit, 1)
            pe.wait_ge(zn_ready, 1)
            for n in range(4):
                if n == 2:
                    pe.wait_ge(zn_ready_act, 1)
                for i in range(4):
                    ins = pe.transpose(ps[:, 4 + n, P * i:P * i + P], zn[:, 4 * n + i, :], ident[:, :])
                ins.then_inc(pe_unit, 1)
            pe.wait_ge(loaded, 16 * len(loads))
            pe.transpose(ps[:, 1, 0:NE * FT], b1_rows[:, :], ident[0:NE * FT, 0:NE * FT]).then_inc(b1_turned, 1)
            pe.wait_ge(wr_zeroed, 1)
            for n in range(CHUNK):
                pe.wait_ge(full_ready, n + 1)
                ins = pe.matmul(ps[32 * n:32 * n + 32, 2, :], wr[:, :], h_T[:, bank_cols(n)], start=True, stop=True)
            ins.then_inc(logits_mm, 1)
            pe.wait_ge(logits_T_ready, 1)
            for i in range(4):
                ins = pe.transpose(ps[:, 3, P * i:P * i + P], logits_T[:, P * i:P * i + P], ident[:, :])
            ins.then_inc(logits_turned, 1)


W_PARTS = ("hi", "lo")


class ExpertWeights:

    def __init__(self, nc, ctx):
        def sb(name, shape, dt=F32):
            return ctx.enter_context(nc.sbuf_tensor("ew_" + name, shape, dt))
        self.w1 = [sb(f"w1_{b}", [P, FF]) for b in range(2)]
        self.w2 = [sb(f"w2_{b}", [P, FT, D]) for b in range(2)]
        self.w1_part = [{p: sb(f"w1_{p}{b}", [P, FF], F32R) for p in W_PARTS} for b in range(2)]
        self.w2_part = [{p: sb(f"w2_{p}{b}", [P, FT, D], F32R) for p in W_PARTS} for b in range(2)]

    def load(self, sp, a, e, b, loaded):
        w1 = a["w1"][bass.ds(e, 1)].rearrange("o p f -> (o p) f")
        w2 = a["w2"].rearrange("e (f p) d -> e p f d", p=P)[bass.ds(e, 1)].rearrange("o p f d -> (o p) f d")
        sp.dma_start(self.w1[b][:, :], w1).then_inc(loaded, 16)
        sp.dma_start(self.w2[b][:, :, :], w2).then_inc(loaded, 16)

    def scalar_hi(self, act, b):
        act.activation(self.w1_part[b]["hi"][:, :], self.w1[b][:, :], ACT.Copy)
        return act.activation(self.w2_part[b]["hi"][:, :, :], self.w2[b][:, :, :], ACT.Copy)

    def pool_lo(self, pool, b):
        pool.tensor_tensor(self.w1_part[b]["lo"][:, :], self.w1[b][:, :], self.w1_part[b]["hi"][:, :].bitcast(F32),
                           ALU.subtract)
        return pool.tensor_tensor(self.w2_part[b]["lo"][:, :, :], self.w2[b][:, :, :],
                                  self.w2_part[b]["hi"][:, :, :].bitcast(F32), ALU.subtract)


def experts(nc, a, x1, z, h_part, ew, ro, ident, scr, out):
    steps = NE * CHUNK
    body = 2 * CHUNK
    loops = (NE - 2) // 2
    with ExitStack() as ctx:
        def sb(name, shape, dt=F32):
            return ctx.enter_context(nc.sbuf_tensor("ex_" + name, shape, dt))

        def sem(name):
            return ctx.enter_context(nc.semaphore("ex_" + name))

        ps_h = ctx.enter_context(nc.psum_tensor("ps_h", [P, FT, BANK], F32))
        ps_y = ctx.enter_context(nc.psum_tensor("ps_y", [P, 2, BANK], F32))
        ps_r = ctx.enter_context(nc.psum_tensor("ps_r", [P, 2, BANK], F32))
        hid = [[sb(f"hid{b}_{f}", [P, BANK]) for f in range(FT)] for b in range(2)]
        hid_hi = [[sb(f"hid_hi{b}_{f}", [P, BANK], F32R) for f in range(FT)] for b in range(2)]
        hid_lo = [[sb(f"hid_lo{b}_{f}", [P, BANK], F32R) for f in range(FT)] for b in range(2)]
        y_0 = sb("y_0", [P, L])
        y_gated = [sb(f"y_gated{b}", [P, BANK]) for b in range(2)]
        y_T = sb("y_T", [P, L])
        gate_b = [sb(f"gate_b{b}", [P, L]) for b in range(2)]
        b1_e = [sb(f"b1_e{b}", [P, FT]) for b in range(2)]
        ones = sb("ones_p", [P, P])
        rank = sb("rank", [P, NE])
        masked = sb("masked", [P, NT, NE])
        probs = sb("probs", [P, NT, NE])
        cand = sb("cand", [P, NT, NE])
        peak = sb("peak", [P, NT])
        chosen = sb("chosen", [P, NT, 2, NE])
        upto = [sb(f"upto{b}", [P, NT, 2 * NE]) for b in range(2)]
        before = sb("before_tile", [P, NT, 2 * NE])
        kept = sb("kept", [P, NT, 2, NE])
        part = sb("part", [P, NT, 2, NE])
        share = sb("share", [P, NT, 2])
        total = sb("total", [P, NT])
        gate = sb("gate", [P, NE, NT])
        gate_T = sb("gate_T", [NE, L])
        norm_4 = [Norm(nc, sb, sem, f"norm_4_{half}") for half in range(2)]
        halves = [range(0, NT // 2), range(NT // 2, NT)]

        w_loaded = [sem(f"w_loaded{b}") for b in range(2)]
        w_hi_ready = sem("w_hi_ready")
        w_split = sem("w_split")
        consts = sem("consts")
        pool_chain = sem("pool_chain")
        chain_d = sem("chain")
        b1_e_ready = sem("b1_e_ready")
        shifted_ready = sem("shifted_ready")
        exp_ready = sem("router_exp_ready")
        counts_ready = sem("counts_ready")
        count_mm = sem("count_mm")
        gate_ready = sem("gate_ready")
        gate_turned = sem("gate_turned")
        gate_T_ready = sem("gate_T_ready")
        gate_stored = sem("gate_stored")
        gate_loaded = [sem(f"gate_loaded{b}") for b in range(2)]
        bias_mm = sem("bias_mm")
        bias_added = sem("bias_added")
        hid_mm = sem("hid_mm")
        hi_ready = sem("hi_ready")
        lo_ready = sem("lo_ready")
        y_mm = sem("y_mm")
        y_taken = sem("y_taken")
        y_added = sem("y_added")
        y_turned = sem("y_turned")
        z_ready_act = sem("z_ready_act")
        out_ready = sem("out_ready")
        out_stored = sem("out_stored")

        block = ctx.enter_context(nc.Block())

        @block.sync
        def _(sp):
            for e in (2, 3):
                ew.load(sp, a, e, e % 2, w_loaded[e % 2])

            def load_gates(e, b):
                sp.dma_start(gate_b[b][:, :], scr["gate"][bass.ds(e, 1), :].to_broadcast([P, L]))\
                  .then_inc(gate_loaded[b], 16)

            sp.wait_ge(gate_T_ready, CHUNK)
            sp.dma_start(scr["gate"][:, :], gate_T[:, :]).then_inc(gate_stored, 16)
            sp.wait_ge(gate_stored, 16)
            load_gates(0, 0)
            load_gates(1, 1)

            def after(it, b):
                sp.wait_ge(y_taken, it * body + (b + 1) * CHUNK)
                sp.wait_ge(y_added, it * body + (b + 1) * CHUNK)
                load_gates(it * 2 + (2 + b), b)

            with sp.Fori(0, loops - 1) as it:
                for b in range(2):
                    after(it, b)
                    sp.wait_ge(w_split, it * 2 + (b + 1))
                    ew.load(sp, a, it * 2 + (4 + b), b, w_loaded[b])
            for b in range(2):
                after(loops - 1, b)
            for half in range(2):
                sp.wait_ge(out_ready, half + 1)
                t = slice(NT // 2 * half, NT // 2 * (half + 1))
                for j, v in enumerate(tiles_of(out)):
                    sp.dma_start(v[:, t, :], x1[H1 * j:H1 * j + H1, t, :]).then_inc(out_stored, 16)
            sp.wait_ge(out_stored, 32 * NJ)

        def split(eng, n, f):
            return eng.tensor_tensor(hid_lo[n % 2][f][:, :], hid[n % 2][f][:, :],
                                     hid_hi[n % 2][f][:, :].bitcast(F32), ALU.subtract)

        @block.gpsimd
        def _(pool):
            link = chain(pool, pool_chain)
            link(pool.memset(ones[:, :], 1.0))
            for e in range(NE):
                link(pool.memset(rank[:, e:e + 1], float(NE - e)))
            pool.nop().then_inc(consts, 1)
            for s in range(CHUNK):
                for f in range(FT):
                    pool.wait_ge(hi_ready, s * FT + f + 1)
                    split(pool, s, f).then_inc(lo_ready, 1)
            with pool.Fori(0, loops) as it:
                for b in range(2):
                    pool.wait_ge(w_hi_ready, it * 2 + (b + 1))
                    ew.pool_lo(pool, b).then_inc(w_split, 1)

        @block.scalar
        def _(act):
            act.wait_ge(shifted_ready, 1)
            act.activation(probs[:, :, :], cand[:, :, :], ACT.Exp).then_inc(exp_ready, 1)

            def bias_of(e, b):
                act.activation(b1_e[b][:, :], ro.b1_T[:, bass.ds(e * FT, FT)], ACT.Copy).then_inc(b1_e_ready, 1)
                act.wait_ge(b1_e_ready, e + 1)

            def hidden(s, n, e):
                b = n // CHUNK % 2
                if n % CHUNK == 0:
                    bias_of(e, b)
                for f in range(FT):
                    act.wait_ge(hid_mm, s * FT + (f + 1))
                    if f == 0 and not (isinstance(s, int) and s < 2):
                        act.wait_ge(y_mm, s - 1)
                    act.activation(hid[n % 2][f][:, :], ps_h[:, f, :], ACT.Relu, bias=b1_e[b][:, f:f + 1])
                    act.activation(hid_hi[n % 2][f][:, :], ps_h[:, f, :], ACT.Relu, bias=b1_e[b][:, f:f + 1])\
                       .then_inc(hi_ready, 1)

            def keep_y_0(s):
                act.wait_ge(y_mm, s + 1)
                act.activation(y_0[:, BANK * s:BANK * s + BANK], ps_y[:, s % 2, :], ACT.Copy).then_inc(y_taken, 1)

            hidden(0, 0, 0)
            for s in range(1, CHUNK + 1):
                hidden(s, s, s // CHUNK)
                keep_y_0(s - 1)
            with act.Fori(0, loops) as it:
                for q in range(body):
                    n = q + CHUNK + 1
                    if n % CHUNK == 1:
                        act.wait_ge(y_mm, it * body + (n - 1))
                        act.wait_ge(w_loaded[(n // CHUNK + 1) % 2], it * 32 + 32)
                        ew.scalar_hi(act, (n // CHUNK + 1) % 2).then_inc(w_hi_ready, 1)
                    hidden(it * body + n, n, it * 2 + n // CHUNK)
            for s in range(loops * body + CHUNK + 1, steps):
                hidden(s, s, s // CHUNK)
            norm_4[0].scalar_sqrt(act, halves[0])
            norm_4[0].scalar_apply(act, z, z, halves[0]).then_inc(z_ready_act, 1)
            norm_4[1].scalar_sqrt(act, halves[1])
            norm_4[1].scalar_apply(act, z, z, halves[1][0:4]).then_inc(z_ready_act, 1)

        @block.vector
        def _(dve):
            link = chain(dve, chain_d)
            wide = lambda v: v.rearrange("p (i o) -> p i o", o=1).to_broadcast([P, NT, NE])
            rank_b = rank[:, :].rearrange("p (o e) -> p o e", o=1).to_broadcast([P, NT, NE])

            def choose(values, w):
                link(dve.tensor_reduce(peak[:, :], values[:, :, :], AX.X, ALU.max))
                link(dve.tensor_tensor(cand[:, :, :], values[:, :, :], wide(peak[:, :]), ALU.is_ge))
                link(dve.tensor_tensor(cand[:, :, :], cand[:, :, :], rank_b, ALU.mult))
                link(dve.tensor_reduce(peak[:, :], cand[:, :, :], AX.X, ALU.max))
                link(dve.tensor_tensor(chosen[:, :, w, :], rank_b, wide(peak[:, :]), ALU.is_equal))

            link(dve.tensor_reduce(peak[:, :], ro.logits[:, :, :], AX.X, ALU.max))
            dve.tensor_tensor(cand[:, :, :], ro.logits[:, :, :], wide(peak[:, :]), ALU.subtract).then_inc(shifted_ready, 1)
            dve.wait_ge(exp_ready, 1)
            link(dve.tensor_reduce(total[:, :], probs[:, :, :], AX.X, ALU.add))
            link(dve.reciprocal(total[:, :], total[:, :]))
            link(dve.tensor_tensor(probs[:, :, :], probs[:, :, :], wide(total[:, :]), ALU.mult))
            dve.wait_ge(consts, 1)
            choose(probs, 0)
            link(dve.scalar_tensor_tensor(out=masked[:, :, :], in0=chosen[:, :, 0, :], scalar=-3.0e38,
                                          in1=ro.logits[:, :, :], op0=ALU.mult, op1=ALU.add))
            choose(masked, 1)
            now = chosen[:, :, :, :].rearrange("p i w e -> p i (w e)")
            for k in range(NT.bit_length() - 1):
                to = upto[k % 2]
                dist = 1 << k
                dve.tensor_copy(to[:, 0:dist, :], now[:, 0:dist, :])
                link(dve.tensor_tensor(to[:, dist:NT, :], now[:, dist:NT, :], now[:, 0:NT - dist, :], ALU.add))
                now = to[:, :, :]
            dve.tensor_tensor(before[:, :, :], now, chosen[:, :, :, :].rearrange("p i w e -> p i (w e)"),
                              ALU.subtract).then_inc(counts_ready, 1)
            dve.wait_ge(count_mm, 1)
            flat = lambda t: t[:, :, :, :].rearrange("p i w e -> p (i w e)")
            link(dve.scalar_tensor_tensor(out=flat(kept), in0=ps_r[:, 0, 0:2 * NT * NE], scalar=float(CAP),
                                          in1=flat(chosen), op0=ALU.is_le, op1=ALU.mult))
            for w in range(2):
                ins = dve.tensor_tensor(part[:, :, w, :], kept[:, :, w, :], probs[:, :, :], ALU.mult)
            link(ins)
            link(dve.tensor_reduce(share[:, :, :].rearrange("p i w -> p (i w)"),
                                   part[:, :, :, :].rearrange("p i w e -> p (i w) e"), AX.X, ALU.add))
            link(dve.tensor_tensor(total[:, :], share[:, :, 0], share[:, :, 1], ALU.add))
            link(dve.tensor_scalar(total[:, :], total[:, :], float(np.finfo(np.float32).eps), None, ALU.max))
            link(dve.reciprocal(total[:, :], total[:, :]))
            link(dve.tensor_scalar(total[:, :], total[:, :], KEEP, None, ALU.mult))
            link(dve.tensor_tensor(part[:, :, 0, :], part[:, :, 0, :], part[:, :, 1, :], ALU.add))
            dve.tensor_tensor(gate[:, :, :].rearrange("p e i -> p i e"), part[:, :, 0, :], wide(total[:, :]),
                              ALU.mult).then_inc(gate_ready, 1)
            for n in range(CHUNK):
                dve.wait_ge(gate_turned, n + 1)
                dve.tensor_copy(gate_T[:, BANK * n:BANK * n + BANK], ps_r[0:NE, n % 2, :]).then_inc(gate_T_ready, 1)

            def lows(s, n, tiles):
                for f in tiles:
                    dve.wait_ge(hi_ready, s * FT + (f + 1))
                    if f == 0:
                        dve.wait_ge(y_mm, s - 1)
                    split(dve, n, f).then_inc(lo_ready, 1)

            def add_bias(n):
                dve.wait_ge(bias_mm, n + 1)
                return dve.tensor_tensor(z[:, 4 * n:4 * n + 4, :], ps_r[:, n % 2, :].rearrange("p (i d) -> p i d", d=D),
                                         z[:, 4 * n:4 * n + 4, :], ALU.add).then_inc(bias_added, 1)

            def gated(s, n):
                b, c = n // CHUNK % 2, n % CHUNK
                if c == 0:
                    dve.wait_ge(gate_loaded[b], s * 2 + (16 if b == 0 else 8))
                dve.wait_ge(y_mm, s + 1)
                dve.tensor_tensor(y_gated[n % 2][:, :], ps_y[:, n % 2, :], gate_b[b][:, BANK * c:BANK * c + BANK],
                                  ALU.mult).then_inc(y_taken, 1)

            def summed(s, n):
                c = slice(BANK * (n % CHUNK), BANK * (n % CHUNK) + BANK)
                dve.wait_ge(y_taken, s + 1)
                dve.wait_ge(y_added, s - (CHUNK - 1))
                return dve.tensor_tensor(y_T[:, c], y_T[:, c], y_gated[n % 2][:, :], ALU.add).then_inc(y_added, 1)

            for n in range(2):
                add_bias(n)
            lows(CHUNK, CHUNK, range(FT))
            dve.wait_ge(gate_loaded[0], 16)
            for c in range(CHUNK):
                dve.wait_ge(y_taken, c + 1)
                at = slice(BANK * c, BANK * c + BANK)
                dve.tensor_tensor(y_T[:, at], y_0[:, at], gate_b[0][:, at], ALU.mult).then_inc(y_added, 1)
            with dve.Fori(0, loops) as it:
                for q in range(body):
                    n = q + CHUNK
                    s = it * body + n
                    gated(s, n)
                    lows(s + 1, n + 1, [0])
                    summed(s, n)
                    lows(s + 1, n + 1, range(1, FT))
            for n in range(2, CHUNK):
                add_bias(n)
            last = steps - 1
            for s in range(steps - CHUNK, last):
                gated(s, s)
                lows(s + 1, s + 1, [0])
                summed(s, s)
                lows(s + 1, s + 1, range(1, FT))

            def from_turned(n):
                dve.wait_ge(y_turned, n + 1)
                dve.wait_ge(bias_added, CHUNK)
                return dve.tensor_tensor(z[:, 4 * n:4 * n + 4, :], ps_h[:, n, :].rearrange("p (i d) -> p i d", d=D),
                                         z[:, 4 * n:4 * n + 4, :], ALU.add)

            def put_out(half):
                for i in (halves[half][0:4], halves[half][4:]):
                    t = slice(i.start, i.stop)
                    ins = dve.tensor_tensor(x1[:, t, :], x1[:, t, :], z[:, t, :], ALU.add)
                ins.then_inc(out_ready, 1)

            from_turned(0)
            link(from_turned(1))
            link(norm_4[0].vector_stats_of(dve, z, halves[0]))
            link(norm_4[0].vector_mv(dve, halves[0]))
            norm_4[0].vector_var_only(dve, halves[0])
            gated(last, last)
            summed(last, last)
            norm_4[0].vector_scales(dve, link, halves[0])
            link(from_turned(2))
            link(norm_4[1].vector_stats_of(dve, z, halves[1][0:4]))
            norm_4[1].vector_mv(dve, halves[1][0:4])
            link(from_turned(3))
            link(norm_4[1].vector_stats_of(dve, z, halves[1][4:]))
            link(norm_4[1].vector_mv(dve, halves[1][4:]))
            norm_4[1].vector_var_only(dve, halves[1])
            dve.wait_ge(z_ready_act, 1)
            put_out(0)
            norm_4[1].vector_scales(dve, link, halves[1])
            link(norm_4[1].vector_apply(dve, link, z, z, halves[1][4:]))
            dve.wait_ge(z_ready_act, 2)
            put_out(1)

        @block.tensor
        def _(pe):
            def products(dst, terms):
                for i, (lhs, rhs) in enumerate(terms):
                    ins = pe.matmul(dst, lhs, rhs, start=(i == 0), stop=(i == len(terms) - 1))
                return ins

            def hidden(s, n):
                b, c = n // CHUNK % 2, n % CHUNK
                for f in range(FT):
                    if not (isinstance(s, int) and s == 0):
                        pe.wait_ge(hi_ready, (s - 1) * FT + (f + 1))
                    w = {p: ew.w1_part[b][p][:, P * f:P * f + P] for p in W_PARTS}
                    h = {p: h_part[p][:, BANK * c:BANK * c + BANK] for p in W_PARTS}
                    products(ps_h[:, f, :], [(w["hi"], h["hi"]), (w["hi"], h["lo"]), (w["lo"], h["hi"])])\
                        .then_inc(hid_mm, 1)

            def second(s, n):
                b = n // CHUNK % 2
                dst = ps_y[:, n % 2, :]
                w = ew.w2_part[b]
                pe.wait_ge(hi_ready, s * FT + FT)
                if not (isinstance(s, int) and s < 2):
                    pe.wait_ge(y_taken, s - 1)
                for f in range(FT):
                    for p in W_PARTS:
                        pe.matmul(dst, w[p][:, f, :], hid_hi[n % 2][f][:, :], start=(f == 0 and p == "hi"), stop=False)
                for f in range(FT):
                    pe.wait_ge(lo_ready, s * FT + (f + 1))
                    ins = pe.matmul(dst, w["hi"][:, f, :], hid_lo[n % 2][f][:, :], start=False, stop=(f == FT - 1))
                ins.then_inc(y_mm, 1)

            def turn_gates(n):
                if n >= 2:
                    pe.wait_ge(gate_T_ready, n - 1)
                for i in range(4):
                    ins = pe.transpose(ps_r[0:NE, n % 2, P * i:P * i + P], gate[:, :, 4 * n + i], ident[:, :])
                ins.then_inc(gate_turned, 1)

            def biases(n):
                if n >= 2:
                    pe.wait_ge(bias_added, n - 1)
                pe.wait_ge(gate_T_ready, CHUNK)
                for i in range(4):
                    m = 4 * n + i
                    ins = pe.matmul(ps_r[:, n % 2, P * i:P * i + P], gate_T[:, P * m:P * m + P], ro.b2[:, :],
                                    start=True, stop=True)
                ins.then_inc(bias_mm, 1)

            hidden(0, 0)
            for s in range(2):
                hidden(s + 1, s + 1)
                second(s, s)
            pe.wait_ge(counts_ready, 1)
            pe.wait_ge(consts, 1)
            w = 2 * NE
            last = upto[(NT.bit_length() - 2) % 2][:, NT - 1:NT, :]
            cnt = ps_r[:, 0, 0:NT * w]
            pe.matmul(cnt, ro.order[:, 0, :], last.to_broadcast([P, NT, w]), start=True, stop=False)
            pe.matmul(cnt, ro.order[:, 1, :], before[:, :, :], start=False, stop=False)
            pe.matmul(cnt.rearrange("p (i w) -> p i w", w=w)[:, :, NE:w], ones[:, :],
                      last[:, :, 0:NE].to_broadcast([P, NT, NE]), start=False, stop=False, skip_group_check=True)
            pe.matmul(cnt, ro.order[:, 2, :], chosen[:, :, :, :].rearrange("p i w e -> p (i w e)"), start=False,
                      stop=True).then_inc(count_mm, 1)
            hidden(3, 3)
            second(2, 2)
            pe.wait_ge(gate_ready, 1)
            for n in range(CHUNK):
                turn_gates(n)
            hidden(4, 4)
            second(3, 3)
            for n in range(2):
                biases(n)
            with pe.Fori(0, loops) as it:
                for q in range(body):
                    n = q + CHUNK
                    s = it * body + n
                    if (n + 1) % CHUNK == 0:
                        pe.wait_ge(w_split, it * 2 + (n + 1) // CHUNK - 1)
                    hidden(s + 1, n + 1)
                    second(s, n)
            for n in range(2, CHUNK):
                biases(n)
            for s in range(steps - CHUNK, steps - 1):
                hidden(s + 1, s + 1)
                second(s, s)

            def turn_y(n):
                pe.wait_ge(y_added, steps - CHUNK + n + 1)
                pe.wait_ge(hi_ready, steps * FT)
                for i in range(4):
                    m = 4 * n + i
                    ins = pe.transpose(ps_h[:, n, P * i:P * i + P], y_T[:, P * m:P * m + P], ident[:, :])
                ins.then_inc(y_turned, 1)

            for n in range(CHUNK - 1):
                turn_y(n)
            second(steps - 1, steps - 1)
            turn_y(CHUNK - 1)


def hyena_moe_layer(nc, a, out):
    with ExitStack() as ctx:
        x1 = ctx.enter_context(nc.sbuf_tensor("x1", [P, NT, D], F32))
        ident = ctx.enter_context(nc.sbuf_tensor("ident", [P, P], F32))
        scr = {n: nc.dram_tensor("scr_" + n, (NH, HD, PARTS, L), BF16).ap() for n in "qk"}
        scr["o"] = nc.dram_tensor("scr_o", (NH, HD + 1, L), F32).ap()
        scr["gate"] = nc.dram_tensor("scr_gate", (NE, L), F32).ap()
        z = ctx.enter_context(nc.sbuf_tensor("z", [P, NT, D], F32))
        sb = lambda name, shape, dt: ctx.enter_context(nc.sbuf_tensor(name, shape, dt))
        sem = lambda name: ctx.enter_context(nc.semaphore(name))
        norm_y = Norm(nc, sb, sem, "norm_y")
        norm_12 = Norm2(nc, sb, sem, "norm_12")
        hyena(nc, a["attn"] | a["const"], x1, z, norm_y, ident)
        ew = ExpertWeights(nc, ctx)
        ho = HeadOutputs(nc, ctx)
        with ExitStack() as att:
            vs = att.enter_context(nc.sbuf_tensor("vs", [P, NH, NT, HD], F32))
            so = ScoreOperands(nc, att)
            attention_operands(nc, a["ffn"], x1, z, norm_y, norm_12, vs, so, ident, scr)
            attention(nc, a["ffn"] | a["const"], x1, z, norm_y, norm_12, vs, so, ho, ew, scr)
        h_part = {p: ctx.enter_context(nc.sbuf_tensor("h_T2_" + p, [P, L], F32R)) for p in W_PARTS}
        ro = Router(nc, ctx)
        with ExitStack() as full:
            h_T = full.enter_context(nc.sbuf_tensor("h_T2", [P, L], F32))
            attention_output(nc, a["ffn"] | a["const"], z, ho, h_T, h_part, ro, ident)
        experts(nc, a["ffn"] | a["const"], x1, z, h_part, ew, ro, ident, scr, out)


def kernel(**inputs):
    import numpy as _np
    import concourse.bacc as _bacc
    from concourse import mybir as _mybir
    from concourse.bass_utils import run_bass_kernel_spmd as _run

    nc = _bacc.Bacc("TRN2", target_bir_lowering=False, num_devices=1)
    arrays, a = {}, {"attn": {}, "ffn": {}, "const": {}}
    named = [(k, _np.ascontiguousarray(v)) for k, v in inputs.items()] + list(shape_constants().items())
    for name, v in named:
        arrays[f"in_{name}_dram"] = v
        ap = nc.dram_tensor(f"in_{name}_dram", v.shape, _mybir.dt.from_np(v.dtype), kind="ExternalInput").ap()
        group = next((g for g in ("attn", "ffn") if name.startswith(f"L0_{g}_")), "const")
        a[group][name.removeprefix(f"L0_{group}_")] = ap
    out = nc.dram_tensor("out_0_dram", (1, L, D), F32, kind="ExternalOutput").ap()
    a["attn"]["u"] = a["attn"]["u"].rearrange("o l d -> (o l) d")
    hyena_moe_layer(nc, a, out.rearrange("o l d -> (o l) d"))
    r = _run(nc, [arrays], core_ids=[0])
    return r.results[0]["out_0_dram"]
```
